# Optimizing a Trainium2 kernel written in Bass

```python
import numpy as np
import jax
import jax.numpy as jnp

def _softmax(x, axis=-1):
    return jax.nn.softmax(x, axis=axis)

def _gelu(x):
    return jax.nn.gelu(x, approximate=True)

def _silu(x):
    return jax.nn.silu(x)

def _sigmoid(x):
    return jax.nn.sigmoid(x)

def _layernorm(x, axis=-1, eps=1e-05):
    m = jnp.mean(x, axis=axis, keepdims=True)
    v = jnp.var(x, axis=axis, keepdims=True)
    return (x - m) / jnp.sqrt(v + eps)

def _scatter_add(tgt, idx, src, axis=0):
    return tgt.at[idx].add(src)

def _segment_sum(src, seg, n):
    return jax.ops.segment_sum(src, seg, n)
kernel_name = 'mk_gnn_ffn_d2_gnn_r8_9377a1'

def setup_inputs(seed: int=0):
    np.random.seed(seed)
    _w = jnp.asarray

    def _rec_inputs():
        import jax
        import jax.numpy as jnp
        _gk = jax.random.key(seed)
        x = -0.0002117 + 1 * jax.random.normal(jax.random.fold_in(_gk, 1), (6250, 256), jnp.float32)
        src = jax.random.randint(jax.random.fold_in(_gk, 2), (100000,), 0, 6250, jnp.int32)
        dst = jax.random.randint(jax.random.fold_in(_gk, 3), (100000,), 0, 6250, jnp.int32)
        _o = jnp.argsort(dst, stable=True)
        src = src[_o]
        dst = dst[_o]
        edge_weight = jax.random.uniform(jax.random.fold_in(_gk, 13), (100000,), jnp.float32, 0.0, 1)
        return (x, src, dst, edge_weight)
    x, src, dst, edge_weight = _rec_inputs()

    def _L0_gnn_setup():
        import jax, jax.numpy as jnp
        import numpy as np
        N_NODES = 12500
        N_EDGES = 400000
        D_IN = 256
        D_OUT = 256
        key = jax.random.key(seed)
        k1, k2, k3, k4, k5, k6 = jax.random.split(key, 6)
        x = jax.random.normal(k1, (N_NODES, D_IN), dtype=jnp.float32)
        edge_src = jax.random.randint(k2, (N_EDGES,), 0, N_NODES, dtype=jnp.int64)
        edge_dst = jax.random.randint(k3, (N_EDGES,), 0, N_NODES, dtype=jnp.int64)
        adj_vals = jax.random.uniform(k4, (N_EDGES,), dtype=jnp.float32)
        bound = 2.0 * np.sqrt(6.0 / (D_IN + D_OUT))
        w_nbr = jax.random.uniform(k5, (D_IN, D_OUT), dtype=jnp.float32, minval=-bound, maxval=bound)
        w_own = jax.random.uniform(k6, (D_IN, D_OUT), dtype=jnp.float32, minval=-bound, maxval=bound)
        bias = jnp.zeros((D_OUT,), dtype=jnp.float32)
        return {'x': x, 'edge_src': edge_src, 'edge_dst': edge_dst, 'adj_vals': adj_vals, 'w_nbr': w_nbr, 'w_own': w_own, 'bias': bias}
    _L0_gnn_all = _L0_gnn_setup()
    _L0_gnn_in = {k: v for k, v in _L0_gnn_all.items() if k in ('w_nbr', 'w_own', 'bias')}
    del _L0_gnn_all

    def _L0_ffn_setup():
        import jax, jax.numpy as jnp
        import numpy as np
        TOP_K = 2
        LN_EPS = 1e-05
        key = jax.random.key(seed)
        ks = jax.random.split(key, 8)
        B, S, D, E, H = (16, 1024, 256, 8, 1024)
        x = jax.random.normal(ks[0], (B, S, D), dtype=jnp.float32)
        Wr = jax.random.normal(ks[1], (D, E), dtype=jnp.float32) * 0.1
        br = jnp.zeros((E,), dtype=jnp.float32)
        ln_g = jnp.ones((E, D), dtype=jnp.float32)
        ln_b = jnp.zeros((E, D), dtype=jnp.float32)
        W1 = jax.random.normal(ks[2], (E, D, H), dtype=jnp.float32) * (1.0 / np.sqrt(D))
        b1 = jnp.zeros((E, H), dtype=jnp.float32)
        W2 = jax.random.normal(ks[3], (E, H, D), dtype=jnp.float32) * (1.0 / np.sqrt(H))
        b2 = jnp.zeros((E, D), dtype=jnp.float32)
        return {'x': x, 'Wr': Wr, 'br': br, 'ln_g': ln_g, 'ln_b': ln_b, 'W1': W1, 'b1': b1, 'W2': W2, 'b2': b2}
    _L0_ffn_all = _L0_ffn_setup()
    _L0_ffn_in = {k: v for k, v in _L0_ffn_all.items() if k in ('Wr', 'br', 'ln_g', 'ln_b', 'W1', 'b1', 'W2', 'b2')}
    del _L0_ffn_all

    def _L1_gnn_setup():
        import jax, jax.numpy as jnp
        import numpy as np
        N_NODES = 6250
        N_EDGES = 100000
        DIM = 256
        N_LAYERS = 3
        LN_EPS = 1e-05

        def _gcn_norm(edge_index, n_nodes, dtype):
            row, col = (edge_index[0], edge_index[1])
            loop = jnp.arange(n_nodes, dtype=edge_index.dtype)
            row = jnp.concatenate([row, loop])
            col = jnp.concatenate([col, loop])
            deg = jax.ops.segment_sum(jnp.ones(row.shape[0], dtype=dtype), col, num_segments=n_nodes)
            dinv = jnp.where(deg > 0, jax.lax.rsqrt(deg), 0.0)
            norm = dinv[row] * dinv[col]
            return (row, col, norm)
        key = jax.random.key(seed)
        ks = jax.random.split(key, 6)
        x = jax.random.normal(ks[0], (N_NODES, DIM), dtype=jnp.float32)
        edge_index = jax.random.randint(ks[1], (2, N_EDGES), 0, N_NODES, dtype=jnp.int64)
        W = jax.random.normal(ks[2], (N_LAYERS, DIM, DIM), dtype=jnp.float32) * (1.0 / np.sqrt(DIM))
        b = jax.random.normal(ks[3], (N_LAYERS, DIM), dtype=jnp.float32) * 0.02
        gamma = jnp.ones((N_LAYERS, DIM), dtype=jnp.float32)
        beta = jnp.zeros((N_LAYERS, DIM), dtype=jnp.float32)
        return {'x': x, 'W': W, 'b': b, 'gamma': gamma, 'beta': beta, 'edge_index': edge_index}
    _L1_gnn_all = _L1_gnn_setup()
    _L1_gnn_in = {k: v for k, v in _L1_gnn_all.items() if k in ('W', 'b', 'gamma', 'beta')}
    del _L1_gnn_all

    def _L1_ffn_setup():
        import jax, jax.numpy as jnp
        import numpy as np
        DIM = 256
        H = 8
        D = 64
        G = 64
        INNER = H * D
        SCALE = D ** (-0.5)
        key = jax.random.key(seed)
        ks = jax.random.split(key, 12)
        B, N = (4, 2048)
        x = jax.random.normal(ks[0], (B, N, DIM), dtype=jnp.float32)
        s = lambda fan_in: 1.0 / np.sqrt(fan_in)
        W_fx = jax.random.normal(ks[1], (DIM, INNER), dtype=jnp.float32) * s(DIM)
        b_fx = jnp.zeros((INNER,), dtype=jnp.float32)
        W_x = jax.random.normal(ks[2], (DIM, INNER), dtype=jnp.float32) * s(DIM)
        b_x = jnp.zeros((INNER,), dtype=jnp.float32)
        A = jax.random.normal(ks[3], (G, D), dtype=jnp.float32)
        Q, _ = jnp.linalg.qr(A.T)
        W_slice = Q[:, :G].astype(jnp.float32)
        b_slice = jnp.zeros((G,), dtype=jnp.float32)
        W_q = jax.random.normal(ks[4], (D, D), dtype=jnp.float32) * s(D)
        W_k = jax.random.normal(ks[5], (D, D), dtype=jnp.float32) * s(D)
        W_v = jax.random.normal(ks[6], (D, D), dtype=jnp.float32) * s(D)
        W_out = jax.random.normal(ks[7], (INNER, DIM), dtype=jnp.float32) * s(INNER)
        b_out = jnp.zeros((DIM,), dtype=jnp.float32)
        temperature = jnp.ones((1, H, 1, 1), dtype=jnp.float32) * 0.5
        return {'x': x, 'W_fx': W_fx, 'b_fx': b_fx, 'W_x': W_x, 'b_x': b_x, 'W_slice': W_slice, 'b_slice': b_slice, 'W_q': W_q, 'W_k': W_k, 'W_v': W_v, 'W_out': W_out, 'b_out': b_out, 'temperature': temperature}
    _L1_ffn_all = _L1_ffn_setup()
    _L1_ffn_in = {k: v for k, v in _L1_ffn_all.items() if k in ('W_fx', 'b_fx', 'W_x', 'b_x', 'W_slice', 'b_slice', 'W_q', 'W_k', 'W_v', 'W_out', 'b_out', 'temperature')}
    del _L1_ffn_all
    return {'x': x, 'src': src, 'dst': dst, 'edge_weight': edge_weight, 'L0_gnn_w_nbr': _L0_gnn_in['w_nbr'], 'L0_gnn_w_own': _L0_gnn_in['w_own'], 'L0_gnn_bias': _L0_gnn_in['bias'], 'L0_ffn_Wr': _L0_ffn_in['Wr'], 'L0_ffn_br': _L0_ffn_in['br'], 'L0_ffn_ln_g': _L0_ffn_in['ln_g'], 'L0_ffn_ln_b': _L0_ffn_in['ln_b'], 'L0_ffn_W1': _L0_ffn_in['W1'], 'L0_ffn_b1': _L0_ffn_in['b1'], 'L0_ffn_W2': _L0_ffn_in['W2'], 'L0_ffn_b2': _L0_ffn_in['b2'], 'L1_gnn_W': _L1_gnn_in['W'], 'L1_gnn_b': _L1_gnn_in['b'], 'L1_gnn_gamma': _L1_gnn_in['gamma'], 'L1_gnn_beta': _L1_gnn_in['beta'], 'L1_ffn_W_fx': _L1_ffn_in['W_fx'], 'L1_ffn_b_fx': _L1_ffn_in['b_fx'], 'L1_ffn_W_x': _L1_ffn_in['W_x'], 'L1_ffn_b_x': _L1_ffn_in['b_x'], 'L1_ffn_W_slice': _L1_ffn_in['W_slice'], 'L1_ffn_b_slice': _L1_ffn_in['b_slice'], 'L1_ffn_W_q': _L1_ffn_in['W_q'], 'L1_ffn_W_k': _L1_ffn_in['W_k'], 'L1_ffn_W_v': _L1_ffn_in['W_v'], 'L1_ffn_W_out': _L1_ffn_in['W_out'], 'L1_ffn_b_out': _L1_ffn_in['b_out'], 'L1_ffn_temperature': _L1_ffn_in['temperature']}

def reference(x, src, dst, edge_weight, L0_gnn_w_nbr, L0_gnn_w_own, L0_gnn_bias, L0_ffn_Wr, L0_ffn_br, L0_ffn_ln_g, L0_ffn_ln_b, L0_ffn_W1, L0_ffn_b1, L0_ffn_W2, L0_ffn_b2, L1_gnn_W, L1_gnn_b, L1_gnn_gamma, L1_gnn_beta, L1_ffn_W_fx, L1_ffn_b_fx, L1_ffn_W_x, L1_ffn_b_x, L1_ffn_W_slice, L1_ffn_b_slice, L1_ffn_W_q, L1_ffn_W_k, L1_ffn_W_v, L1_ffn_W_out, L1_ffn_b_out, L1_ffn_temperature):
    import jax
    import jax.numpy as jnp

    def _L0_gnn_ref(x, edge_src, edge_dst, adj_vals, w_nbr, w_own, bias):
        import jax, jax.numpy as jnp
        import numpy as np
        N_NODES = 12500
        N_EDGES = 400000
        D_IN = 256
        D_OUT = 256
        h = x @ w_nbr
        msgs = adj_vals[:, None] * h[edge_src]
        agg = jax.ops.segment_sum(msgs, edge_dst, num_segments=x.shape[0])
        return agg + x @ w_own + bias

    def _L0_ffn_ref(x, Wr, br, ln_g, ln_b, W1, b1, W2, b2):
        import jax, jax.numpy as jnp
        import numpy as np
        TOP_K = 2
        LN_EPS = 1e-05
        B, S, D = x.shape
        N = B * S
        xt = x.reshape(N, D)
        logits = xt @ Wr + br
        probs = jax.nn.softmax(logits, axis=-1)
        top_p, top_idx = jax.lax.top_k(probs, TOP_K)
        weights = top_p / top_p.sum(axis=-1, keepdims=True)
        mu = xt.mean(axis=-1, keepdims=True)
        var = ((xt - mu) ** 2).mean(axis=-1, keepdims=True)
        xn = (xt - mu) * jax.lax.rsqrt(var + LN_EPS)
        xe = xn[None, :, :] * ln_g[:, None, :] + ln_b[:, None, :]
        h = jax.nn.gelu(jnp.einsum('end,edh->enh', xe, W1) + b1[:, None, :], approximate=False)
        y = jnp.einsum('enh,ehd->end', h, W2) + b2[:, None, :]
        y_tok = jnp.transpose(y, (1, 0, 2))
        sel = jnp.take_along_axis(y_tok, top_idx[:, :, None], axis=1)
        out = (weights[:, :, None] * sel).sum(axis=1)
        return out.reshape(B, S, D)

    def _L1_gnn_ref(x, W, b, gamma, beta, edge_index):
        import jax, jax.numpy as jnp
        import numpy as np
        N_NODES = 6250
        N_EDGES = 100000
        DIM = 256
        N_LAYERS = 3
        LN_EPS = 1e-05

        def _gcn_norm(edge_index, n_nodes, dtype):
            row, col = (edge_index[0], edge_index[1])
            loop = jnp.arange(n_nodes, dtype=edge_index.dtype)
            row = jnp.concatenate([row, loop])
            col = jnp.concatenate([col, loop])
            deg = jax.ops.segment_sum(jnp.ones(row.shape[0], dtype=dtype), col, num_segments=n_nodes)
            dinv = jnp.where(deg > 0, jax.lax.rsqrt(deg), 0.0)
            norm = dinv[row] * dinv[col]
            return (row, col, norm)
        n = x.shape[0]
        row, col, norm = _gcn_norm(edge_index, n, x.dtype)
        for i in range(N_LAYERS):
            h = x @ W[i]
            msg = h[row] * norm[:, None]
            h = jax.ops.segment_sum(msg, col, num_segments=n) + b[i]
            mu = jnp.mean(h, axis=-1, keepdims=True)
            var = jnp.mean((h - mu) ** 2, axis=-1, keepdims=True)
            h = (h - mu) * jax.lax.rsqrt(var + LN_EPS) * gamma[i] + beta[i]
            x = jax.nn.relu(h)
        return x

    def _L1_ffn_ref(x, W_fx, b_fx, W_x, b_x, W_slice, b_slice, W_q, W_k, W_v, W_out, b_out, temperature):
        import jax, jax.numpy as jnp
        import numpy as np
        DIM = 256
        H = 8
        D = 64
        G = 64
        INNER = H * D
        SCALE = D ** (-0.5)
        B, N, _ = x.shape
        fx_mid = (x @ W_fx + b_fx).reshape(B, N, H, D).transpose(0, 2, 1, 3)
        x_mid = (x @ W_x + b_x).reshape(B, N, H, D).transpose(0, 2, 1, 3)
        temp = jnp.clip(temperature, 0.1, 5.0)
        slice_weights = jax.nn.softmax((x_mid @ W_slice + b_slice) / temp, axis=-1)
        slice_norm = slice_weights.sum(axis=2)
        slice_token = jnp.einsum('bhnc,bhng->bhgc', fx_mid, slice_weights)
        slice_token = slice_token / (slice_norm[..., None] + 1e-05)
        q = slice_token @ W_q
        k = slice_token @ W_k
        v = slice_token @ W_v
        attn = jax.nn.softmax(jnp.einsum('bhgc,bhkc->bhgk', q, k) * SCALE, axis=-1)
        out_slice = jnp.einsum('bhgk,bhkc->bhgc', attn, v)
        out_x = jnp.einsum('bhgc,bhng->bhnc', out_slice, slice_weights)
        out_x = out_x.transpose(0, 2, 1, 3).reshape(B, N, INNER)
        return out_x @ W_out + b_out
    edge_index = jnp.stack([src, dst])
    x = x + _L0_gnn_ref(_layernorm(x, axis=-1), src, dst, edge_weight, L0_gnn_w_nbr, L0_gnn_w_own, L0_gnn_bias)
    x = x + _L0_ffn_ref(_layernorm(x, axis=-1)[None], L0_ffn_Wr, L0_ffn_br, L0_ffn_ln_g, L0_ffn_ln_b, L0_ffn_W1, L0_ffn_b1, L0_ffn_W2, L0_ffn_b2)[0]
    x = x + _L1_gnn_ref(_layernorm(x, axis=-1), L1_gnn_W, L1_gnn_b, L1_gnn_gamma, L1_gnn_beta, edge_index)
    x = x + _L1_ffn_ref(_layernorm(x, axis=-1)[None], L1_ffn_W_fx, L1_ffn_b_fx, L1_ffn_W_x, L1_ffn_b_x, L1_ffn_W_slice, L1_ffn_b_slice, L1_ffn_W_q, L1_ffn_W_k, L1_ffn_W_v, L1_ffn_W_out, L1_ffn_b_out, L1_ffn_temperature)[0]
    return x

_drawn_inputs = setup_inputs


def setup_inputs(seed=0):
    import zlib

    import numpy as np

    out = dict(_drawn_inputs(seed))
    spreads = {'L0_gnn_bias': (0.0, 0.308),
     'L0_ffn_br': (0.0, 0.323),
     'L0_ffn_ln_g': (1.0, 0.6),
     'L0_ffn_ln_b': (0.0, 0.75),
     'L0_ffn_b1': (0.0, 0.744),
     'L0_ffn_b2': (0.0, 0.515),
     'L1_gnn_gamma': (1.0, 0.2),
     'L1_gnn_beta': (0.0, 0.31),
     'L1_ffn_b_fx': (0.0, 0.42),
     'L1_ffn_b_x': (0.0, 2.0),
     'L1_ffn_b_slice': (0.0, 2.0),
     'L1_ffn_b_out': (0.0, 0.434),
     'L1_ffn_temperature': (0.5, 0.6)}
    factors = {'L1_gnn_b': 4.306,
     'L1_ffn_W_x': 8.0,
     'L1_ffn_W_slice': 8.0,
     'L1_ffn_W_q': 8.0,
     'L1_ffn_W_k': 8.0}
    for name, (base, spread) in spreads.items():
        noise = np.random.default_rng([zlib.crc32(name.encode()), seed]).standard_normal(out[name].shape)
        drawn = base * np.exp(spread * noise) if base else spread * noise
        out[name] = jnp.asarray(drawn.astype(out[name].dtype))
    for name, factor in factors.items():
        out[name] = (out[name] * factor).astype(out[name].dtype)
    return out
```

```python
from contextlib import ExitStack

import concourse.bass as bass
from concourse import mybir

P = 128
F32 = mybir.dt.float32
I32 = mybir.dt.int32
U32 = mybir.dt.uint32
ALU = mybir.AluOpType
ACT = mybir.ActivationFunctionType
AX = mybir.AxisListType
EPS = 1e-5

N = 6250
D = 256
KD = D // P
NT = -(-N // P)
LAST = N - (NT - 1) * P
TG = 7
NG = NT // TG
E = 100000
ET = -(-E // P)
EC = -(-ET // P)
U = 32
NB = -(-(ET + NT - 1) // U)
STEPS = NB * U
HALF = STEPS // 2
R = 16
OH = 4
AHEAD = OH - 1
Q = 4
LOADS = 8
AW = D + 1
FAR = 1 << 27
NE = 8
HID = 1024
HJ = HID // P
BR = 2 * P
NBLK = (2 * N + NE * (BR - 1)) // BR
NBLK += NBLK % 2
SLOTS = NBLK * BR
LAYERS = 3
HEADS = 8
DH = 64
GS = 64
PAIRS = HEADS // 2
PRM = KD + KD + HJ


def build(nc, ins, out, dram):
    with ExitStack() as top:
        def sb(name, shape, dt=F32, ctx=top):
            return ctx.enter_context(nc.sbuf_tensor(name, shape, dt))

        def pb(name, ctx, shape=(P, 512), dt=F32):
            return ctx.enter_context(nc.psum_tensor(name, list(shape), dt))

        def sem(name):
            return top.enter_context(nc.semaphore(name))

        c = dict(ident=sb("ident", [P, P]), eps=sb("eps", [P, 1]), valid=sb("valid", [P, NT]), X=sb("X", [P, NT, D]))
        with ExitStack() as g:
            c.update(
                lane=sb("lane", [P, P], F32, g), ACC=sb("ACC", [P, NT, AW], F32, g),
                ones_row=sb("ones_row", [P, NT], F32, g),
                step_src=sb("step_src", [P, STEPS + R], I32, g), step_dst=sb("step_dst", [P, STEPS + AHEAD], F32, g),
                step_w=sb("step_w", [P, STEPS], F32, g), step_off=sb("step_off", [P, STEPS], I32, g),
                dinv=sb("dinv", [P, NT], F32, g),
            )
            c["ring"] = gather_ring(nc, dram["table"], sb, sem, g)
            prepare(nc, ins, dram, c, sb, pb, sem)
            first_layer(nc, ins, dram, c, sb, pb, sem)
            mixture(nc, ins, dram, c, sb, pb, sem)
            convolutions(nc, ins, dram, c, sb, pb, sem)
        slices(nc, ins, out, c, sb, pb, sem)


def prepare(nc, ins, dram, c, sb, pb, sem):
    full = (EC - 1) * P * P
    rows = (E - full) // P
    rest = E - full - rows * P
    with ExitStack() as ctx:
        src_i = sb("src_i", [P, EC, P], I32, ctx)
        dst_i = sb("dst_i", [P, EC, P], I32, ctx)
        w_f = sb("w_f", [P, EC, P], F32, ctx)
        src_f = sb("src_f", [P, EC, P], F32, ctx)
        dst_f = sb("dst_f", [P, EC, P], F32, ctx)
        tile_f = sb("tile_f", [P, EC, P], F32, ctx)
        ends_i = sb("ends_i", [P, 2, EC], I32, ctx)
        ends_b = sb("ends_b", [P, 2, EC], I32, ctx)
        ends_f = sb("ends_f", [P, 2, EC], F32, ctx)
        start_f = sb("start_f", [P, 2, EC], F32, ctx)
        step_i = sb("step_i", [P, STEPS], F32, ctx)
        sel = sb("sel", [P, EC, STEPS], F32, ctx)
        ge = sb("ge", [P, 2, STEPS], F32, ctx)
        tmp = sb("tmp", [P, STEPS], F32, ctx)
        tmp2 = sb("tmp2", [P, STEPS], F32, ctx)
        ps = [pb(f"pp{k}", ctx) for k in range(8)]
        s_clear = sem("p_clear")
        s_const = sem("p_const")
        s_x = sem("p_x")
        s_edges = sem("p_edges")
        s_ends = sem("p_ends")
        s_cast = sem("p_cast")
        s_start = sem("p_start")
        s_ge = sem("p_ge")
        s_sel = sem("p_sel")
        s_mm = sem("p_mm")
        s_out = sem("p_out")

        def by_tile(a, t):
            return [(t[:, 0:EC - 1, :], a[0:full].rearrange("(c p e) -> p c e", p=P, e=P)),
                    (t[0:rows, EC - 1, :], a[full:full + rows * P].rearrange("(p e) -> p e", e=P)),
                    (t[rows:rows + 1, EC - 1, 0:rest], a[full + rows * P:E].rearrange("(p e) -> p e", p=1))]

        def heads(a, t, shift):
            o = shift * P
            r = rows - shift
            out = [(t[:, shift, 0:EC - 1], a[o:o + full].rearrange("(c p e) -> p c e", p=P, e=P)[:, :, 0]),
                   (t[0:r, shift, EC - 1:EC], a[o + full:o + full + r * P].rearrange("(p e) -> p e", e=P)[:, 0:1]),
                   (t[r:r + 1, shift, EC - 1:EC], a[full + rows * P:full + rows * P + 1].rearrange("(p e) -> p e", p=1))]
            return out

        block = ctx.enter_context(nc.Block())

        @block.sync
        def _(sp):
            sp.wait_ge(s_clear, 5)
            for t, a in (*by_tile(ins["dst"], dst_i), *by_tile(ins["src"], src_i),
                         *by_tile(ins["edge_weight"], w_f)):
                sp.dma_start(t, a).then_inc(s_edges, 16)
            for t, a in (*heads(ins["dst"], ends_i, 0), *heads(ins["dst"], ends_i, 1)):
                sp.dma_start(t, a, allow_slow_non_contiguous=True).then_inc(s_ends, 16)

        @block.scalar
        def _(act):
            act.wait_ge(s_clear, 5)
            x = ins["x"]
            act.dma_start(c["X"][:, 0:NT - 1, :], x[0:(NT - 1) * P, :].rearrange("(t p) d -> p t d", p=P)).then_inc(s_x, 16)
            act.dma_start(c["X"][0:LAST, NT - 1, :], x[(NT - 1) * P:N, :]).then_inc(s_x, 16)
            act.wait_ge(s_x, 32)

        @block.gpsimd
        def _(g):
            nc.gpsimd.iota(step_i[:, :], [[1, STEPS]], base=0, channel_multiplier=0,
                           allow_small_or_imprecise_dtypes=True).then_inc(s_const, 1)
            nc.gpsimd.iota(tile_f[:, :, :], [[P, EC], [0, P]], base=0, channel_multiplier=1,
                           allow_small_or_imprecise_dtypes=True).then_inc(s_const, 1)
            nc.gpsimd.iota(c["lane"][:, :], [[1, P]], base=0, channel_multiplier=0,
                           allow_small_or_imprecise_dtypes=True).then_inc(s_const, 1)
            nc.gpsimd.memset(c["ident"][:, :], 0.0).then_inc(s_const, 1)
            g.wait_ge(s_const, 4)
            nc.gpsimd.affine_select(out=c["ident"][:, :], in_=c["ident"][:, :], compare_op=ALU.not_equal,
                                    fill=1.0, base=0, pattern=[[-1, P]], channel_multiplier=1).then_inc(s_const, 1)

        @block.vector
        def _(v):
            v.memset(dst_i[:, EC - 1, :], -1).then_inc(s_clear, 1)
            v.memset(src_i[:, EC - 1, :], 0).then_inc(s_clear, 1)
            v.memset(w_f[:, EC - 1, :], 0.0).then_inc(s_clear, 1)
            v.memset(ends_i[:, :, :], FAR).then_inc(s_clear, 1)
            v.memset(c["X"][:, NT - 1, :], 0.0).then_inc(s_clear, 1)
            v.memset(c["eps"][:, :], EPS)
            v.memset(c["ones_row"][:, :], 1.0)
            v.memset(c["step_dst"][:, STEPS:STEPS + AHEAD], -1.0)
            v.memset(c["step_src"][:, STEPS:STEPS + R], 0)
            v.wait_ge(s_ends, 16 * 6)
            v.tensor_scalar(ends_b[:, :, :], ends_i[:, :, :], 7, None, ALU.arith_shift_right).then_inc(s_start, 1)
            v.wait_ge(s_start, 1)
            v.tensor_copy(ends_f[:, :, :], ends_b[:, :, :]).then_inc(s_start, 1)
            v.wait_ge(s_start, 2)
            v.wait_ge(s_const, 5)
            for k in range(2):
                v.tensor_tensor(start_f[:, k, :], ends_f[:, k, :], tile_f[:, :, 0], ALU.add).then_inc(s_start, 1)
            v.wait_ge(s_start, 4)
            v.tensor_scalar(start_f[:, 1, :], start_f[:, 1, :], 1.0, None, ALU.add).then_inc(s_start, 1)
            v.wait_ge(s_start, 5)
            for k in range(EC):
                if k >= 2:
                    v.wait_ge(s_sel, k - 1)
                v.tensor_scalar(ge[:, k % 2, :], step_i[:, :], start_f[:, 0, k:k + 1], None, ALU.is_ge).then_inc(s_ge, 1)
                v.wait_ge(s_ge, k + 1)
                v.scalar_tensor_tensor(out=sel[:, k, :], in0=step_i[:, :], scalar=start_f[:, 1, k:k + 1],
                                       in1=ge[:, k % 2, :], op0=ALU.is_lt, op1=ALU.mult).then_inc(s_sel, 1)
            v.wait_ge(s_edges, 16 * 9)
            v.tensor_copy(src_f[:, :, :], src_i[:, :, :]).then_inc(s_cast, 1)
            v.tensor_scalar(dst_f[:, :, :], dst_i[:, :, :], 1.0, None, ALU.add).then_inc(s_cast, 1)
            v.wait_ge(s_mm, 8)
            n = 0
            for h in range(2):
                r = slice(h * HALF, h * HALF + HALF)
                v.tensor_copy(c["step_src"][:, r], ps[0 + h][:, 0:HALF])
                v.tensor_copy(c["step_w"][:, r], ps[4 + h][:, 0:HALF])
                v.tensor_tensor(tmp[:, r], step_i[:, r], ps[6 + h][:, 0:HALF], ALU.subtract).then_inc(s_out, 1)
                n += 1
                v.wait_ge(s_out, n)
                v.tensor_scalar(c["step_off"][:, r], tmp[:, r], float(NT - 1), float(AW), ALU.min, ALU.mult)
                v.tensor_scalar(tmp2[:, r], tmp[:, r], float(-P), -1.0, ALU.mult, ALU.add).then_inc(s_out, 1)
                n += 1
                v.wait_ge(s_out, n)
                v.tensor_tensor(c["step_dst"][:, r], tmp2[:, r], ps[2 + h][:, 0:HALF], ALU.add)

        @block.tensor
        def _(pe):
            pe.wait_ge(s_const, 5)
            pe.wait_ge(s_sel, EC)
            pe.wait_ge(s_edges, 16 * 9)
            pe.wait_ge(s_cast, 2)
            for q, lst in enumerate((src_f, dst_f, w_f, tile_f)):
                for h in range(2):
                    for k in range(EC):
                        mm = pe.matmul(ps[2 * q + h][:, 0:HALF], lst[:, k, :], sel[:, k, h * HALF:(h + 1) * HALF],
                                       start=(k == 0), stop=(k == EC - 1))
                    mm.then_inc(s_mm, 1)


def settle(eng):
    eng.nop(nofuse=True)


def gather_ring(nc, table, sb, sem, ctx):
    return dict(
        rows=sb("rows", [P, R, AW], F32, ctx), now=sb("now", [P, R], I32, ctx), hot=sb("hot", [P, OH, P], F32, ctx),
        table=table, s_now=sem("s_now"), s_row=[sem(f"s_row{u}") for u in range(R)],
        s_scaled=sem("s_scaled"), s_hot=sem("s_hot"), s_mm=sem("s_mm"), s_add=sem("s_add"),
    )


def steps_pool(nc, c, r, g, layer):
    with g.Fori(0, NB) as i:
        now = g.snap((layer * NB + i) * (U // Q) + layer * (R // Q))
        for u in range(U):
            x = u % R
            if u % Q == 0:
                g.wait_ge(r["s_now"], now + (u // Q + 1))
                settle(g)
            nc.gpsimd.indirect_dma_start(
                out=r["rows"][:, x, 0:D], out_offset=None, in_=r["table"][:, :],
                in_offset=bass.IndirectOffsetOnAxis(ap=r["now"][:, x:x + 1], axis=0)).then_inc(r["s_row"][x], 16)


def steps_tensor(nc, c, r, pe, psum, width, layer):
    with pe.Fori(0, NB) as i:
        landed = [pe.snap((layer * NB + i) * (16 * U // R) + 16 * (n + 1)) for n in range(U // R)]
        step = pe.snap((layer * NB + i) * U)
        hots = pe.snap(step + layer * AHEAD)
        for u in range(U):
            if layer == 0 if isinstance(layer, int) else False:
                if u % 2 == 0:
                    pe.wait_ge(r["s_scaled"], step + (u + 2))
            else:
                pe.wait_ge(r["s_row"][u % R], landed[u // R])
            if u % 2 == 0:
                pe.wait_ge(r["s_hot"], hots + (u + 2))
                pe.wait_ge(r["s_add"], step + (u + 2))
            pe.matmul(psum[u % OH][:, 0:width], r["hot"][:, u % OH, :], r["rows"][:, u % R, 0:width],
                      start=True, stop=True).then_inc(r["s_mm"], 1)


def steps_vector(nc, c, r, v, psum, width, layer):
    acc = c["ACC"][:, :, :].rearrange("p t d -> p (t d)")

    def hot(s, slot):
        v.tensor_scalar(r["hot"][:, slot, :], c["lane"][:, :], c["step_dst"][:, bass.ds(s, 1)], None,
                        ALU.is_equal).then_inc(r["s_hot"], 1)

    def indices(s, slot):
        v.tensor_copy(r["now"][:, slot:slot + Q], c["step_src"][:, bass.ds(s, Q)]).then_inc(r["s_now"], 1)

    for u in range(0, R, Q):
        indices(u, u)
    for s in range(AHEAD):
        hot(s, s)
    with v.Fori(0, NB) as i:
        col = v.snap(i * U)
        step = v.snap((layer * NB + i) * U)
        for u in range(U):
            hot(col + (u + AHEAD), (u + AHEAD) % OH)
            if u % LOADS == 0:
                _, offs = nc.values_load_multi_w_load_instructions(
                    c["step_off"][0:1, bass.ds(col + u, LOADS)], engines=(mybir.EngineType.DVE,),
                    min_val=0, max_val=AW * (NT - 1),
                    skip_runtime_bounds_check_because="prepare() keeps every step's bucket within 0 and NT - 1")
            a = acc[:, bass.ds(offs[u % LOADS], width)]
            v.wait_ge(r["s_mm"], step + (u + 1))
            v.wait_ge(r["s_add"], step + (u + OH))
            v.tensor_tensor(a, psum[u % OH][:, 0:width], a, ALU.add).then_inc(r["s_add"], 1)
            if u % Q == Q - 1:
                indices(col + (u + 1 - Q + R), (u + 1 - Q) % R)


def steps_scale(nc, c, r, act, layer):
    with act.Fori(0, NB) as i:
        landed = [act.snap((layer * NB + i) * (16 * U // R) + 16 * (n + 1)) for n in range(U // R)]
        col = act.snap(i * U)
        for u in range(U):
            act.wait_ge(r["s_row"][u % R], landed[u // R])
            settle(act)
            act.activation(r["rows"][:, u % R, 0:D], r["rows"][:, u % R, 0:D], ACT.Copy,
                           scale=c["step_w"][:, bass.ds(col + u, 1)]).then_inc(r["s_scaled"], 1)


def credits(nc, r, v):
    v.memset(r["rows"][:, :, D:AW], 1.0)
    v.memset(r["hot"][:, :, :], 0.0).then_inc(r["s_add"], OH)


def first_layer(nc, ins, dram, c, sb, pb, sem):
    with ExitStack() as ctx:
        r = c["ring"]
        w = sb("w_both", [P, KD, 2 * D], F32, ctx)
        bias = sb("bias_a", [P, D], F32, ctx)
        xn = sb("xn_a", [P, TG, D], F32, ctx)
        xt = sb("xt_a", [P, TG, D], F32, ctx)
        h = sb("h_a", [P, NT, D], F32, ctx)
        stat = sb("stat_a", [P, TG, 6], F32, ctx)
        mv = sb("mv_a", [P, TG, 2], F32, ctx)
        sd = sb("sd_a", [P, TG], F32, ctx)
        rs = sb("rs_a", [P, TG], F32, ctx)
        s_w = sem("n_w")
        s_stat = sem("n_stat")
        s_mv = sem("n_mv")
        s_sd = sem("n_sd")
        s_rs = sem("n_rs")
        s_xn = sem("n_xn")
        s_T = sem("n_T")
        s_xt = sem("n_xt")
        s_M = sem("n_M")
        s_h = sem("n_h")
        s_own = sem("n_own")
        s_acc = sem("n_acc")
        s_tab = sem("n_tab")

        with ExitStack() as pc, nc.Block() as block:
            pT = [pb(f"pT_a{k}", pc) for k in range(2)]
            pN = [pb(f"pN_a{k}", pc) for k in range(3)]
            pO = [pb(f"pO_a{k}", pc) for k in range(3)]

            @block.sync
            def _(sp):
                sp.dma_start(w[:, :, 0:D], ins["L0_gnn_w_nbr"].rearrange("(k p) d -> p k d", p=P)).then_inc(s_w, 16)
                sp.dma_start(w[:, :, D:2 * D], ins["L0_gnn_w_own"].rearrange("(k p) d -> p k d", p=P)).then_inc(s_w, 16)
                sp.dma_start(bias[:, :], ins["L0_gnn_bias"].rearrange("(o d) -> o d", o=1).to_broadcast([P, D])).then_inc(s_w, 16)
                table = dram["table"].rearrange("(t p) d -> p t d", p=P)
                with sp.Fori(0, NG) as g:
                    sp.wait_ge(s_h, g * TG + TG)
                    sp.dma_start(table[:, bass.ds(g * TG, TG), :], h[:, bass.ds(g * TG, TG), :]).then_inc(s_tab, 16)
                sp.wait_ge(s_tab, 16 * NG)

            @block.vector
            def _(v):
                credits(nc, r, v)
                v.wait_ge(s_w, 48)
                with v.Fori(0, NG) as g:
                    for u in range(TG):
                        v.bn_stats(stat[:, u, :], c["X"][:, g * TG + u, :]).then_inc(s_stat, 1)
                    v.wait_ge(s_stat, g * TG + TG)
                    settle(v)
                    for u in range(TG):
                        v.bn_aggr(mv[:, u, :], stat[:, u, :]).then_inc(s_mv, 1)
                    v.wait_ge(s_sd, g + 1)
                    v.reciprocal(rs[:, :], sd[:, :]).then_inc(s_rs, 1)
                    v.wait_ge(s_rs, g + 1)
                    for u in range(TG):
                        v.wait_ge(s_M, g * TG + 1)
                        v.tensor_scalar(xn[:, u, :], c["X"][:, g * TG + u, :], mv[:, u, 0:1], rs[:, u:u + 1],
                                        ALU.subtract, ALU.mult).then_inc(s_xn, 1)
                    for u in range(TG):
                        t = g * TG + u
                        v.wait_ge(s_M, t + 2)
                        v.tensor_tensor(c["ACC"][:, t, 0:D], pO[u % 3][:, 0:D], c["X"][:, t, :], ALU.add).then_inc(s_own, 1)
                        v.wait_ge(s_own, t + 1)
                        v.tensor_tensor(c["ACC"][:, t, 0:D], c["ACC"][:, t, 0:D], bias[:, :], ALU.add).then_inc(s_acc, 1)
                v.memset(c["ACC"][:, :, D:AW], 1.0)

            @block.scalar
            def _(act):
                with act.Fori(0, NG) as g:
                    act.wait_ge(s_mv, g * TG + TG)
                    act.activation(sd[:, :], mv[:, :, 1], ACT.Sqrt, bias=c["eps"][:, 0:1]).then_inc(s_sd, 1)
                    for u in range(TG + 1):
                        if u < TG:
                            t = g * TG + u
                            act.wait_ge(s_T, t + 1)
                            act.activation(xt[:, u, :], pT[u % 2][:, 0:D], ACT.Copy).then_inc(s_xt, 1)
                        if u > 0:
                            t = g * TG + u - 1
                            act.wait_ge(s_M, t + 2)
                            settle(act)
                            act.activation(h[:, t, :], pN[(u - 1) % 3][:, 0:D], ACT.Copy).then_inc(s_h, 1)

            @block.tensor
            def _(pe):
                pe.wait_ge(s_w, 48)
                pe.matmul(pN[0][:, 0:P], c["ident"][:, :], c["ident"][:, :], start=True, stop=True).then_inc(s_M, 1)

                def turn(g, u):
                    pe.wait_ge(s_xn, g * TG + u + 1)
                    if u >= 2:
                        pe.wait_ge(s_xt, g * TG + u - 1)
                    for k in range(KD):
                        mm = pe.transpose(pT[u % 2][:, k * P:(k + 1) * P], xn[:, u, k * P:(k + 1) * P], c["ident"][:, :])
                    mm.then_inc(s_T, 1)

                with pe.Fori(0, NG) as g:
                    turn(g, 0)
                    for u in range(TG):
                        if u + 1 < TG:
                            turn(g, u + 1)
                        t = g * TG + u
                        pe.wait_ge(s_xt, t + 1)
                        if u >= 3:
                            pe.wait_ge(s_h, t - 2)
                            pe.wait_ge(s_own, t - 2)
                        for n, bank in enumerate((pN[u % 3], pO[u % 3])):
                            for k in range(KD):
                                mm = pe.matmul(bank[:, 0:D], xt[:, u, k * P:(k + 1) * P], w[:, k, n * D:(n + 1) * D],
                                               start=(k == 0), stop=(k == KD - 1))
                        mm.then_inc(s_M, 1)

        with ExitStack() as pc, nc.Block() as block:
            psum = [pb(f"pa{k}", pc) for k in range(OH)]

            @block.gpsimd
            def _(g):
                steps_pool(nc, c, r, g, 0)

            @block.scalar
            def _(act):
                steps_scale(nc, c, r, act, 0)

            @block.tensor
            def _(pe):
                steps_tensor(nc, c, r, pe, psum, AW, 0)

            @block.vector
            def _(v):
                steps_vector(nc, c, r, v, psum, AW, 0)



def wait(eng, s, value):
    if not isinstance(value, int) or value > 0:
        eng.wait_ge(s, value)


def route(nc, ins, dram, c, moe, sb, pb, sem):
    with ExitStack() as ctx:
        u1 = sb("u_r", [P, TG, D], F32, ctx)
        ut = sb("ut_r", [P, TG, D], F32, ctx)
        wr = sb("wr_r", [P, KD, NE], F32, ctx)
        br = sb("br_r", [P, NE], F32, ctx)
        lg = sb("lg_r", [P, TG, NE], F32, ctx)
        zero = sb("zero_r", [P, 2 * D], F32, ctx)
        stat = sb("stat_r", [P, TG, 6], F32, ctx)
        mv = sb("mv_r", [P, TG, 2], F32, ctx)
        sd = sb("sd_r", [P, TG], F32, ctx)
        rs = sb("rs_r", [P, TG], F32, ctx)
        t8 = sb("t8_r", [P, TG, 8], F32, ctx)
        i8 = sb("i8_r", [P, TG, 8], U32, ctx)
        dsd = sb("dsd_r", [P, NT], F32, ctx)
        s_w, s_zero, s_fill = sem("r_w"), sem("r_zero"), sem("r_fill")
        s_deg, s_stat, s_mv, s_sd, s_rs = sem("r_deg"), sem("r_stat"), sem("r_mv"), sem("r_sd"), sem("r_rs")
        s_u, s_x, s_T, s_ut, s_L, s_lg, s_top = (sem("r_u"), sem("r_x"), sem("r_T"), sem("r_ut"), sem("r_L"),
                                                 sem("r_lg"), sem("r_top"))
        pT = [pb(f"pT_r{k}", ctx) for k in range(3)]
        pL = [pb(f"pL_r{k}", ctx) for k in range(3)]
        block = ctx.enter_context(nc.Block())

        @block.sync
        def _(sp):
            sp.dma_start(wr[:, :, :], ins["L0_ffn_Wr"].rearrange("(k p) e -> p k e", p=P)).then_inc(s_w, 16)
            sp.dma_start(br[:, :], ins["L0_ffn_br"].rearrange("(o e) -> o e", o=1).to_broadcast([P, NE])).then_inc(s_w, 16)
            for e in range(NE):
                at = 0
                for name, n in (("L0_ffn_ln_g", KD), ("L0_ffn_ln_b", KD), ("L0_ffn_b1", HJ)):
                    sp.dma_start(moe["prm"][:, e, at:at + n], ins[name][e, :].rearrange("(k p) -> p k", p=P),
                                 allow_slow_non_contiguous=True).then_inc(s_w, 16)
                    at += n
            sp.wait_ge(s_zero, 1)
            sp.dma_start(dram["disp"].rearrange("(b p r) d -> p b (r d)", p=P, r=2),
                         zero[:, :].rearrange("p (o d) -> p o d", o=1).to_broadcast([P, NBLK + 1, 2 * D])).then_inc(s_fill, 16)
            sp.dma_start(dram["y"][SLOTS:SLOTS + BR, :].rearrange("(p r) d -> p (r d)", r=2), zero[:, :]).then_inc(s_fill, 16)
            sp.wait_ge(s_fill, 32)
            sp.wait_ge(s_w, 16 * (2 + 3 * NE))

        @block.vector
        def _(v):
            v.memset(zero[:, :], 0.0).then_inc(s_zero, 1)
            v.wait_ge(s_deg, 1)
            v.reciprocal(c["dinv"][:, :], dsd[:, :])
            v.wait_ge(s_w, 16 * (2 + 3 * NE))

            def normalise(g, src, dst, r, done):
                for u in range(TG):
                    v.bn_stats(stat[:, u, :], src(u)).then_inc(s_stat, 1)
                v.wait_ge(s_stat, r * TG + TG)
                settle(v)
                for u in range(TG):
                    v.bn_aggr(mv[:, u, :], stat[:, u, :]).then_inc(s_mv, 1)
                v.wait_ge(s_sd, r + 1)
                v.reciprocal(rs[:, :], sd[:, :]).then_inc(s_rs, 1)
                v.wait_ge(s_rs, r + 1)
                for u in range(TG):
                    v.tensor_scalar(dst(u), src(u), mv[:, u, 0:1], rs[:, u:u + 1],
                                    ALU.subtract, ALU.mult).then_inc(done, 1)

            with v.Fori(0, NG) as g:
                normalise(g, lambda u: c["ACC"][:, g * TG + u, 0:D], lambda u: u1[:, u, :], g * 2, s_u)
                v.wait_ge(s_u, g * TG + TG)
                normalise(g, lambda u: u1[:, u, :], lambda u: c["X"][:, g * TG + u, :], g * 2 + 1, s_x)
                for u in range(TG):
                    v.wait_ge(s_L, g * TG + u + 1)
                    v.tensor_tensor(lg[:, u, :], pL[u % 3][:, 0:NE], br[:, :], ALU.add).then_inc(s_lg, 1)
                v.wait_ge(s_lg, g * TG + TG)
                settle(v)
                for u in range(TG):
                    v.max(t8[:, u, :], lg[:, u, :]).then_inc(s_top, 1)
                v.wait_ge(s_top, g * (3 * TG) + TG)
                settle(v)
                for u in range(TG):
                    v.max_index(i8[:, u, :], t8[:, u, :], lg[:, u, :]).then_inc(s_top, 2)
                v.wait_ge(s_top, g * (3 * TG) + 3 * TG)
                settle(v)
                v.tensor_copy(moe["top"][:, bass.ds(g * TG, TG), :], t8[:, :, 0:2])
                v.tensor_copy(moe["idx"][:, bass.ds(g * TG, TG), :], i8[:, :, 0:2])

        @block.scalar
        def _(act):
            act.activation(dsd[:, :], c["ACC"][:, :, D], ACT.Sqrt).then_inc(s_deg, 1)
            with act.Fori(0, NG) as g:
                for k in range(2):
                    act.wait_ge(s_mv, (g * 2 + k) * TG + TG)
                    act.activation(sd[:, :], mv[:, :, 1], ACT.Sqrt, bias=c["eps"][:, 0:1]).then_inc(s_sd, 1)
                for u in range(TG):
                    act.wait_ge(s_T, g * TG + u + 1)
                    act.activation(ut[:, u, :], pT[u % 3][:, 0:D], ACT.Copy).then_inc(s_ut, 1)

        @block.tensor
        def _(pe):
            pe.wait_ge(s_w, 16 * (2 + 3 * NE))

            def turn(g, u):
                pe.wait_ge(s_u, g * TG + u + 1)
                if u >= 3:
                    pe.wait_ge(s_ut, g * TG + u - 2)
                for k in range(KD):
                    mm = pe.transpose(pT[u % 3][:, k * P:(k + 1) * P], u1[:, u, k * P:(k + 1) * P], c["ident"][:, :])
                mm.then_inc(s_T, 1)

            with pe.Fori(0, NG) as g:
                turn(g, 0)
                for u in range(TG):
                    if u + 1 < TG:
                        turn(g, u + 1)
                    pe.wait_ge(s_ut, g * TG + u + 1)
                    if u >= 3:
                        pe.wait_ge(s_lg, g * TG + u - 2)
                    for k in range(KD):
                        mm = pe.matmul(pL[u % 3][:, 0:NE], ut[:, u, k * P:(k + 1) * P], wr[:, k, :],
                                       start=(k == 0), stop=(k == KD - 1))
                    mm.then_inc(s_L, 1)


def place(nc, c, moe, sb, pb, sem):
    with ExitStack() as ctx:
        EN = NE * NT
        node = sb("node", [P, NT], F32, ctx)
        blk = sb("blk", [P, NBLK + 1], F32, ctx)
        before = sb("before", [P, P], F32, ctx)
        ones = sb("ones", [P, P], F32, ctx)
        idxf = sb("idxf", [P, 2, NT], F32, ctx)
        gap = sb("gap", [P, NT], F32, ctx)
        ratio = sb("ratio", [P, NT], F32, ctx)
        den = sb("den", [P, NT], F32, ctx)
        spare = sb("spare", [P, 2, NT], F32, ctx)
        mk = sb("mk", [P, 2, NE, NT], F32, ctx)
        m = sb("m", [P, NE, NT], F32, ctx)
        cnt = sb("cnt", [P, NE, NT], F32, ctx)
        inc = sb("inc", [P, NE, NT], F32, ctx)
        row = sb("row", [P, NE, NT], F32, ctx)
        nbi = sb("nbi", [P, 2, NE], I32, ctx)
        nbf = sb("nbf", [P, NE], F32, ctx)
        cum = sb("cum", [P, NE], F32, ctx)
        base = sb("base", [P, NE], F32, ctx)
        posf = sb("posf", [P, 2, NT], F32, ctx)
        ebf = sb("ebf", [P, NBLK + 1], F32, ctx)
        pW, pC = pb("pW", ctx), pb("pC", ctx)
        s_c, s_v, s_e, s_r, s_mm = sem("l_const"), sem("l_step"), sem("l_exp"), sem("l_gap"), sem("l_mm")
        s_m = sem("l_m")
        block = ctx.enter_context(nc.Block())

        @block.gpsimd
        def _(g):
            nc.gpsimd.iota(node[:, :], [[P, NT]], base=0, channel_multiplier=1,
                           allow_small_or_imprecise_dtypes=True).then_inc(s_c, 1)
            nc.gpsimd.iota(blk[:, :], [[1, NBLK + 1]], base=0, channel_multiplier=0,
                           allow_small_or_imprecise_dtypes=True).then_inc(s_c, 1)
            nc.gpsimd.memset(ones[:, :], 1.0).then_inc(s_c, 1)
            g.wait_ge(s_c, 3)
            nc.gpsimd.affine_select(out=before[:, :], in_=ones[:, :], compare_op=ALU.is_gt, fill=0.0,
                                    base=0, pattern=[[1, P]], channel_multiplier=-1).then_inc(s_c, 1)

        @block.scalar
        def _(act):
            act.wait_ge(s_r, 1)
            act.activation(ratio[:, :], gap[:, :], ACT.Exp).then_inc(s_e, 1)

        @block.tensor
        def _(pe):
            pe.wait_ge(s_c, 4)
            pe.wait_ge(s_m, 1)
            mf = m[:, :, :].rearrange("p e t -> p (e t)")
            pe.matmul(pW[:, 0:EN], before[:, :], mf, start=True, stop=True).then_inc(s_mm, 1)
            pe.matmul(pC[:, 0:EN], ones[:, :], mf, start=True, stop=True).then_inc(s_mm, 1)

        @block.vector
        def _(v):
            n = [0]

            def then(ins):
                ins.then_inc(s_v, 1)
                n[0] += 1
                v.wait_ge(s_v, n[0])

            v.wait_ge(s_c, 4)
            v.tensor_tensor(gap[:, :], moe["top"][:, :, 1], moe["top"][:, :, 0], ALU.subtract).then_inc(s_r, 1)
            v.tensor_scalar(c["valid"][:, :], node[:, :], float(N), None, ALU.is_lt)
            for k in range(2):
                ins = v.tensor_copy(idxf[:, k, :], moe["idx"][:, :, k])
            then(ins)
            for k in range(2):
                for e in range(NE):
                    ins = v.scalar_tensor_tensor(out=mk[:, k, e, :], in0=idxf[:, k, :], scalar=float(e),
                                                 in1=c["valid"][:, :], op0=ALU.is_equal, op1=ALU.mult)
            then(ins)
            v.tensor_tensor(m[:, :, :], mk[:, 0, :, :], mk[:, 1, :, :], ALU.add).then_inc(s_m, 1)
            v.wait_ge(s_e, 1)
            then(v.tensor_scalar(den[:, :], ratio[:, :], 1.0, None, ALU.add))
            then(v.reciprocal(moe["wt"][:, 0, :], den[:, :]))
            v.tensor_tensor(moe["wt"][:, 1, :], moe["wt"][:, 0, :], ratio[:, :], ALU.mult)
            for k in range(2):
                v.tensor_scalar(spare[:, k, :], node[:, :], float(SLOTS - (NT - 1) * P + k * P), None, ALU.add)
            then(v.tensor_scalar(gap[:, :], c["valid"][:, :], -1.0, 1.0, ALU.mult, ALU.add))
            for k in range(2):
                ins = v.tensor_tensor(spare[:, k, :], spare[:, k, :], gap[:, :], ALU.mult)
            then(ins)
            v.wait_ge(s_mm, 2)
            then(v.tensor_copy(cnt[:, :, :], pC[:, 0:EN].rearrange("p (e t) -> p e t", e=NE)))
            for e in range(NE):
                ins = v.tensor_tensor_scan(out=inc[:, e, :], data0=c["ones_row"][:, :], data1=cnt[:, e, :],
                                           initial=0.0, op0=ALU.mult, op1=ALU.add)
            then(ins)
            then(v.tensor_scalar(nbi[:, 0, :], inc[:, :, NT - 1], float(BR - 1), None, ALU.add))
            then(v.tensor_scalar(nbi[:, 1, :], nbi[:, 0, :], 8, None, ALU.arith_shift_right))
            then(v.tensor_copy(nbf[:, :], nbi[:, 1, :]))
            then(v.tensor_tensor_scan(out=cum[:, :], data0=c["ones_row"][:, 0:NE], data1=nbf[:, :],
                                      initial=0.0, op0=ALU.mult, op1=ALU.add))
            then(v.tensor_tensor(base[:, :], cum[:, :], nbf[:, :], ALU.subtract))
            then(v.tensor_scalar(base[:, :], base[:, :], float(BR), None, ALU.mult))
            then(v.tensor_tensor(row[:, :, :], inc[:, :, :], cnt[:, :, :], ALU.subtract))
            then(v.tensor_tensor(row[:, :, :], row[:, :, :], pW[:, 0:EN].rearrange("p (e t) -> p e t", e=NE), ALU.add))
            for e in range(NE):
                ins = v.tensor_scalar(row[:, e, :], row[:, e, :], base[:, e:e + 1], None, ALU.add)
            then(ins)
            for k in range(2):
                ins = v.tensor_tensor(mk[:, k, :, :], mk[:, k, :, :], row[:, :, :], ALU.mult)
            then(ins)
            for k in range(2):
                ins = v.tensor_reduce(posf[:, k, :], mk[:, k, :, :].rearrange("p e t -> p t e"), AX.X, ALU.add)
            then(ins)
            v.tensor_tensor(moe["pos"][:, :, :], posf[:, :, :], spare[:, :, :], ALU.add)
            then(v.memset(ebf[:, :], 0.0))
            for e in range(NE):
                then(v.scalar_tensor_tensor(out=ebf[:, :], in0=blk[:, :], scalar=cum[:, e:e + 1], in1=ebf[:, :],
                                            op0=ALU.is_ge, op1=ALU.add))
            v.tensor_scalar(moe["expert"][:, :], ebf[:, :], float(NE - 1), None, ALU.min)


def dispatch(nc, dram, c, moe, sb, sem):
    with ExitStack() as ctx:
        stage = sb("stage_d", [P, TG, D], F32, ctx)
        now = sb("now_d", [P, 2, TG], I32, ctx)
        s_now, s_stage, s_put = sem("d_now"), sem("d_stage"), sem("d_put")
        block = ctx.enter_context(nc.Block())

        @block.scalar
        def _(act):
            def body(g):
                wait(act, s_put, g * (32 * TG))
                if not isinstance(g, int):
                    settle(act)
                for u in range(TG):
                    act.activation(stage[:, u, :], c["X"][:, g * TG + u, :], ACT.Copy).then_inc(s_stage, 1)
            body(0)
            with act.Fori(1, NG) as g:
                body(g)

        @block.gpsimd
        def _(q):
            def body(g):
                wait(q, s_put, g * (32 * TG))
                if not isinstance(g, int):
                    settle(q)
                for k in range(2):
                    nc.gpsimd.tensor_copy(now[:, k, :], moe["pos"][:, k, bass.ds(g * TG, TG)]).then_inc(s_now, 1)
                q.wait_ge(s_now, g * 2 + 2)
                for u in range(TG):
                    q.wait_ge(s_stage, g * TG + u + 1)
                    settle(q)
                    for k in range(2):
                        nc.gpsimd.indirect_dma_start(
                            out=dram["disp"][:, :], out_offset=bass.IndirectOffsetOnAxis(ap=now[:, k, u:u + 1], axis=0),
                            in_=stage[:, u, :], in_offset=None).then_inc(s_put, 16)
            body(0)
            with q.Fori(1, NG) as g:
                body(g)
            q.wait_ge(s_put, NG * 32 * TG)


def experts(nc, ins, dram, c, moe, sb, pb, sem):
    with ExitStack() as ctx:
        w1 = sb("w1_e", [P, 2, KD, HID], F32, ctx)
        w2 = sb("w2_e", [P, 2, HJ, D], F32, ctx)
        b2 = sb("b2_e", [P, 2, D], F32, ctx)
        tok = sb("tok_e", [P, 2, 2, D], F32, ctx)
        prm = sb("prm_e", [P, 2, PRM], F32, ctx)
        xe = sb("xe_e", [P, 2, KD, BR], F32, ctx)
        h = sb("h_e", [P, HJ, BR], F32, ctx)
        y = sb("y_e", [P, 2, 2, D], F32, ctx)
        pT = pb("pT_e", ctx)
        pH = [pb(f"pH_e{k}", ctx) for k in range(HJ // 2)]
        pY = [pb(f"pY_e{k}", ctx) for k in range(2)]
        s_w = [sem(f"e_w{q}") for q in range(2)]
        s_tok = [sem(f"e_tok{q}") for q in range(2)]
        s_st = [sem(f"e_store{q}") for q in range(2)]
        s_prm, s_T, s_xe, s_mm1, s_h, s_mm2, s_y = (sem("e_prm"), sem("e_T"), sem("e_xe"), sem("e_mm1"), sem("e_h"),
                                                    sem("e_mm2"), sem("e_y"))
        rows = dram["disp"].rearrange("(b m p) d -> p b m d", m=2, p=P)
        yrows = dram["y"].rearrange("(b m p) d -> p b m d", m=2, p=P)
        w1_d = ins["L0_ffn_W1"].rearrange("e (k p) h -> p e k h", p=P)
        w2_d = ins["L0_ffn_W2"].rearrange("e (j p) d -> p e j d", p=P)
        b2_d = ins["L0_ffn_b2"]
        block = ctx.enter_context(nc.Block())

        def pairs(eng, body):
            body(0)
            with eng.Fori(1, NBLK // 2) as i:
                body(i)

        @block.sync
        def _(sp):
            def tokens(b, q, use):
                wait(sp, s_T, b - 1)
                sp.dma_start(tok[:, q, :, :], rows[:, b, :, :]).then_inc(s_tok[q], 16)

            tokens(0, 0, 0)

            def body(i):
                for q in range(2):
                    b = i * 2 + q
                    e = sp.value_load(moe["expert"][0:1, bass.ds(b, 1)], min_val=0, max_val=NE - 1)
                    wait(sp, s_mm2, b - 1)
                    sp.dma_start(w1[:, q, :, :], w1_d[:, bass.ds(e, 1), :, :].rearrange("p o k h -> p (o k) h")).then_inc(s_w[q], 16)
                    sp.dma_start(w2[:, q, :, :], w2_d[:, bass.ds(e, 1), :, :].rearrange("p o j d -> p (o j) d")).then_inc(s_w[q], 16)
                    wait(sp, s_y, b * 2 - 2)
                    sp.dma_start(b2[:, q, :], b2_d[bass.ds(e, 1), :].to_broadcast([P, D])).then_inc(s_w[q], 16)
                    tokens(b + 1, 1 - q, None)
            pairs(sp, body)

        @block.vector
        def _(v):
            def inputs(b, q):
                e = v.value_load(moe["expert"][0:1, bass.ds(b, 1)], min_val=0, max_val=NE - 1)
                wait(v, s_h, b * 4 - 4)
                v.tensor_copy(prm[:, q, :], moe["prm"][:, bass.ds(e, 1), :].rearrange("p o n -> p (o n)")).then_inc(s_prm, 1)
                v.wait_ge(s_prm, b + 1)
                v.wait_ge(s_T, b + 1)
                for k in range(KD):
                    ins_ = v.tensor_scalar(xe[:, q, k, :], pT[:, k * BR:(k + 1) * BR], prm[:, q, k:k + 1],
                                           prm[:, q, KD + k:KD + k + 1], ALU.mult, ALU.add)
                ins_.then_inc(s_xe, 1)

            inputs(0, 0)

            def body(i):
                for q in range(2):
                    b = i * 2 + q
                    inputs(b + 1, 1 - q)
                    wait(v, s_st[q], i * 16)
                    if not isinstance(i, int):
                        settle(v)
                    v.wait_ge(s_mm2, b + 1)
                    for m in range(2):
                        v.tensor_tensor(y[:, q, m, :], pY[m][:, 0:D], b2[:, q, :], ALU.add).then_inc(s_y, 1)
            pairs(v, body)

        @block.scalar
        def _(act):
            def body(i):
                for q in range(2):
                    b = i * 2 + q
                    for j in range(HJ // 2):
                        act.wait_ge(s_mm1, b * (HJ // 2) + j + 1)
                        for n in range(2):
                            k = 2 * j + n
                            a = act.activation(h[:, k, :], pH[j][:, n * BR:(n + 1) * BR], ACT.Gelu,
                                               bias=prm[:, q, 2 * KD + k:2 * KD + k + 1])
                        a.then_inc(s_h, 1)
            pairs(act, body)

        @block.tensor
        def _(pe):
            def turn(b, q):
                pe.wait_ge(s_tok[q], 16)
                for m in range(2):
                    for k in range(KD):
                        mm = pe.transpose(pT[:, k * BR + m * P:k * BR + (m + 1) * P], tok[:, q, m, k * P:(k + 1) * P], c["ident"][:, :])
                mm.then_inc(s_T, 1)

            turn(0, 0)

            def body(i):
                for q in range(2):
                    b = i * 2 + q
                    pe.wait_ge(s_xe, b + 1)
                    pe.wait_ge(s_w[q], i * 48 + 48)
                    for j in range(HJ // 2):
                        for n in range(2):
                            o = (2 * j + n) * P
                            for k in range(KD):
                                mm = pe.matmul(pH[j][:, n * BR:(n + 1) * BR], w1[:, q, k, o:o + P], xe[:, q, k, :],
                                               start=(k == 0), stop=(k == KD - 1))
                        mm.then_inc(s_mm1, 1)
                    pe.wait_ge(s_tok[1 - q], i * 16 + 16 * (1 + q))
                    for m in range(2):
                        for k in range(KD):
                            mm = pe.transpose(pT[:, k * BR + m * P:k * BR + (m + 1) * P], tok[:, 1 - q, m, k * P:(k + 1) * P],
                                              c["ident"][:, :])
                    mm.then_inc(s_T, 1)
                    wait(pe, s_y, b * 2)
                    for j in range(HJ):
                        if j % 2 == 0:
                            pe.wait_ge(s_h, b * (HJ // 2) + j // 2 + 1)
                        for m in range(2):
                            mm = pe.matmul(pY[m][:, 0:D], h[:, j, m * P:(m + 1) * P], w2[:, q, j, :],
                                           start=(j == 0), stop=(j == HJ - 1))
                    mm.then_inc(s_mm2, 1)
            pairs(pe, body)

        @block.gpsimd
        def _(g):
            def body(i):
                for q in range(2):
                    b = i * 2 + q
                    g.wait_ge(s_y, b * 2 + 2)
                    settle(g)
                    g.dma_start(yrows[:, b, :, :], y[:, q, :, :]).then_inc(s_st[q], 16)
            pairs(g, body)
            for q in range(2):
                g.wait_ge(s_st[q], 16 * (NBLK // 2))


def combine(nc, dram, c, moe, sb, sem):
    with ExitStack() as ctx:
        got = sb("got_c", [P, 2, TG, D], F32, ctx)
        now = sb("now_c", [P, 2, TG], I32, ctx)
        s_now, s_sum = sem("c_now"), sem("c_sum")
        s_got = [sem(f"c_got{u}") for u in range(TG)]
        block = ctx.enter_context(nc.Block())

        @block.gpsimd
        def _(q):
            def body(g):
                wait(q, s_sum, g * (2 * TG))
                if not isinstance(g, int):
                    settle(q)
                for k in range(2):
                    nc.gpsimd.tensor_copy(now[:, k, :], moe["pos"][:, k, bass.ds(g * TG, TG)]).then_inc(s_now, 1)
                q.wait_ge(s_now, g * 2 + 2)
                settle(q)
                for u in range(TG):
                    for k in range(2):
                        nc.gpsimd.indirect_dma_start(
                            out=got[:, k, u, :], out_offset=None, in_=dram["y"][:, :],
                            in_offset=bass.IndirectOffsetOnAxis(ap=now[:, k, u:u + 1], axis=0)).then_inc(s_got[u], 16)
            body(0)
            with q.Fori(1, NG) as g:
                body(g)

        @block.vector
        def _(v):
            with v.Fori(0, NG) as g:
                for u in range(TG):
                    t = g * TG + u
                    v.wait_ge(s_got[u], g * 32 + 32)
                    v.scalar_tensor_tensor(out=c["X"][:, t, :], in0=got[:, 0, u, :], scalar=moe["wt"][:, 0, bass.ds(t, 1)],
                                           in1=c["ACC"][:, t, 0:D], op0=ALU.mult, op1=ALU.add).then_inc(s_sum, 1)
                    v.wait_ge(s_sum, t * 2 + 1)
                    v.scalar_tensor_tensor(out=c["X"][:, t, :], in0=got[:, 1, u, :], scalar=moe["wt"][:, 1, bass.ds(t, 1)],
                                           in1=c["X"][:, t, :], op0=ALU.mult, op1=ALU.add).then_inc(s_sum, 1)


def mixture(nc, ins, dram, c, sb, pb, sem):
    with ExitStack() as ctx:
        moe = dict(
            wt=sb("moe_w", [P, 2, NT], F32, ctx), pos=sb("moe_pos", [P, 2, NT], I32, ctx),
            expert=sb("moe_expert", [P, NBLK + 1], I32, ctx), top=sb("moe_top", [P, NT, 2], F32, ctx),
            idx=sb("moe_idx", [P, NT, 2], U32, ctx), prm=sb("moe_prm", [P, NE, PRM], F32, ctx),
        )
        route(nc, ins, dram, c, moe, sb, pb, sem)
        place(nc, c, moe, sb, pb, sem)
        dispatch(nc, dram, c, moe, sb, sem)
        experts(nc, ins, dram, c, moe, sb, pb, sem)
        combine(nc, dram, c, moe, sb, sem)


def convolutions(nc, ins, dram, c, sb, pb, sem):
    with ExitStack() as ctx:
        r = c["ring"]
        w = sb("w_g", [P, LAYERS, KD, D], F32, ctx)
        vec = sb("vec_g", [P, 3, LAYERS, D], F32, ctx)
        z = sb("z_g", [P, TG, D], F32, ctx)
        xin = sb("xin_g", [P, TG, D], F32, ctx)
        xt = sb("xt_g", [P, TG, D], F32, ctx)
        stat = sb("stat_g", [P, TG, 6], F32, ctx)
        mv = sb("mv_g", [P, TG, 2], F32, ctx)
        sd = sb("sd_g", [P, TG], F32, ctx)
        rs = sb("rs_g", [P, TG], F32, ctx)
        s_w = sem("g_w")
        s_z, s_stat, s_mv, s_sd, s_rs, s_zz = sem("g_z"), sem("g_stat"), sem("g_mv"), sem("g_sd"), sem("g_rs"), sem("g_zz")
        s_z2, s_z3, s_xin, s_T, s_xt, s_M, s_h, s_tab = (sem("g_z2"), sem("g_z3"), sem("g_xin"), sem("g_T"),
                                                         sem("g_xt"), sem("g_M"), sem("g_h"), sem("g_tab"))
        bank = [pb(f"bank_g{k}", ctx) for k in range(8)]
        pS, pT, pM = bank[0:OH], bank[4:6], bank[6:8]
        table = dram["table"].rearrange("(t p) d -> p t d", p=P)
        block = ctx.enter_context(nc.Block())

        @block.sync
        def _(sp):
            sp.dma_start(w[:, :, :, :], ins["L1_gnn_W"].rearrange("l (k p) d -> p l k d", p=P)).then_inc(s_w, 16)
            for k, name in enumerate(("L1_gnn_b", "L1_gnn_gamma", "L1_gnn_beta")):
                sp.dma_start(vec[:, k, :, :], ins[name].rearrange("(o l) d -> o l d", o=1).to_broadcast([P, LAYERS, D])).then_inc(s_w, 16)
            with sp.Fori(0, LAYERS) as l:
                with sp.Fori(0, NG) as g:
                    sp.wait_ge(s_h, l * NT + g * TG + TG)
                    sp.dma_start(table[:, bass.ds(g * TG, TG), :], c["ACC"][:, bass.ds(g * TG, TG), 0:D]).then_inc(s_tab, 16)
            sp.wait_ge(s_tab, 16 * NG * LAYERS)

        @block.gpsimd
        def _(q):
            with q.Fori(0, LAYERS) as l:
                q.wait_ge(s_tab, l * (16 * NG) + 16 * NG)
                settle(q)
                steps_pool(nc, c, r, q, l + 1)

        @block.tensor
        def _(pe):
            pe.wait_ge(s_w, 64)
            pe.matmul(pM[0][:, 0:P], c["ident"][:, :], c["ident"][:, :], start=True, stop=True).then_inc(s_M, 1)

            def nodes(l):
                def turn(g, u):
                    t = g * TG + u
                    pe.wait_ge(s_xin, l * NT + t + 1)
                    if u >= 1:
                        pe.wait_ge(s_xt, l * NT + t)
                    for k in range(KD):
                        mm = pe.transpose(pT[0][:, k * P:(k + 1) * P], xin[:, u, k * P:(k + 1) * P], c["ident"][:, :])
                    mm.then_inc(s_T, 1)

                with pe.Fori(0, NG) as g:
                    turn(g, 0)
                    for u in range(TG):
                        if u + 1 < TG:
                            turn(g, u + 1)
                        t = g * TG + u
                        pe.wait_ge(s_xt, l * NT + t + 1)
                        if u >= 2:
                            pe.wait_ge(s_h, l * NT + t - 1)
                        for k in range(KD):
                            mm = pe.matmul(pM[u % 2][:, 0:D], xt[:, u, k * P:(k + 1) * P],
                                           w[:, l, k, :] if isinstance(l, int) else w[:, bass.ds(l, 1), k, :].rearrange("p o d -> p (o d)"),
                                           start=(k == 0), stop=(k == KD - 1))
                        mm.then_inc(s_M, 1)

            nodes(0)
            with pe.Fori(1, LAYERS) as l:
                steps_tensor(nc, c, r, pe, pS, D, l)
                nodes(l)
            steps_tensor(nc, c, r, pe, pS, D, LAYERS)

        @block.scalar
        def _(act):
            def nodes(l):
                with act.Fori(0, NG) as g:
                    act.wait_ge(s_mv, l * NT + g * TG + TG)
                    act.activation(sd[:, :], mv[:, :, 1], ACT.Sqrt, bias=c["eps"][:, 0:1]).then_inc(s_sd, 1)
                    if not isinstance(l, int):
                        for u in range(TG):
                            act.wait_ge(s_z3, (l - 1) * NT + g * TG + u + 1)
                            act.activation(xin[:, u, :], z[:, u, :], ACT.Relu).then_inc(s_xin, 1)
                    for u in range(TG + 1):
                        if u < TG:
                            act.wait_ge(s_T, l * NT + g * TG + u + 1)
                            act.activation(xt[:, u, :], pT[0][:, 0:D], ACT.Copy).then_inc(s_xt, 1)
                        if u > 0:
                            t = g * TG + u - 1
                            act.wait_ge(s_M, l * NT + t + 2)
                            settle(act)
                            act.activation(c["ACC"][:, t, 0:D], pM[(u - 1) % 2][:, 0:D], ACT.Copy,
                                           scale=c["dinv"][:, bass.ds(t, 1)]).then_inc(s_h, 1)

            nodes(0)
            with act.Fori(1, LAYERS) as l:
                nodes(l)
            with act.Fori(0, NG) as g:
                act.wait_ge(s_mv, LAYERS * NT + g * TG + TG)
                act.activation(sd[:, :], mv[:, :, 1], ACT.Sqrt, bias=c["eps"][:, 0:1]).then_inc(s_sd, 1)

        @block.vector
        def _(v):
            v.wait_ge(s_w, 64)

            def moments(n, src):
                for u in range(TG):
                    v.bn_stats(stat[:, u, :], src(u)).then_inc(s_stat, 1)
                v.wait_ge(s_stat, n * TG + TG)
                settle(v)
                for u in range(TG):
                    v.bn_aggr(mv[:, u, :], stat[:, u, :]).then_inc(s_mv, 1)
                v.wait_ge(s_sd, n + 1)
                v.reciprocal(rs[:, :], sd[:, :]).then_inc(s_rs, 1)
                v.wait_ge(s_rs, n + 1)

            def row(k, l):
                return vec[:, k, bass.ds(l, 1), :].rearrange("p o d -> p (o d)")

            def epilogue(l, g):
                n = l * NG + g
                for u in range(TG):
                    t = g * TG + u
                    v.scalar_tensor_tensor(out=z[:, u, :], in0=c["ACC"][:, t, 0:D], scalar=c["dinv"][:, bass.ds(t, 1)],
                                           in1=row(0, l), op0=ALU.mult, op1=ALU.add).then_inc(s_z, 1)
                v.wait_ge(s_z, n * TG + TG)
                moments(n + NG, lambda u: z[:, u, :])
                for u in range(TG):
                    v.scalar_tensor_tensor(out=z[:, u, :], in0=z[:, u, :], scalar=mv[:, u, 0:1], in1=row(1, l),
                                           op0=ALU.subtract, op1=ALU.mult).then_inc(s_z2, 1)
                for u in range(TG):
                    v.wait_ge(s_z2, n * TG + u + 1)
                    v.scalar_tensor_tensor(out=z[:, u, :], in0=z[:, u, :], scalar=rs[:, u:u + 1], in1=row(2, l),
                                           op0=ALU.mult, op1=ALU.add).then_inc(s_z3, 1)

            with v.Fori(0, NG) as g:
                moments(g, lambda u: c["X"][:, g * TG + u, :])
                for u in range(TG):
                    v.wait_ge(s_M, g * TG + 1)
                    v.tensor_scalar(xin[:, u, :], c["X"][:, g * TG + u, :], mv[:, u, 0:1], rs[:, u:u + 1],
                                    ALU.subtract, ALU.mult).then_inc(s_xin, 1)
            with v.Fori(1, LAYERS) as l:
                steps_vector(nc, c, r, v, pS, D, l)
                v.wait_ge(r["s_add"], (l + 1) * STEPS + OH)
                settle(v)
                with v.Fori(0, NG) as g:
                    v.wait_ge(s_xin, l * NT + g * TG)
                    epilogue(l - 1, g)
            steps_vector(nc, c, r, v, pS, D, LAYERS)
            v.wait_ge(r["s_add"], (LAYERS + 1) * STEPS + OH)
            with v.Fori(0, NG) as g:
                epilogue(LAYERS - 1, g)
                v.wait_ge(s_z3, (LAYERS - 1) * NT + g * TG + TG)
                for u in range(TG):
                    t = g * TG + u
                    v.scalar_tensor_tensor(out=c["X"][:, t, :], in0=z[:, u, :], scalar=0.0, in1=c["X"][:, t, :],
                                           op0=ALU.max, op1=ALU.add).then_inc(s_zz, 1)
                v.wait_ge(s_zz, g * TG + TG)


def slices(nc, ins, out, c, sb, pb, sem):
    with ExitStack() as ctx:
        wc = sb("wc", [P, KD, HEADS * GS], F32, ctx)
        bc = sb("bc", [P, HEADS * GS], F32, ctx)
        SWT = sb("SWT", [P, NT, HEADS * GS], F32, ctx)
        mo = sb("mo", [P, PAIRS, D], F32, ctx)
        diag = sb("diag", [P, 4, P], F32, ctx)
        sums = sb("sums", [P, PAIRS, AW], F32, ctx)
        fold_weights(nc, ins, c, wc, bc, diag, sb, pb, sem)
        slice_nodes(nc, c, wc, bc, SWT, sums, sb, pb, sem)
        attend(nc, ins, c, diag, sums, mo, sb, pb, sem)
        project(nc, ins, out, c, SWT, mo, sb, pb, sem)


def fold_weights(nc, ins, c, wc, bc, diag, sb, pb, sem):
    with ExitStack() as ctx:
        wx = sb("wx_f", [P, KD, HEADS * DH], F32, ctx)
        wxt = sb("wxt_f", [P, KD, PAIRS, P], F32, ctx)
        bx = sb("bx_f", [P, PAIRS], F32, ctx)
        bxb = sb("bxb_f", [P, PAIRS, P], F32, ctx)
        bs = sb("bs_f", [P, GS], F32, ctx)
        tp = sb("tp_f", [P, HEADS], F32, ctx)
        rt = sb("rt_f", [P, HEADS], F32, ctx)
        pT = [pb(f"pT_f{k}", ctx) for k in range(KD)]
        pW = [pb(f"pW_f{k}", ctx) for k in range(KD)]
        pB = pb("pB_f", ctx)
        s_zero, s_in, s_xt, s_T, s_mm, s_v = (sem("f_zero"), sem("f_in"), sem("f_xt"), sem("f_T"), sem("f_mm"), sem("f_v"))
        s_mask = sem("f_mask")
        NIN = 2 * 4 + 4
        block = ctx.enter_context(nc.Block())

        @block.sync
        def _(sp):
            sp.wait_ge(s_zero, 1)
            for n, name in enumerate(("L1_ffn_W_slice", "L1_ffn_W_q", "L1_ffn_W_k", "L1_ffn_W_v")):
                for a in range(2):
                    sp.dma_start(diag[a * DH:(a + 1) * DH, n, a * DH:(a + 1) * DH], ins[name]).then_inc(s_in, 16)
            sp.dma_start(wx[:, :, :], ins["L1_ffn_W_x"].rearrange("(k p) n -> p k n", p=P)).then_inc(s_in, 16)
            sp.dma_start(bx[:, :], ins["L1_ffn_b_x"].rearrange("(a p) -> p a", p=P), allow_slow_non_contiguous=True).then_inc(s_in, 16)
            sp.dma_start(bs[:, :], ins["L1_ffn_b_slice"].rearrange("(o g) -> o g", o=1).to_broadcast([P, GS])).then_inc(s_in, 16)
            sp.dma_start(tp[:, :], ins["L1_ffn_temperature"].rearrange("o h a b -> o (h a b)").to_broadcast([P, HEADS])).then_inc(s_in, 16)

        @block.gpsimd
        def _(g):
            nc.gpsimd.affine_select(out=c["X"][:, NT - 1, :], in_=c["X"][:, NT - 1, :], compare_op=ALU.is_ge,
                                    fill=0.0, base=LAST - 1, pattern=[[0, D]], channel_multiplier=-1).then_inc(s_mask, 1)

        @block.vector
        def _(v):
            v.memset(diag[:, :, :], 0.0).then_inc(s_zero, 1)
            v.wait_ge(s_in, 16 * NIN)
            for a in range(PAIRS):
                ins_ = v.tensor_copy(bxb[:, a, :], bx[:, a:a + 1].to_broadcast([P, P]))
            ins_.then_inc(s_v, 1)
            v.tensor_scalar(tp[:, :], tp[:, :], 0.1, 5.0, ALU.max, ALU.min).then_inc(s_v, 1)
            v.wait_ge(s_v, 2)
            v.reciprocal(rt[:, :], tp[:, :]).then_inc(s_v, 1)
            for k in range(KD):
                v.wait_ge(s_T, k + 1)
                v.tensor_copy(wxt[:, k, :, :].rearrange("p a n -> p (a n)"), pT[k][:, :]).then_inc(s_xt, 1)
            v.wait_ge(s_v, 3)
            v.wait_ge(s_mm, KD + 1)
            for h in range(HEADS):
                cols = slice(h * GS, (h + 1) * GS)
                for k in range(KD):
                    v.tensor_scalar(wc[:, k, cols], pW[k][:, cols], rt[:, h:h + 1], None, ALU.mult)
                ins_ = v.tensor_tensor(bc[:, cols], pB[:, cols], bs[:, :], ALU.add)
            ins_.then_inc(s_v, 1)
            v.wait_ge(s_v, 4)
            for h in range(HEADS):
                cols = slice(h * GS, (h + 1) * GS)
                v.tensor_scalar(bc[:, cols], bc[:, cols], rt[:, h:h + 1], None, ALU.mult)

        @block.tensor
        def _(pe):
            pe.wait_ge(s_in, 16 * NIN)
            for k in range(KD):
                for a in range(PAIRS):
                    mm = pe.transpose(pT[k][:, a * P:(a + 1) * P], wx[:, k, a * P:(a + 1) * P], c["ident"][:, :])
                mm.then_inc(s_T, 1)
            for k in range(KD):
                pe.wait_ge(s_xt, k + 1)
                for a in range(PAIRS):
                    mm = pe.matmul(pW[k][:, a * P:(a + 1) * P], wxt[:, k, a, :], diag[:, 0, :], start=True, stop=True)
                mm.then_inc(s_mm, 1)
            pe.wait_ge(s_v, 1)
            for a in range(PAIRS):
                mm = pe.matmul(pB[:, a * P:(a + 1) * P], bxb[:, a, :], diag[:, 0, :], start=True, stop=True)
            mm.then_inc(s_mm, 1)


def slice_nodes(nc, c, wc, bc, SWT, sums, sb, pb, sem):
    SW = HEADS * GS
    RS = 3
    with ExitStack() as ctx:
        un = sb("un_s", [P, TG, AW], F32, ctx)
        ut = sb("ut_s", [P, 2, D], F32, ctx)
        z = sb("z_s", [P, RS, SW], F32, ctx)
        sw = sb("sw_s", [P, RS, SW], F32, ctx)
        red = sb("red_s", [P, RS, 3, HEADS], F32, ctx)
        zero = sb("zero_s", [P, AW], F32, ctx)
        stat = sb("stat_s", [P, TG, 6], F32, ctx)
        mv = sb("mv_s", [P, TG, 2], F32, ctx)
        sd = sb("sd_s", [P, TG], F32, ctx)
        rs = sb("rs_s", [P, TG], F32, ctx)
        s_stat, s_mv, s_sd, s_rs, s_un = sem("s_stat"), sem("s_mv"), sem("s_sd"), sem("s_rs"), sem("s_un")
        s_T, s_ut, s_L, s_z, s_max, s_sub, s_exp = (sem("s_T"), sem("s_ut"), sem("s_L"), sem("s_z"), sem("s_max"),
                                                    sem("s_sub"), sem("s_exp"))
        s_sum, s_inv, s_sw, s_W, s_swt, s_S, s_zero, s_end = (sem("s_sum"), sem("s_inv"), sem("s_sw"), sem("s_W"),
                                                              sem("s_swt"), sem("s_S"), sem("s_zero"), sem("s_end"))
        pT = pb("pT_s", ctx)
        pL = [pb(f"pL_s{k}", ctx) for k in range(2)]
        pW = pb("pW_s", ctx)
        pS = [pb(f"pS_s{k}", ctx) for k in range(PAIRS)]
        block = ctx.enter_context(nc.Block())

        def heads(ap):
            return ap.rearrange("p (h g) -> p h g", h=HEADS)

        @block.vector
        def _(v):
            v.memset(zero[:, :], 0.0).then_inc(s_zero, 1)
            v.memset(z[:, :, :], 0.0).then_inc(s_z, 1)

            def logits(g, u):
                t = g * TG + u
                x = u % RS
                v.wait_ge(s_L, t + 1)
                v.tensor_tensor(z[:, x, :], pL[u % 2][:, :], bc[:, :], ALU.add).then_inc(s_z, 1)
                v.wait_ge(s_z, t + 2)
                v.tensor_reduce(red[:, x, 0, :], heads(z[:, x, :]), AX.X, ALU.max).then_inc(s_max, 1)
                v.wait_ge(s_max, t + 1)
                v.tensor_tensor(heads(z[:, x, :]), heads(z[:, x, :]),
                                red[:, x, 0, :].rearrange("p (h o) -> p h o", o=1).to_broadcast([P, HEADS, GS]),
                                ALU.subtract).then_inc(s_sub, 1)

            def weights(g, u):
                t = g * TG + u
                x = u % RS
                v.wait_ge(s_exp, t + 1)
                v.tensor_reduce(red[:, x, 1, :], heads(z[:, x, :]), AX.X, ALU.add).then_inc(s_sum, 1)
                v.wait_ge(s_sum, t + 1)
                v.reciprocal(red[:, x, 2, :], red[:, x, 1, :]).then_inc(s_inv, 1)
                if u == 0:
                    v.wait_ge(s_S, t + 1)
                if u >= RS:
                    v.wait_ge(s_S, t - RS + 2)
                v.wait_ge(s_inv, t + 1)
                v.tensor_tensor(heads(sw[:, x, :]), heads(z[:, x, :]),
                                red[:, x, 2, :].rearrange("p (h o) -> p h o", o=1).to_broadcast([P, HEADS, GS]),
                                ALU.mult).then_inc(s_sw, 1)

            with v.Fori(0, NG) as g:
                for u in range(TG):
                    v.bn_stats(stat[:, u, :], c["X"][:, g * TG + u, :]).then_inc(s_stat, 1)
                v.wait_ge(s_stat, g * TG + TG)
                settle(v)
                for u in range(TG):
                    v.bn_aggr(mv[:, u, :], stat[:, u, :]).then_inc(s_mv, 1)
                v.wait_ge(s_sd, g + 1)
                v.reciprocal(rs[:, :], sd[:, :]).then_inc(s_rs, 1)
                v.wait_ge(s_rs, g + 1)
                v.wait_ge(s_S, g * TG + 1)
                v.tensor_copy(un[:, :, D:AW].rearrange("p u o -> p (u o)"), c["valid"][:, bass.ds(g * TG, TG)])
                for u in range(TG):
                    v.tensor_scalar(un[:, u, 0:D], c["X"][:, g * TG + u, :], mv[:, u, 0:1], rs[:, u:u + 1],
                                    ALU.subtract, ALU.mult).then_inc(s_un, 1)
                logits(g, 0)
                for u in range(TG):
                    if u + 1 < TG:
                        logits(g, u + 1)
                    weights(g, u)
            v.wait_ge(s_end, 1)
            for a in range(PAIRS):
                v.tensor_copy(sums[:, a, :], pS[a][:, 0:AW])

        @block.scalar
        def _(act):
            with act.Fori(0, NG) as g:
                act.wait_ge(s_mv, g * TG + TG)
                act.activation(sd[:, :], mv[:, :, 1], ACT.Sqrt, bias=c["eps"][:, 0:1]).then_inc(s_sd, 1)
                for k in range(TG + 4):
                    if k < TG:
                        act.wait_ge(s_T, g * TG + k + 1)
                        act.activation(ut[:, k % 2, :], pT[:, 0:D], ACT.Copy).then_inc(s_ut, 1)
                    if 0 <= k - 2 < TG:
                        act.wait_ge(s_sub, g * TG + k - 2 + 1)
                        act.activation(z[:, (k - 2) % RS, :], z[:, (k - 2) % RS, :], ACT.Exp).then_inc(s_exp, 1)
                    if 0 <= k - 4 < TG:
                        t = g * TG + k - 4
                        act.wait_ge(s_W, t + 1)
                        settle(act)
                        act.activation(SWT[:, t, :], pW[:, :], ACT.Copy).then_inc(s_swt, 1)

        @block.tensor
        def _(pe):
            pe.wait_ge(s_zero, 1)
            for a in range(PAIRS):
                mm = pe.matmul(pS[a][:, 0:AW], zero[:, 0:P], zero[:, :], start=True, stop=False, skip_group_check=True)
            mm.then_inc(s_S, 1)
            with pe.Fori(0, NG) as g:
                for k in range(TG + 3):
                    if k < TG:
                        t = g * TG + k
                        pe.wait_ge(s_un, t + 1)
                        if k >= 1:
                            pe.wait_ge(s_ut, t)
                        for n in range(KD):
                            mm = pe.transpose(pT[:, n * P:(n + 1) * P], un[:, k, n * P:(n + 1) * P], c["ident"][:, :])
                        mm.then_inc(s_T, 1)
                    if 0 <= k - 1 < TG:
                        u = k - 1
                        t = g * TG + u
                        pe.wait_ge(s_ut, t + 1)
                        if u == 0:
                            pe.wait_ge(s_z, t + 1)
                        if u >= 2:
                            pe.wait_ge(s_z, t)
                        for n in range(KD):
                            mm = pe.matmul(pL[u % 2][:, :], ut[:, u % 2, n * P:(n + 1) * P], wc[:, n, :],
                                           start=(n == 0), stop=(n == KD - 1))
                        mm.then_inc(s_L, 1)
                    if 0 <= k - 3 < TG:
                        u = k - 3
                        t = g * TG + u
                        pe.wait_ge(s_sw, t + 1)
                        if u >= 1:
                            pe.wait_ge(s_swt, t)
                        for a in range(PAIRS):
                            mm = pe.transpose(pW[:, a * P:(a + 1) * P], sw[:, u % RS, a * P:(a + 1) * P], c["ident"][:, :])
                        mm.then_inc(s_W, 1)
                        for a in range(PAIRS):
                            mm = pe.matmul(pS[a][:, 0:AW], sw[:, u % RS, a * P:(a + 1) * P], un[:, u, :],
                                           start=False, stop=False, skip_group_check=True)
                        mm.then_inc(s_S, 1)
            for a in range(PAIRS):
                mm = pe.matmul(pS[a][:, 0:AW], zero[:, 0:P], zero[:, :], start=False, stop=True, skip_group_check=True)
            mm.then_inc(s_end, 1)


def attend(nc, ins, c, diag, sums, mo, sb, pb, sem):
    with ExitStack() as ctx:
        wfx = sb("wfx_t", [P, KD, HEADS * DH], F32, ctx)
        bfx = sb("bfx_t", [P, HEADS * DH], F32, ctx)
        wo = sb("wo_t", [P, PAIRS, D], F32, ctx)
        st = sb("st_t", [P, KD, PAIRS, P], F32, ctx)
        inv = sb("inv_t", [P, 2, PAIRS], F32, ctx)
        tok = sb("tok_t", [P, PAIRS, P], F32, ctx)
        tokT = sb("tokT_t", [P, PAIRS, P], F32, ctx)
        qT = sb("qT_t", [P, PAIRS, P], F32, ctx)
        kT = sb("kT_t", [P, PAIRS, P], F32, ctx)
        vv = sb("vv_t", [P, PAIRS, P], F32, ctx)
        sc = sb("sc_t", [P, PAIRS, DH], F32, ctx)
        red = sb("red_t", [P, 3, PAIRS], F32, ctx)
        at = sb("at_t", [P, PAIRS, P], F32, ctx)
        atT = sb("atT_t", [P, PAIRS, P], F32, ctx)
        oT = sb("oT_t", [P, PAIRS, P], F32, ctx)
        bank = [pb(f"bank_t{k}", ctx) for k in range(8)]
        s_in, s_pe, s_v, s_exp = sem("t_in"), sem("t_pe"), sem("t_v"), sem("t_exp")
        block = ctx.enter_context(nc.Block())
        HALVES = [slice(0, DH), slice(DH, 2 * DH)]

        def flat(x):
            return x[:, :, :].rearrange("p a n -> p (a n)")

        @block.sync
        def _(sp):
            sp.dma_start(wfx[:, :, :], ins["L1_ffn_W_fx"].rearrange("(k p) n -> p k n", p=P)).then_inc(s_in, 16)
            sp.dma_start(bfx[:, :], ins["L1_ffn_b_fx"].rearrange("(o n) -> o n", o=1).to_broadcast([P, HEADS * DH])).then_inc(s_in, 16)
            sp.dma_start(wo[:, :, :], ins["L1_ffn_W_out"].rearrange("(a p) d -> p a d", p=P)).then_inc(s_in, 16)

        @block.tensor
        def _(pe):
            def done(n, fn):
                pe.wait_ge(s_v, n)
                for a in range(PAIRS):
                    mm = fn(a)
                mm.then_inc(s_pe, 1)

            pe.wait_ge(s_in, 48)
            cols = [slice(a * P, (a + 1) * P) for a in range(PAIRS)]
            for k in range(KD):
                for a in range(PAIRS):
                    mm = pe.transpose(bank[k][:, cols[a]], sums[:, a, k * P:(k + 1) * P], c["ident"][:, :])
            mm.then_inc(s_pe, 1)

            def tokens(a):
                for k in range(KD):
                    mm = pe.matmul(bank[2][:, cols[a]], st[:, k, a, :], wfx[:, k, cols[a]], start=(k == 0), stop=(k == KD - 1))
                return mm
            done(1, tokens)
            done(2, lambda a: pe.transpose(bank[3][:, cols[a]], tok[:, a, :], c["ident"][:, :]))

            def qkv(a):
                pe.matmul(bank[4][:, cols[a]], diag[:, 1, :], tokT[:, a, :], start=True, stop=True)
                pe.matmul(bank[5][:, cols[a]], diag[:, 2, :], tokT[:, a, :], start=True, stop=True)
                return pe.matmul(bank[6][:, cols[a]], tokT[:, a, :], diag[:, 3, :], start=True, stop=True)
            done(3, qkv)
            done(4, lambda a: pe.matmul(bank[7][:, cols[a]], qT[:, a, :], kT[:, a, :], start=True, stop=True))
            done(5, lambda a: pe.transpose(bank[0][:, cols[a]], at[:, a, :], c["ident"][:, :]))
            done(6, lambda a: pe.matmul(bank[1][:, cols[a]], vv[:, a, :], atT[:, a, :], start=True, stop=True))
            done(7, lambda a: pe.matmul(bank[2 + a // 2][:, (a % 2) * D:(a % 2 + 1) * D], oT[:, a, :], wo[:, a, :], start=True, stop=True))

        @block.scalar
        def _(act):
            act.wait_ge(s_exp, 1)
            act.activation(sc[:, :, :], sc[:, :, :], ACT.Exp).then_inc(s_exp, 1)

        @block.vector
        def _(v):
            s_c = sem("t_chain")
            n = [0]

            def then(i):
                i.then_inc(s_c, 1)
                n[0] += 1
                v.wait_ge(s_c, n[0])

            v.memset(tok[:, :, :], 0.0)
            v.memset(at[:, :, :], 0.0)
            v.tensor_scalar(inv[:, 0, :], sums[:, :, D], 1e-5, None, ALU.add)
            v.wait_ge(s_in, 48)
            v.wait_ge(s_pe, 1)
            v.tensor_copy(st[:, 0, :, :].rearrange("p a n -> p (a n)"), bank[0][:, :])
            then(v.tensor_copy(st[:, 1, :, :].rearrange("p a n -> p (a n)"), bank[1][:, :]))
            then(v.reciprocal(inv[:, 1, :], inv[:, 0, :]))
            v.memset(red[:, :, :], 0.0).then_inc(s_v, 1)
            v.wait_ge(s_pe, 2)
            for a in range(PAIRS):
                for x in range(2):
                    hs = slice(a * P + x * DH, a * P + (x + 1) * DH)
                    i = v.scalar_tensor_tensor(out=tok[HALVES[x], a, HALVES[x]], in0=bfx[HALVES[x], hs], scalar=sums[HALVES[x], a, D:AW],
                                               in1=bank[2][HALVES[x], hs], op0=ALU.mult, op1=ALU.add)
            then(i)
            for a in range(PAIRS):
                i = v.tensor_scalar(tok[:, a, :], tok[:, a, :], inv[:, 1, a:a + 1], None, ALU.mult)
            i.then_inc(s_v, 1)
            v.wait_ge(s_pe, 3)
            v.tensor_copy(flat(tokT), bank[3][:, :]).then_inc(s_v, 1)
            v.wait_ge(s_pe, 4)
            v.tensor_copy(flat(qT), bank[4][:, :])
            v.tensor_copy(flat(kT), bank[5][:, :])
            v.tensor_copy(flat(vv), bank[6][:, :]).then_inc(s_v, 1)
            v.wait_ge(s_pe, 5)
            for a in range(PAIRS):
                for x in range(2):
                    i = v.tensor_scalar(sc[HALVES[x], a, :], bank[7][HALVES[x], a * P + x * DH:a * P + (x + 1) * DH],
                                        float(DH) ** -0.5, None, ALU.mult)
            then(i)
            then(v.tensor_reduce(red[:, 0, :], sc[:, :, :], AX.X, ALU.max))

            def wide(k):
                return red[:, k, :].rearrange("p (a o) -> p a o", o=1).to_broadcast([P, PAIRS, DH])
            v.tensor_tensor(sc[:, :, :], sc[:, :, :], wide(0), ALU.subtract).then_inc(s_exp, 1)
            v.wait_ge(s_exp, 2)
            then(v.tensor_reduce(red[:, 1, :], sc[:, :, :], AX.X, ALU.add))
            then(v.reciprocal(red[:, 2, :], red[:, 1, :]))
            for x in range(2):
                i = v.tensor_tensor(at[HALVES[x], :, HALVES[x]], sc[HALVES[x], :, :],
                                    red[HALVES[x], 2, :].rearrange("p (a o) -> p a o", o=1).to_broadcast([DH, PAIRS, DH]), ALU.mult)
            i.then_inc(s_v, 1)
            v.wait_ge(s_pe, 6)
            v.tensor_copy(flat(atT), bank[0][:, :]).then_inc(s_v, 1)
            v.wait_ge(s_pe, 7)
            v.tensor_copy(flat(oT), bank[1][:, :]).then_inc(s_v, 1)
            v.wait_ge(s_pe, 8)
            for a in range(PAIRS):
                v.tensor_copy(mo[:, a, :], bank[2 + a // 2][:, (a % 2) * D:(a % 2 + 1) * D])


def project(nc, ins, out, c, SWT, mo, sb, pb, sem):
    with ExitStack() as ctx:
        bo = sb("bo_o", [P, D], F32, ctx)
        wt = sb("wt_o", [P, TG, HEADS * GS], F32, ctx)
        pO = [pb(f"pO_o{k}", ctx) for k in range(TG)]
        s_in, s_wt, s_b, s_mm, s_x, s_out = sem("o_in"), sem("o_wt"), sem("o_b"), sem("o_mm"), sem("o_x"), sem("o_out")
        block = ctx.enter_context(nc.Block())

        @block.sync
        def _(sp):
            sp.dma_start(bo[:, :], ins["L1_ffn_b_out"].rearrange("(o d) -> o d", o=1).to_broadcast([P, D])).then_inc(s_in, 16)
            rows = out[0:(NT - 1) * P, :].rearrange("(t p) d -> p t d", p=P)
            with sp.Fori(0, NG - 1) as g:
                sp.wait_ge(s_x, g * TG + TG)
                sp.dma_start(rows[:, bass.ds(g * TG, TG), :], c["X"][:, bass.ds(g * TG, TG), :]).then_inc(s_out, 16)
            sp.wait_ge(s_x, NT)
            sp.dma_start(rows[:, (NG - 1) * TG:NT - 1, :], c["X"][:, (NG - 1) * TG:NT - 1, :]).then_inc(s_out, 16)
            sp.dma_start(out[(NT - 1) * P:N, :], c["X"][0:LAST, NT - 1, :]).then_inc(s_out, 16)
            sp.wait_ge(s_out, 16 * (NG + 1))

        @block.scalar
        def _(act):
            def body(g):
                for u in range(TG):
                    wait(act, s_mm, (g - 1) * TG + u + 1)
                    if not isinstance(g, int):
                        settle(act)
                    act.activation(wt[:, u, :], SWT[:, g * TG + u, :], ACT.Copy).then_inc(s_wt, 1)
            body(0)
            with act.Fori(1, NG) as g:
                body(g)

        @block.tensor
        def _(pe):
            def body(g):
                for u in range(TG):
                    t = g * TG + u
                    pe.wait_ge(s_wt, t + 1)
                    wait(pe, s_x, t - TG + 1)
                    for a in range(PAIRS):
                        mm = pe.matmul(pO[u][:, 0:D], wt[:, u, a * P:(a + 1) * P], mo[:, a, :], start=(a == 0), stop=(a == PAIRS - 1))
                    mm.then_inc(s_mm, 1)
            body(0)
            with pe.Fori(1, NG) as g:
                body(g)

        @block.vector
        def _(v):
            v.wait_ge(s_in, 16)
            with v.Fori(0, NG) as g:
                for u in range(TG):
                    t = g * TG + u
                    v.tensor_tensor(c["X"][:, t, :], c["X"][:, t, :], bo[:, :], ALU.add).then_inc(s_b, 1)
                for u in range(TG):
                    t = g * TG + u
                    v.wait_ge(s_b, t + 1)
                    v.wait_ge(s_mm, t + 1)
                    v.tensor_tensor(c["X"][:, t, :], pO[u][:, 0:D], c["X"][:, t, :], ALU.add).then_inc(s_x, 1)


_INS = ['x', 'src', 'dst', 'edge_weight', 'L0_gnn_w_nbr', 'L0_gnn_w_own', 'L0_gnn_bias',
        'L0_ffn_Wr', 'L0_ffn_br', 'L0_ffn_ln_g', 'L0_ffn_ln_b', 'L0_ffn_W1', 'L0_ffn_b1', 'L0_ffn_W2', 'L0_ffn_b2',
        'L1_gnn_W', 'L1_gnn_b', 'L1_gnn_gamma', 'L1_gnn_beta', 'L1_ffn_W_fx', 'L1_ffn_b_fx', 'L1_ffn_W_x',
        'L1_ffn_b_x', 'L1_ffn_W_slice', 'L1_ffn_b_slice', 'L1_ffn_W_q', 'L1_ffn_W_k', 'L1_ffn_W_v', 'L1_ffn_W_out',
        'L1_ffn_b_out', 'L1_ffn_temperature']


def kernel(**inputs):
    import numpy as _np
    import concourse.bacc as _bacc
    from concourse import mybir as _mybir
    from concourse.bass_utils import run_bass_kernel_spmd as _run

    nc = _bacc.Bacc("TRN2", target_bir_lowering=False, num_devices=1)
    arrays, ins = {}, {}
    for name in _INS:
        a = _np.ascontiguousarray(inputs[name])
        arrays[f"in_{name}"] = a
        ins[name] = nc.dram_tensor(f"in_{name}", a.shape, _mybir.dt.from_np(a.dtype), kind="ExternalInput").ap()
    out = nc.dram_tensor("out_0", (N, D), _mybir.dt.float32, kind="ExternalOutput").ap()
    dram = {name: nc.dram_tensor(name, (rows, D), _mybir.dt.float32, kind="Internal").ap()
            for name, rows in (("table", NT * P), ("disp", SLOTS + BR), ("y", SLOTS + BR))}
    build(nc, ins, out, dram)
    r = _run(nc, [arrays], core_ids=[0])
    return r.results[0]["out_0"]
```

```python
from contextlib import ExitStack

import concourse.bass as bass
from concourse import mybir

P = 128
F32 = mybir.dt.float32
I32 = mybir.dt.int32
U32 = mybir.dt.uint32
ALU = mybir.AluOpType
ACT = mybir.ActivationFunctionType
AX = mybir.AxisListType
EPS = 1e-5

N = 6250
D = 256
KD = D // P
NT = -(-N // P)
LAST = N - (NT - 1) * P
TG = 7
NG = NT // TG
E = 100000
ET = -(-E // P)
EC = -(-ET // P)
EF = -(-E // P)
EB = 17
U = 32
NB = -(-(ET + NT - 1) // U)
STEPS = NB * U
HALF = STEPS // 2
R = 16
OH = 4
AHEAD = OH - 1
Q = 4
LOADS = 8
AW = D + 1
FAR = 1 << 27
NE = 8
HID = 1024
HJ = HID // P
BR = 2 * P
NBLK = (2 * N + NE * (BR - 1)) // BR
NBLK += NBLK % 2
SLOTS = NBLK * BR
LAYERS = 3
TPB = 2
LAG = 3
BATCHES = NB - LAG + 1
TAIL = NT - (NB - LAG) * TPB
HEADS = 8
DH = 64
GS = 64
PAIRS = HEADS // 2
PRM = KD + KD + HJ


def build(nc, ins, out, dram):
    with ExitStack() as top:
        def sb(name, shape, dt=F32, ctx=top):
            return ctx.enter_context(nc.sbuf_tensor(name, shape, dt))

        def pb(name, ctx, shape=(P, 512), dt=F32):
            return ctx.enter_context(nc.psum_tensor(name, list(shape), dt))

        def sem(name):
            return top.enter_context(nc.semaphore(name))

        c = dict(ident=sb("ident", [P, P]), eps=sb("eps", [P, 1]), valid=sb("valid", [P, NT]), X=sb("X", [P, NT, D]))
        with ExitStack() as g:
            c.update(
                lane=sb("lane", [P, P], F32, g), ACC=sb("ACC", [P, NT, AW], F32, g),
                ones_row=sb("ones_row", [P, NT], F32, g),
                step_src=sb("step_src", [P, STEPS + R], I32, g), step_dst=sb("step_dst", [P, STEPS + AHEAD], F32, g),
                step_w=sb("step_w", [P, STEPS], F32, g), step_off=sb("step_off", [P, STEPS], I32, g),
                dinv=sb("dinv", [P, NT], F32, g), late=sb("late", [P, 1], I32, g),
            )
            c["ring"] = gather_ring(nc, dram["table"], sb, sem, g)
            order_edges(nc, ins, dram, c, sb, pb, sem)
            prepare(nc, ins, dram, c, sb, pb, sem)
            first_layer(nc, ins, dram, c, sb, pb, sem)
            moe = dict(
                wt=sb("moe_w", [P, 2, NT], F32, g), pos=sb("moe_pos", [P, 2, NT], I32, g),
                expert=sb("moe_expert", [P, NBLK + 1], I32, g), top=sb("moe_top", [P, NT, 2], F32, g),
                idx=sb("moe_idx", [P, NT, 2], U32, g), prm=sb("moe_prm", [P, NE, PRM], F32, g),
            )
            mixture(nc, ins, dram, c, moe, sb, pb, sem)
            convolutions(nc, ins, dram, c, moe, sb, pb, sem)
        slices(nc, ins, out, c, sb, pb, sem)


def order_edges(nc, ins, dram, c, sb, pb, sem):
    full = P - 1
    rest = E - full * EF
    with ExitStack() as ctx:
        dst_i = sb("dst_o", [P, EF + 1], I32, ctx)
        dst_f = sb("dstf_o", [P, EF + 1], F32, ctx)
        falls = sb("falls", [P, EF], F32, ctx)
        nfalls = sb("nfalls", [P, 1], F32, ctx)
        ones = sb("ones_o", [P, P], F32, ctx)
        flag_i = sb("flag_i", [P, 1], I32, ctx)
        BK = NT + 1
        t = dict(
            src_i=sb("src_o", [P, EF], I32, ctx),
            w_f=sb("w_o", [P, EF], F32, ctx),
            rec=sb("rec_o", [P, EF, 4], F32, ctx),
            bkt_i=sb("bkti_o", [P, EF], I32, ctx),
            bkt=sb("bkt_o", [P, EF], F32, ctx),
            mask=sb("mask_o", [P, EF], F32, ctx),
            run=sb("run_o", [P, EF], F32, ctx),
            one=sb("one_o", [P, EF], F32, ctx),
            pos_f=sb("posf_o", [P, EF], F32, ctx),
            pos_i=sb("posi_o", [P, EF], I32, ctx),
            number=sb("number_o", [P, BK], F32, ctx),
            cnt=sb("cnt_o", [P, BK], F32, ctx),
            tot=sb("tot_o", [P, BK], F32, ctx),
            off=sb("off_o", [P, BK], F32, ctx),
            before=sb("before_o", [P, P], F32, ctx),
            now=sb("now_o", [P, EB], I32, ctx),
            stage=sb("stage_o", [P, EB, 4], F32, ctx),
            pW=pb("pW_o", ctx), pC=pb("pC_o", ctx), dst_i=dst_i, ones=ones,
        )
        s_in, s_v, s_mm = sem("y_in"), sem("y_v"), sem("y_mm")

        def rows(a, t):
            return [(t[0:full, 0:EF], a[0:full * EF].rearrange("(p n) -> p n", p=full)),
                    (t[full:P, 0:rest], a[full * EF:E].rearrange("(p n) -> p n", p=1))]

        with ExitStack() as pc, nc.Block() as block:
            pN = pb("pN_o", pc)

            @block.sync
            def _(sp):
                sp.wait_ge(s_v, 1)
                for t, a in rows(ins["dst"], dst_i):
                    sp.dma_start(t, a).then_inc(s_in, 16)
                sp.dma_start(dst_i[0:full - 1, EF:EF + 1], ins["dst"][EF:full * EF].rearrange("(p n) -> p n", n=EF)[:, 0:1],
                             allow_slow_non_contiguous=True).then_inc(s_in, 16)
                sp.dma_start(dst_i[full - 1:full, EF:EF + 1], ins["dst"][full * EF:full * EF + 1].rearrange("(p n) -> p n", n=1)).then_inc(s_in, 16)

            @block.vector
            def _(v):
                v.memset(dst_i[:, :], NT * P).then_inc(s_v, 1)
                v.memset(ones[:, :], 1.0).then_inc(s_v, 1)
                v.wait_ge(s_in, 64)
                v.tensor_copy(dst_f[:, :], dst_i[:, :]).then_inc(s_v, 1)
                v.wait_ge(s_v, 3)
                v.tensor_tensor(falls[:, :], dst_f[:, 0:EF], dst_f[:, 1:EF + 1], ALU.is_gt).then_inc(s_v, 1)
                v.wait_ge(s_v, 4)
                v.tensor_reduce(nfalls[:, :], falls[:, :], AX.X, ALU.add).then_inc(s_v, 1)
                v.wait_ge(s_mm, 1)
                v.tensor_scalar(flag_i[:, :], pN[:, 0:1], 1.0, None, ALU.min)

            @block.tensor
            def _(pe):
                pe.wait_ge(s_v, 5)
                pe.matmul(pN[:, 0:1], ones[:, :], nfalls[:, :], start=True, stop=True).then_inc(s_mm, 1)

        unsorted = nc.values_load(flag_i[0:1, 0:1], min_val=0, max_val=1,
                                  skip_runtime_bounds_check_because="it is the minimum of 1 and a count")
        with nc.If(unsorted > 0):
            sort_edges(nc, ins, dram, t, rows, sem)
        with nc.Else():
            s_copy = sem("y_copy")
            with nc.Block() as block:
                def copy(eng, name, a):
                    eng.dma_start(dram[name].rearrange("(p n) -> p n", p=80), a.rearrange("(p n) -> p n", p=80)).then_inc(s_copy, 16)

                @block.sync
                def _(sp):
                    copy(sp, "dst", ins["dst"])
                    copy(sp, "src", ins["src"])
                    sp.wait_ge(s_copy, 48)

                @block.scalar
                def _(act):
                    copy(act, "weight", ins["edge_weight"])
                    act.wait_ge(s_copy, 48)


def sort_edges(nc, ins, dram, t, rows, sem):
    BK = NT + 1
    G = EF // EB
    src_i, w_f, rec, bkt_i, bkt, mask, run, one, pos_f = (t[k] for k in (
        "src_i", "w_f", "rec", "bkt_i", "bkt", "mask", "run", "one", "pos_f"))
    pos_i, number, cnt, tot, off, before, now, stage, pW, pC, dst_i, ones = (t[k] for k in (
        "pos_i", "number", "cnt", "tot", "off", "before", "now", "stage", "pW", "pC", "dst_i", "ones"))
    s_c, s_dma, s_v, s_b, s_d = sem("z_c"), sem("z_dma"), sem("z_v"), sem("z_b"), sem("z_d")
    s_cnt, s_mm, s_now, s_put = sem("z_cnt"), sem("z_mm"), sem("z_now"), sem("z_put")
    RECORDS = 9
    with nc.Block() as block:
        @block.sync
        def _(sp):
            sp.wait_ge(s_v, 2)
            for t, a in rows(ins["src"], src_i):
                sp.dma_start(t, a).then_inc(s_dma, 16)

        @block.scalar
        def _(act):
            act.wait_ge(s_v, 2)
            for t, a in rows(ins["edge_weight"], w_f):
                act.dma_start(t, a).then_inc(s_dma, 16)

        @block.gpsimd
        def _(g):
            nc.gpsimd.iota(number[:, :], [[1, BK]], base=0, channel_multiplier=0,
                           allow_small_or_imprecise_dtypes=True).then_inc(s_c, 1)
            nc.gpsimd.affine_select(out=before[:, :], in_=ones[:, :], compare_op=ALU.is_gt, fill=0.0,
                                    base=0, pattern=[[1, P]], channel_multiplier=-1).then_inc(s_c, 1)
            g.wait_ge(s_v, RECORDS)
            with g.Fori(0, G) as i:
                nc.gpsimd.tensor_copy(now[:, :], pos_i[:, bass.ds(i * EB, EB)]).then_inc(s_now, 1)
                nc.gpsimd.tensor_copy(stage[:, :, :], rec[:, bass.ds(i * EB, EB), :]).then_inc(s_now, 1)
                g.wait_ge(s_now, i * 2 + 2)
                settle(g)
                for u in range(EB):
                    nc.gpsimd.indirect_dma_start(
                        out=dram["rec"][:, :], out_offset=bass.IndirectOffsetOnAxis(ap=now[:, u:u + 1], axis=0),
                        in_=stage[:, u, :], in_offset=None).then_inc(s_put, 16)
                g.wait_ge(s_put, i * (16 * EB) + 16 * EB)
                settle(g)

        @block.tensor
        def _(pe):
            pe.wait_ge(s_c, 2)
            pe.wait_ge(s_cnt, 2 * BK)
            pe.matmul(pW[:, 0:BK], before[:, :], cnt[:, :], start=True, stop=True).then_inc(s_mm, 1)
            pe.matmul(pC[:, 0:BK], ones[:, :], cnt[:, :], start=True, stop=True).then_inc(s_mm, 1)

        @block.vector
        def _(v):
            n = [0]

            def then(i):
                i.then_inc(s_v, 1)
                n[0] += 1
                v.wait_ge(s_v, n[0])

            then(v.memset(src_i[:, :], 0))
            then(v.memset(w_f[:, :], 0.0))
            v.memset(one[:, :], 1.0)
            v.memset(pos_f[:, :], -1.0)
            v.memset(rec[:, :, 3], 0.0)
            then(v.tensor_scalar(bkt_i[:, :], dst_i[:, 0:EF], 7, None, ALU.arith_shift_right))
            then(v.tensor_copy(bkt[:, :], bkt_i[:, :]))
            v.wait_ge(s_c, 2)
            with v.Fori(0, BK) as b:
                v.tensor_scalar(mask[:, :], bkt[:, :], number[:, bass.ds(b, 1)], None, ALU.is_equal).then_inc(s_cnt, 1)
                v.wait_ge(s_cnt, b * 2 + 1)
                v.tensor_reduce(cnt[:, bass.ds(b, 1)], mask[:, :], AX.X, ALU.add).then_inc(s_cnt, 1)
                v.wait_ge(s_cnt, b * 2 + 2)
                settle(v)
            v.wait_ge(s_mm, 2)
            then(v.tensor_copy(tot[:, :], pC[:, 0:BK]))
            then(v.tensor_tensor_scan(out=off[:, :], data0=one[:, 0:BK], data1=tot[:, :], initial=0.0,
                                      op0=ALU.mult, op1=ALU.add))
            then(v.tensor_tensor(off[:, :], off[:, :], tot[:, :], ALU.subtract))
            then(v.tensor_tensor(off[:, :], off[:, :], pW[:, 0:BK], ALU.add))
            with v.Fori(0, BK) as b:
                v.tensor_scalar(mask[:, :], bkt[:, :], number[:, bass.ds(b, 1)], None, ALU.is_equal).then_inc(s_b, 1)
                v.wait_ge(s_b, b * 4 + 1)
                v.tensor_tensor_scan(out=run[:, :], data0=one[:, :], data1=mask[:, :], initial=off[:, bass.ds(b, 1)],
                                     op0=ALU.mult, op1=ALU.add).then_inc(s_b, 1)
                v.wait_ge(s_b, b * 4 + 2)
                v.tensor_tensor(run[:, :], run[:, :], mask[:, :], ALU.mult).then_inc(s_b, 1)
                v.wait_ge(s_b, b * 4 + 3)
                v.tensor_tensor(pos_f[:, :], pos_f[:, :], run[:, :], ALU.add).then_inc(s_b, 1)
                v.wait_ge(s_b, b * 4 + 4)
                settle(v)
            v.wait_ge(s_dma, 64)
            v.tensor_copy(pos_i[:, :], pos_f[:, :])
            v.tensor_copy(rec[:, :, 0], src_i[:, :])
            v.tensor_copy(rec[:, :, 1], dst_i[:, 0:EF])
            then(v.tensor_copy(rec[:, :, 2], w_f[:, :]))
            assert n[0] == RECORDS

    with nc.Block() as block:
        @block.sync
        def _(sp):
            got = dram["rec"].rearrange("n c -> (n c)")
            sp.dma_start(rec[0:P - 1, :, :].rearrange("p n c -> p (n c)"),
                         got[0:(P - 1) * EF * 4].rearrange("(p n) -> p n", p=P - 1)).then_inc(s_dma, 16)
            rest = E - (P - 1) * EF
            sp.dma_start(rec[P - 1:P, 0:rest, :].rearrange("p n c -> p (n c)"),
                         got[(P - 1) * EF * 4:E * 4].rearrange("(p n) -> p n", p=1)).then_inc(s_dma, 16)
            sp.wait_ge(s_d, 3)
            for name, t in (("src", src_i), ("dst", bkt_i), ("weight", w_f)):
                for on_chip, a in rows(dram[name], t):
                    sp.dma_start(a, on_chip).then_inc(s_dma, 16)
            sp.wait_ge(s_dma, 64 + 32 + 96)

        @block.vector
        def _(v):
            v.wait_ge(s_dma, 64 + 32)
            v.tensor_copy(src_i[:, :], rec[:, :, 0]).then_inc(s_d, 1)
            v.tensor_copy(bkt_i[:, :], rec[:, :, 1]).then_inc(s_d, 1)
            v.tensor_copy(w_f[:, :], rec[:, :, 2]).then_inc(s_d, 1)


def prepare(nc, ins, dram, c, sb, pb, sem):
    full = (EC - 1) * P * P
    rows = (E - full) // P
    rest = E - full - rows * P
    with ExitStack() as ctx:
        src_i = sb("src_i", [P, EC, P], I32, ctx)
        dst_i = sb("dst_i", [P, EC, P], I32, ctx)
        w_f = sb("w_f", [P, EC, P], F32, ctx)
        src_f = sb("src_f", [P, EC, P], F32, ctx)
        dst_f = sb("dst_f", [P, EC, P], F32, ctx)
        tile_f = sb("tile_f", [P, EC, P], F32, ctx)
        ends_i = sb("ends_i", [P, 2, EC], I32, ctx)
        ends_b = sb("ends_b", [P, 2, EC], I32, ctx)
        ends_f = sb("ends_f", [P, 2, EC], F32, ctx)
        start_f = sb("start_f", [P, 2, EC], F32, ctx)
        step_i = sb("step_i", [P, STEPS], F32, ctx)
        sel = sb("sel", [P, EC, STEPS], F32, ctx)
        ge = sb("ge", [P, 2, STEPS], F32, ctx)
        tmp = sb("tmp", [P, STEPS], F32, ctx)
        tmp2 = sb("tmp2", [P, STEPS], F32, ctx)
        need = sb("need", [P, NB - LAG], F32, ctx)
        seen = sb("seen", [P, NB - LAG], F32, ctx)
        nlate = sb("nlate", [P, 1], F32, ctx)
        ps = [pb(f"pp{k}", ctx) for k in range(8)]
        s_clear = sem("p_clear")
        s_const = sem("p_const")
        s_x = sem("p_x")
        s_edges = sem("p_edges")
        s_ends = sem("p_ends")
        s_cast = sem("p_cast")
        s_start = sem("p_start")
        s_ge = sem("p_ge")
        s_sel = sem("p_sel")
        s_mm = sem("p_mm")
        s_out = sem("p_out")

        def by_tile(a, t):
            return [(t[:, 0:EC - 1, :], a[0:full].rearrange("(c p e) -> p c e", p=P, e=P)),
                    (t[0:rows, EC - 1, :], a[full:full + rows * P].rearrange("(p e) -> p e", e=P)),
                    (t[rows:rows + 1, EC - 1, 0:rest], a[full + rows * P:E].rearrange("(p e) -> p e", p=1))]

        def heads(a, t, shift):
            o = shift * P
            r = rows - shift
            out = [(t[:, shift, 0:EC - 1], a[o:o + full].rearrange("(c p e) -> p c e", p=P, e=P)[:, :, 0]),
                   (t[0:r, shift, EC - 1:EC], a[o + full:o + full + r * P].rearrange("(p e) -> p e", e=P)[:, 0:1]),
                   (t[r:r + 1, shift, EC - 1:EC], a[full + rows * P:full + rows * P + 1].rearrange("(p e) -> p e", p=1))]
            return out

        block = ctx.enter_context(nc.Block())

        @block.sync
        def _(sp):
            sp.wait_ge(s_clear, 5)
            for t, a in (*by_tile(dram["dst"], dst_i), *by_tile(dram["src"], src_i),
                         *by_tile(dram["weight"], w_f)):
                sp.dma_start(t, a).then_inc(s_edges, 16)
            for t, a in (*heads(dram["dst"], ends_i, 0), *heads(dram["dst"], ends_i, 1)):
                sp.dma_start(t, a, allow_slow_non_contiguous=True).then_inc(s_ends, 16)

        @block.scalar
        def _(act):
            act.wait_ge(s_clear, 5)
            x = ins["x"]
            act.dma_start(c["X"][:, 0:NT - 1, :], x[0:(NT - 1) * P, :].rearrange("(t p) d -> p t d", p=P)).then_inc(s_x, 16)
            act.dma_start(c["X"][0:LAST, NT - 1, :], x[(NT - 1) * P:N, :]).then_inc(s_x, 16)
            act.wait_ge(s_x, 32)

        @block.gpsimd
        def _(g):
            nc.gpsimd.iota(step_i[:, :], [[1, STEPS]], base=0, channel_multiplier=0,
                           allow_small_or_imprecise_dtypes=True).then_inc(s_const, 1)
            nc.gpsimd.iota(tile_f[:, :, :], [[P, EC], [0, P]], base=0, channel_multiplier=1,
                           allow_small_or_imprecise_dtypes=True).then_inc(s_const, 1)
            nc.gpsimd.iota(c["lane"][:, :], [[1, P]], base=0, channel_multiplier=0,
                           allow_small_or_imprecise_dtypes=True).then_inc(s_const, 1)
            nc.gpsimd.memset(c["ident"][:, :], 0.0).then_inc(s_const, 1)
            nc.gpsimd.iota(need[:, :], [[AW * TPB, NB - LAG]], base=AW * TPB, channel_multiplier=0,
                           allow_small_or_imprecise_dtypes=True).then_inc(s_const, 1)
            g.wait_ge(s_const, 5)
            nc.gpsimd.affine_select(out=c["ident"][:, :], in_=c["ident"][:, :], compare_op=ALU.not_equal,
                                    fill=1.0, base=0, pattern=[[-1, P]], channel_multiplier=1).then_inc(s_const, 1)

        @block.vector
        def _(v):
            v.memset(dst_i[:, EC - 1, :], -1).then_inc(s_clear, 1)
            v.memset(src_i[:, EC - 1, :], 0).then_inc(s_clear, 1)
            v.memset(w_f[:, EC - 1, :], 0.0).then_inc(s_clear, 1)
            v.memset(ends_i[:, :, :], FAR).then_inc(s_clear, 1)
            v.memset(c["X"][:, NT - 1, :], 0.0).then_inc(s_clear, 1)
            v.memset(c["eps"][:, :], EPS)
            v.memset(c["ones_row"][:, :], 1.0)
            v.memset(c["step_dst"][:, STEPS:STEPS + AHEAD], -1.0)
            v.memset(c["step_src"][:, STEPS:STEPS + R], 0)
            v.wait_ge(s_ends, 16 * 6)
            v.tensor_scalar(ends_b[:, :, :], ends_i[:, :, :], 7, None, ALU.arith_shift_right).then_inc(s_start, 1)
            v.wait_ge(s_start, 1)
            v.tensor_copy(ends_f[:, :, :], ends_b[:, :, :]).then_inc(s_start, 1)
            v.wait_ge(s_start, 2)
            v.wait_ge(s_const, 6)
            for k in range(2):
                v.tensor_tensor(start_f[:, k, :], ends_f[:, k, :], tile_f[:, :, 0], ALU.add).then_inc(s_start, 1)
            v.wait_ge(s_start, 4)
            v.tensor_scalar(start_f[:, 1, :], start_f[:, 1, :], 1.0, None, ALU.add).then_inc(s_start, 1)
            v.wait_ge(s_start, 5)
            for k in range(EC):
                if k >= 2:
                    v.wait_ge(s_sel, k - 1)
                v.tensor_scalar(ge[:, k % 2, :], step_i[:, :], start_f[:, 0, k:k + 1], None, ALU.is_ge).then_inc(s_ge, 1)
                v.wait_ge(s_ge, k + 1)
                v.scalar_tensor_tensor(out=sel[:, k, :], in0=step_i[:, :], scalar=start_f[:, 1, k:k + 1],
                                       in1=ge[:, k % 2, :], op0=ALU.is_lt, op1=ALU.mult).then_inc(s_sel, 1)
            v.wait_ge(s_edges, 16 * 9)
            v.tensor_copy(src_f[:, :, :], src_i[:, :, :]).then_inc(s_cast, 1)
            v.tensor_scalar(dst_f[:, :, :], dst_i[:, :, :], 1.0, None, ALU.add).then_inc(s_cast, 1)
            v.wait_ge(s_mm, 8)
            n = 0
            for h in range(2):
                r = slice(h * HALF, h * HALF + HALF)
                v.tensor_copy(c["step_src"][:, r], ps[0 + h][:, 0:HALF])
                v.tensor_copy(c["step_w"][:, r], ps[4 + h][:, 0:HALF])
                v.tensor_tensor(tmp[:, r], step_i[:, r], ps[6 + h][:, 0:HALF], ALU.subtract).then_inc(s_out, 1)
                n += 1
                v.wait_ge(s_out, n)
                v.tensor_scalar(c["step_off"][:, r], tmp[:, r], float(NT - 1), float(AW), ALU.min, ALU.mult).then_inc(s_out, 1)
                n += 1
                v.tensor_scalar(tmp2[:, r], tmp[:, r], float(-P), -1.0, ALU.mult, ALU.add).then_inc(s_out, 1)
                n += 1
                v.wait_ge(s_out, n)
                v.tensor_tensor(c["step_dst"][:, r], tmp2[:, r], ps[2 + h][:, 0:HALF], ALU.add)
            v.tensor_copy(seen[:, :], c["step_off"][:, U * LAG:STEPS:U]).then_inc(s_out, 1)
            v.wait_ge(s_out, n + 1)
            v.tensor_tensor(seen[:, :], seen[:, :], need[:, :], ALU.is_lt).then_inc(s_out, 1)
            v.wait_ge(s_out, n + 2)
            v.tensor_reduce(nlate[:, :], seen[:, :], AX.X, ALU.add).then_inc(s_out, 1)
            v.wait_ge(s_out, n + 3)
            v.tensor_scalar(c["late"][:, :], nlate[:, :], 1.0, None, ALU.min)

        @block.tensor
        def _(pe):
            pe.wait_ge(s_const, 6)
            pe.wait_ge(s_sel, EC)
            pe.wait_ge(s_edges, 16 * 9)
            pe.wait_ge(s_cast, 2)
            for q, lst in enumerate((src_f, dst_f, w_f, tile_f)):
                for h in range(2):
                    for k in range(EC):
                        mm = pe.matmul(ps[2 * q + h][:, 0:HALF], lst[:, k, :], sel[:, k, h * HALF:(h + 1) * HALF],
                                       start=(k == 0), stop=(k == EC - 1))
                    mm.then_inc(s_mm, 1)


def settle(eng):
    eng.nop(nofuse=True)


def gather_ring(nc, table, sb, sem, ctx):
    return dict(
        rows=sb("rows", [P, R, AW], F32, ctx), now=sb("now", [P, R], I32, ctx), hot=sb("hot", [P, OH, P], F32, ctx),
        table=table, s_now=sem("s_now"), s_row=[sem(f"s_row{u}") for u in range(R)],
        s_scaled=sem("s_scaled"), s_hot=sem("s_hot"), s_mm=sem("s_mm"), s_add=sem("s_add"),
    )


def steps_pool(nc, c, r, g, layer, table=None):
    table = r["table"] if table is None else table
    with g.Fori(0, NB) as i:
        now = g.snap((layer * NB + i) * (U // Q) + layer * (R // Q))
        for u in range(U):
            x = u % R
            if u % Q == 0:
                g.wait_ge(r["s_now"], now + (u // Q + 1))
                settle(g)
            nc.gpsimd.indirect_dma_start(
                out=r["rows"][:, x, 0:D], out_offset=None, in_=table[:, :],
                in_offset=bass.IndirectOffsetOnAxis(ap=r["now"][:, x:x + 1], axis=0)).then_inc(r["s_row"][x], 16)


def steps_tensor(nc, c, r, pe, psum, width, layer, bodies=(0, NB), between=None):
    scaled = isinstance(layer, int) and layer == 0
    with pe.Fori(*bodies) as i:
        landed = [pe.snap((layer * NB + i) * (16 * U // R) + 16 * (n + 1)) for n in range(U // R)]
        step = pe.snap((layer * NB + i) * U)
        hots = pe.snap(step + layer * AHEAD)
        for u in range(U):
            if scaled:
                if u % 2 == 0:
                    pe.wait_ge(r["s_scaled"], step + (u + 2))
            else:
                pe.wait_ge(r["s_row"][u % R], landed[u // R])
            if u % 2 == 0:
                pe.wait_ge(r["s_hot"], hots + (u + 2))
                pe.wait_ge(r["s_add"], step + (u + 2))
            pe.matmul(psum[u % OH][:, 0:width], r["hot"][:, u % OH, :], r["rows"][:, u % R, 0:width],
                      start=True, stop=True).then_inc(r["s_mm"], 1)
            if between is not None:
                between(i, u)


def steps_vector(nc, c, r, v, psum, width, layer, bodies=(0, NB), between=None):
    acc = c["ACC"][:, :, :].rearrange("p t d -> p (t d)")

    def hot(s, slot):
        v.tensor_scalar(r["hot"][:, slot, :], c["lane"][:, :], c["step_dst"][:, bass.ds(s, 1)], None,
                        ALU.is_equal).then_inc(r["s_hot"], 1)

    def indices(s, slot):
        v.tensor_copy(r["now"][:, slot:slot + Q], c["step_src"][:, bass.ds(s, Q)]).then_inc(r["s_now"], 1)

    if bodies[0] == 0:
        for u in range(0, R, Q):
            indices(u, u)
        for s in range(AHEAD):
            hot(s, s)
    with v.Fori(*bodies) as i:
        col = v.snap(i * U)
        step = v.snap((layer * NB + i) * U)
        for u in range(U):
            hot(col + (u + AHEAD), (u + AHEAD) % OH)
            if u % LOADS == 0:
                _, offs = nc.values_load_multi_w_load_instructions(
                    c["step_off"][0:1, bass.ds(col + u, LOADS)], engines=(mybir.EngineType.DVE,),
                    min_val=0, max_val=AW * (NT - 1),
                    skip_runtime_bounds_check_because="prepare() keeps every step's bucket within 0 and NT - 1")
            a = acc[:, bass.ds(offs[u % LOADS], width)]
            v.wait_ge(r["s_mm"], step + (u + 1))
            v.wait_ge(r["s_add"], step + (u + OH))
            v.tensor_tensor(a, psum[u % OH][:, 0:width], a, ALU.add).then_inc(r["s_add"], 1)
            if u % Q == Q - 1:
                indices(col + (u + 1 - Q + R), (u + 1 - Q) % R)
            if between is not None:
                between(i, u)


def steps_scale(nc, c, r, act, layer):
    with act.Fori(0, NB) as i:
        landed = [act.snap((layer * NB + i) * (16 * U // R) + 16 * (n + 1)) for n in range(U // R)]
        col = act.snap(i * U)
        for u in range(U):
            act.wait_ge(r["s_row"][u % R], landed[u // R])
            settle(act)
            act.activation(r["rows"][:, u % R, 0:D], r["rows"][:, u % R, 0:D], ACT.Copy,
                           scale=c["step_w"][:, bass.ds(col + u, 1)]).then_inc(r["s_scaled"], 1)


def credits(nc, r, v):
    v.memset(r["rows"][:, :, D:AW], 1.0)
    v.memset(r["hot"][:, :, :], 0.0).then_inc(r["s_add"], OH)


def first_layer(nc, ins, dram, c, sb, pb, sem):
    with ExitStack() as ctx:
        r = c["ring"]
        w = sb("w_both", [P, KD, 2 * D], F32, ctx)
        bias = sb("bias_a", [P, D], F32, ctx)
        xn = sb("xn_a", [P, TG, D], F32, ctx)
        xt = sb("xt_a", [P, TG, D], F32, ctx)
        h = sb("h_a", [P, NT, D], F32, ctx)
        stat = sb("stat_a", [P, TG, 6], F32, ctx)
        mv = sb("mv_a", [P, TG, 2], F32, ctx)
        sd = sb("sd_a", [P, TG], F32, ctx)
        rs = sb("rs_a", [P, TG], F32, ctx)
        s_w = sem("n_w")
        s_stat = sem("n_stat")
        s_mv = sem("n_mv")
        s_sd = sem("n_sd")
        s_rs = sem("n_rs")
        s_xn = sem("n_xn")
        s_T = sem("n_T")
        s_xt = sem("n_xt")
        s_M = sem("n_M")
        s_h = sem("n_h")
        s_own = sem("n_own")
        s_acc = sem("n_acc")
        s_tab = sem("n_tab")

        with ExitStack() as pc, nc.Block() as block:
            pT = [pb(f"pT_a{k}", pc) for k in range(2)]
            pN = [pb(f"pN_a{k}", pc) for k in range(3)]
            pO = [pb(f"pO_a{k}", pc) for k in range(3)]

            @block.sync
            def _(sp):
                sp.dma_start(w[:, :, 0:D], ins["L0_gnn_w_nbr"].rearrange("(k p) d -> p k d", p=P)).then_inc(s_w, 16)
                sp.dma_start(w[:, :, D:2 * D], ins["L0_gnn_w_own"].rearrange("(k p) d -> p k d", p=P)).then_inc(s_w, 16)
                sp.dma_start(bias[:, :], ins["L0_gnn_bias"].rearrange("(o d) -> o d", o=1).to_broadcast([P, D])).then_inc(s_w, 16)
                table = dram["table"].rearrange("(t p) d -> p t d", p=P)
                with sp.Fori(0, NG) as g:
                    sp.wait_ge(s_h, g * TG + TG)
                    sp.dma_start(table[:, bass.ds(g * TG, TG), :], h[:, bass.ds(g * TG, TG), :]).then_inc(s_tab, 16)
                sp.wait_ge(s_tab, 16 * NG)

            @block.vector
            def _(v):
                credits(nc, r, v)
                v.wait_ge(s_w, 48)
                with v.Fori(0, NG) as g:
                    for u in range(TG):
                        v.bn_stats(stat[:, u, :], c["X"][:, g * TG + u, :]).then_inc(s_stat, 1)
                    v.wait_ge(s_stat, g * TG + TG)
                    settle(v)
                    for u in range(TG):
                        v.bn_aggr(mv[:, u, :], stat[:, u, :]).then_inc(s_mv, 1)
                    v.wait_ge(s_sd, g + 1)
                    v.reciprocal(rs[:, :], sd[:, :]).then_inc(s_rs, 1)
                    v.wait_ge(s_rs, g + 1)
                    for u in range(TG):
                        v.wait_ge(s_M, g * TG + 1)
                        v.tensor_scalar(xn[:, u, :], c["X"][:, g * TG + u, :], mv[:, u, 0:1], rs[:, u:u + 1],
                                        ALU.subtract, ALU.mult).then_inc(s_xn, 1)
                    for u in range(TG):
                        t = g * TG + u
                        v.wait_ge(s_M, t + 2)
                        v.tensor_tensor(c["ACC"][:, t, 0:D], pO[u % 3][:, 0:D], c["X"][:, t, :], ALU.add).then_inc(s_own, 1)
                        v.wait_ge(s_own, t + 1)
                        v.tensor_tensor(c["ACC"][:, t, 0:D], c["ACC"][:, t, 0:D], bias[:, :], ALU.add).then_inc(s_acc, 1)
                v.memset(c["ACC"][:, :, D:AW], 1.0)

            @block.scalar
            def _(act):
                with act.Fori(0, NG) as g:
                    act.wait_ge(s_mv, g * TG + TG)
                    act.activation(sd[:, :], mv[:, :, 1], ACT.Sqrt, bias=c["eps"][:, 0:1]).then_inc(s_sd, 1)
                    for u in range(TG + 1):
                        if u < TG:
                            t = g * TG + u
                            act.wait_ge(s_T, t + 1)
                            act.activation(xt[:, u, :], pT[u % 2][:, 0:D], ACT.Copy).then_inc(s_xt, 1)
                        if u > 0:
                            t = g * TG + u - 1
                            act.wait_ge(s_M, t + 2)
                            settle(act)
                            act.activation(h[:, t, :], pN[(u - 1) % 3][:, 0:D], ACT.Copy).then_inc(s_h, 1)

            @block.tensor
            def _(pe):
                pe.wait_ge(s_w, 48)
                pe.matmul(pN[0][:, 0:P], c["ident"][:, :], c["ident"][:, :], start=True, stop=True).then_inc(s_M, 1)

                def turn(g, u):
                    pe.wait_ge(s_xn, g * TG + u + 1)
                    if u >= 2:
                        pe.wait_ge(s_xt, g * TG + u - 1)
                    for k in range(KD):
                        mm = pe.transpose(pT[u % 2][:, k * P:(k + 1) * P], xn[:, u, k * P:(k + 1) * P], c["ident"][:, :])
                    mm.then_inc(s_T, 1)

                with pe.Fori(0, NG) as g:
                    turn(g, 0)
                    for u in range(TG):
                        if u + 1 < TG:
                            turn(g, u + 1)
                        t = g * TG + u
                        pe.wait_ge(s_xt, t + 1)
                        if u >= 3:
                            pe.wait_ge(s_h, t - 2)
                            pe.wait_ge(s_own, t - 2)
                        for n, bank in enumerate((pN[u % 3], pO[u % 3])):
                            for k in range(KD):
                                mm = pe.matmul(bank[:, 0:D], xt[:, u, k * P:(k + 1) * P], w[:, k, n * D:(n + 1) * D],
                                               start=(k == 0), stop=(k == KD - 1))
                        mm.then_inc(s_M, 1)

        with ExitStack() as pc, nc.Block() as block:
            psum = [pb(f"pa{k}", pc) for k in range(OH)]

            @block.gpsimd
            def _(g):
                steps_pool(nc, c, r, g, 0)

            @block.scalar
            def _(act):
                steps_scale(nc, c, r, act, 0)

            @block.tensor
            def _(pe):
                steps_tensor(nc, c, r, pe, psum, AW, 0)

            @block.vector
            def _(v):
                steps_vector(nc, c, r, v, psum, AW, 0)



def wait(eng, s, value):
    if not isinstance(value, int) or value > 0:
        eng.wait_ge(s, value)


def route(nc, ins, dram, c, moe, sb, pb, sem):
    with ExitStack() as ctx:
        u1 = sb("u_r", [P, TG, D], F32, ctx)
        ut = sb("ut_r", [P, TG, D], F32, ctx)
        wr = sb("wr_r", [P, KD, NE], F32, ctx)
        br = sb("br_r", [P, NE], F32, ctx)
        lg = sb("lg_r", [P, TG, NE], F32, ctx)
        zero = sb("zero_r", [P, 2 * D], F32, ctx)
        stat = sb("stat_r", [P, TG, 6], F32, ctx)
        mv = sb("mv_r", [P, TG, 2], F32, ctx)
        sd = sb("sd_r", [P, TG], F32, ctx)
        rs = sb("rs_r", [P, TG], F32, ctx)
        t8 = sb("t8_r", [P, TG, 8], F32, ctx)
        i8 = sb("i8_r", [P, TG, 8], U32, ctx)
        dsd = sb("dsd_r", [P, NT], F32, ctx)
        s_w, s_zero, s_fill = sem("r_w"), sem("r_zero"), sem("r_fill")
        s_deg, s_stat, s_mv, s_sd, s_rs = sem("r_deg"), sem("r_stat"), sem("r_mv"), sem("r_sd"), sem("r_rs")
        s_u, s_x, s_T, s_ut, s_L, s_lg, s_top = (sem("r_u"), sem("r_x"), sem("r_T"), sem("r_ut"), sem("r_L"),
                                                 sem("r_lg"), sem("r_top"))
        pT = [pb(f"pT_r{k}", ctx) for k in range(3)]
        pL = [pb(f"pL_r{k}", ctx) for k in range(3)]
        block = ctx.enter_context(nc.Block())

        @block.sync
        def _(sp):
            sp.dma_start(wr[:, :, :], ins["L0_ffn_Wr"].rearrange("(k p) e -> p k e", p=P)).then_inc(s_w, 16)
            sp.dma_start(br[:, :], ins["L0_ffn_br"].rearrange("(o e) -> o e", o=1).to_broadcast([P, NE])).then_inc(s_w, 16)
            for e in range(NE):
                at = 0
                for name, n in (("L0_ffn_ln_g", KD), ("L0_ffn_ln_b", KD), ("L0_ffn_b1", HJ)):
                    sp.dma_start(moe["prm"][:, e, at:at + n], ins[name][e, :].rearrange("(k p) -> p k", p=P),
                                 allow_slow_non_contiguous=True).then_inc(s_w, 16)
                    at += n
            sp.wait_ge(s_zero, 1)
            sp.dma_start(dram["disp"].rearrange("(b p r) d -> p b (r d)", p=P, r=2),
                         zero[:, :].rearrange("p (o d) -> p o d", o=1).to_broadcast([P, NBLK + 1, 2 * D])).then_inc(s_fill, 16)
            sp.dma_start(dram["y"][SLOTS:SLOTS + BR, :].rearrange("(p r) d -> p (r d)", r=2), zero[:, :]).then_inc(s_fill, 16)
            sp.wait_ge(s_fill, 32)
            sp.wait_ge(s_w, 16 * (2 + 3 * NE))

        @block.vector
        def _(v):
            v.memset(zero[:, :], 0.0).then_inc(s_zero, 1)
            v.wait_ge(s_deg, 1)
            v.reciprocal(c["dinv"][:, :], dsd[:, :])
            v.wait_ge(s_w, 16 * (2 + 3 * NE))

            def normalise(g, src, dst, r, done):
                for u in range(TG):
                    v.bn_stats(stat[:, u, :], src(u)).then_inc(s_stat, 1)
                v.wait_ge(s_stat, r * TG + TG)
                settle(v)
                for u in range(TG):
                    v.bn_aggr(mv[:, u, :], stat[:, u, :]).then_inc(s_mv, 1)
                v.wait_ge(s_sd, r + 1)
                v.reciprocal(rs[:, :], sd[:, :]).then_inc(s_rs, 1)
                v.wait_ge(s_rs, r + 1)
                for u in range(TG):
                    v.tensor_scalar(dst(u), src(u), mv[:, u, 0:1], rs[:, u:u + 1],
                                    ALU.subtract, ALU.mult).then_inc(done, 1)

            with v.Fori(0, NG) as g:
                normalise(g, lambda u: c["ACC"][:, g * TG + u, 0:D], lambda u: u1[:, u, :], g * 2, s_u)
                v.wait_ge(s_u, g * TG + TG)
                normalise(g, lambda u: u1[:, u, :], lambda u: c["X"][:, g * TG + u, :], g * 2 + 1, s_x)
                for u in range(TG):
                    v.wait_ge(s_L, g * TG + u + 1)
                    v.tensor_tensor(lg[:, u, :], pL[u % 3][:, 0:NE], br[:, :], ALU.add).then_inc(s_lg, 1)
                v.wait_ge(s_lg, g * TG + TG)
                settle(v)
                for u in range(TG):
                    v.max(t8[:, u, :], lg[:, u, :]).then_inc(s_top, 1)
                v.wait_ge(s_top, g * (3 * TG) + TG)
                settle(v)
                for u in range(TG):
                    v.max_index(i8[:, u, :], t8[:, u, :], lg[:, u, :]).then_inc(s_top, 2)
                v.wait_ge(s_top, g * (3 * TG) + 3 * TG)
                settle(v)
                v.tensor_copy(moe["top"][:, bass.ds(g * TG, TG), :], t8[:, :, 0:2])
                v.tensor_copy(moe["idx"][:, bass.ds(g * TG, TG), :], i8[:, :, 0:2])

        @block.scalar
        def _(act):
            act.activation(dsd[:, :], c["ACC"][:, :, D], ACT.Sqrt).then_inc(s_deg, 1)
            with act.Fori(0, NG) as g:
                for k in range(2):
                    act.wait_ge(s_mv, (g * 2 + k) * TG + TG)
                    act.activation(sd[:, :], mv[:, :, 1], ACT.Sqrt, bias=c["eps"][:, 0:1]).then_inc(s_sd, 1)
                for u in range(TG):
                    act.wait_ge(s_T, g * TG + u + 1)
                    act.activation(ut[:, u, :], pT[u % 3][:, 0:D], ACT.Copy).then_inc(s_ut, 1)

        @block.tensor
        def _(pe):
            pe.wait_ge(s_w, 16 * (2 + 3 * NE))

            def turn(g, u):
                pe.wait_ge(s_u, g * TG + u + 1)
                if u >= 3:
                    pe.wait_ge(s_ut, g * TG + u - 2)
                for k in range(KD):
                    mm = pe.transpose(pT[u % 3][:, k * P:(k + 1) * P], u1[:, u, k * P:(k + 1) * P], c["ident"][:, :])
                mm.then_inc(s_T, 1)

            with pe.Fori(0, NG) as g:
                turn(g, 0)
                for u in range(TG):
                    if u + 1 < TG:
                        turn(g, u + 1)
                    pe.wait_ge(s_ut, g * TG + u + 1)
                    if u >= 3:
                        pe.wait_ge(s_lg, g * TG + u - 2)
                    for k in range(KD):
                        mm = pe.matmul(pL[u % 3][:, 0:NE], ut[:, u, k * P:(k + 1) * P], wr[:, k, :],
                                       start=(k == 0), stop=(k == KD - 1))
                    mm.then_inc(s_L, 1)


def place(nc, c, moe, sb, pb, sem):
    with ExitStack() as ctx:
        EN = NE * NT
        node = sb("node", [P, NT], F32, ctx)
        blk = sb("blk", [P, NBLK + 1], F32, ctx)
        before = sb("before", [P, P], F32, ctx)
        ones = sb("ones", [P, P], F32, ctx)
        idxf = sb("idxf", [P, 2, NT], F32, ctx)
        gap = sb("gap", [P, NT], F32, ctx)
        ratio = sb("ratio", [P, NT], F32, ctx)
        den = sb("den", [P, NT], F32, ctx)
        spare = sb("spare", [P, 2, NT], F32, ctx)
        mk = sb("mk", [P, 2, NE, NT], F32, ctx)
        m = sb("m", [P, NE, NT], F32, ctx)
        cnt = sb("cnt", [P, NE, NT], F32, ctx)
        inc = sb("inc", [P, NE, NT], F32, ctx)
        row = sb("row", [P, NE, NT], F32, ctx)
        nbi = sb("nbi", [P, 2, NE], I32, ctx)
        nbf = sb("nbf", [P, NE], F32, ctx)
        cum = sb("cum", [P, NE], F32, ctx)
        base = sb("base", [P, NE], F32, ctx)
        posf = sb("posf", [P, 2, NT], F32, ctx)
        ebf = sb("ebf", [P, NBLK + 1], F32, ctx)
        pW, pC = pb("pW", ctx), pb("pC", ctx)
        s_c, s_v, s_e, s_r, s_mm = sem("l_const"), sem("l_step"), sem("l_exp"), sem("l_gap"), sem("l_mm")
        s_m = sem("l_m")
        block = ctx.enter_context(nc.Block())

        @block.gpsimd
        def _(g):
            nc.gpsimd.iota(node[:, :], [[P, NT]], base=0, channel_multiplier=1,
                           allow_small_or_imprecise_dtypes=True).then_inc(s_c, 1)
            nc.gpsimd.iota(blk[:, :], [[1, NBLK + 1]], base=0, channel_multiplier=0,
                           allow_small_or_imprecise_dtypes=True).then_inc(s_c, 1)
            nc.gpsimd.memset(ones[:, :], 1.0).then_inc(s_c, 1)
            g.wait_ge(s_c, 3)
            nc.gpsimd.affine_select(out=before[:, :], in_=ones[:, :], compare_op=ALU.is_gt, fill=0.0,
                                    base=0, pattern=[[1, P]], channel_multiplier=-1).then_inc(s_c, 1)

        @block.scalar
        def _(act):
            act.wait_ge(s_r, 1)
            act.activation(ratio[:, :], gap[:, :], ACT.Exp).then_inc(s_e, 1)

        @block.tensor
        def _(pe):
            pe.wait_ge(s_c, 4)
            pe.wait_ge(s_m, 1)
            mf = m[:, :, :].rearrange("p e t -> p (e t)")
            pe.matmul(pW[:, 0:EN], before[:, :], mf, start=True, stop=True).then_inc(s_mm, 1)
            pe.matmul(pC[:, 0:EN], ones[:, :], mf, start=True, stop=True).then_inc(s_mm, 1)

        @block.vector
        def _(v):
            n = [0]

            def then(ins):
                ins.then_inc(s_v, 1)
                n[0] += 1
                v.wait_ge(s_v, n[0])

            v.wait_ge(s_c, 4)
            v.tensor_tensor(gap[:, :], moe["top"][:, :, 1], moe["top"][:, :, 0], ALU.subtract).then_inc(s_r, 1)
            v.tensor_scalar(c["valid"][:, :], node[:, :], float(N), None, ALU.is_lt)
            for k in range(2):
                ins = v.tensor_copy(idxf[:, k, :], moe["idx"][:, :, k])
            then(ins)
            for k in range(2):
                for e in range(NE):
                    ins = v.scalar_tensor_tensor(out=mk[:, k, e, :], in0=idxf[:, k, :], scalar=float(e),
                                                 in1=c["valid"][:, :], op0=ALU.is_equal, op1=ALU.mult)
            then(ins)
            v.tensor_tensor(m[:, :, :], mk[:, 0, :, :], mk[:, 1, :, :], ALU.add).then_inc(s_m, 1)
            v.wait_ge(s_e, 1)
            then(v.tensor_scalar(den[:, :], ratio[:, :], 1.0, None, ALU.add))
            then(v.reciprocal(moe["wt"][:, 0, :], den[:, :]))
            v.tensor_tensor(moe["wt"][:, 1, :], moe["wt"][:, 0, :], ratio[:, :], ALU.mult)
            for k in range(2):
                v.tensor_scalar(spare[:, k, :], node[:, :], float(SLOTS - (NT - 1) * P + k * P), None, ALU.add)
            then(v.tensor_scalar(gap[:, :], c["valid"][:, :], -1.0, 1.0, ALU.mult, ALU.add))
            for k in range(2):
                ins = v.tensor_tensor(spare[:, k, :], spare[:, k, :], gap[:, :], ALU.mult)
            then(ins)
            v.wait_ge(s_mm, 2)
            then(v.tensor_copy(cnt[:, :, :], pC[:, 0:EN].rearrange("p (e t) -> p e t", e=NE)))
            for e in range(NE):
                ins = v.tensor_tensor_scan(out=inc[:, e, :], data0=c["ones_row"][:, :], data1=cnt[:, e, :],
                                           initial=0.0, op0=ALU.mult, op1=ALU.add)
            then(ins)
            then(v.tensor_scalar(nbi[:, 0, :], inc[:, :, NT - 1], float(BR - 1), None, ALU.add))
            then(v.tensor_scalar(nbi[:, 1, :], nbi[:, 0, :], 8, None, ALU.arith_shift_right))
            then(v.tensor_copy(nbf[:, :], nbi[:, 1, :]))
            then(v.tensor_tensor_scan(out=cum[:, :], data0=c["ones_row"][:, 0:NE], data1=nbf[:, :],
                                      initial=0.0, op0=ALU.mult, op1=ALU.add))
            then(v.tensor_tensor(base[:, :], cum[:, :], nbf[:, :], ALU.subtract))
            then(v.tensor_scalar(base[:, :], base[:, :], float(BR), None, ALU.mult))
            then(v.tensor_tensor(row[:, :, :], inc[:, :, :], cnt[:, :, :], ALU.subtract))
            then(v.tensor_tensor(row[:, :, :], row[:, :, :], pW[:, 0:EN].rearrange("p (e t) -> p e t", e=NE), ALU.add))
            for e in range(NE):
                ins = v.tensor_scalar(row[:, e, :], row[:, e, :], base[:, e:e + 1], None, ALU.add)
            then(ins)
            for k in range(2):
                ins = v.tensor_tensor(mk[:, k, :, :], mk[:, k, :, :], row[:, :, :], ALU.mult)
            then(ins)
            for k in range(2):
                ins = v.tensor_reduce(posf[:, k, :], mk[:, k, :, :].rearrange("p e t -> p t e"), AX.X, ALU.add)
            then(ins)
            v.tensor_tensor(moe["pos"][:, :, :], posf[:, :, :], spare[:, :, :], ALU.add)
            then(v.memset(ebf[:, :], 0.0))
            for e in range(NE):
                then(v.scalar_tensor_tensor(out=ebf[:, :], in0=blk[:, :], scalar=cum[:, e:e + 1], in1=ebf[:, :],
                                            op0=ALU.is_ge, op1=ALU.add))
            v.tensor_scalar(moe["expert"][:, :], ebf[:, :], float(NE - 1), None, ALU.min)


def dispatch(nc, dram, c, moe, sb, sem):
    with ExitStack() as ctx:
        stage = sb("stage_d", [P, TG, D], F32, ctx)
        now = sb("now_d", [P, 2, TG], I32, ctx)
        s_now, s_stage, s_put = sem("d_now"), sem("d_stage"), sem("d_put")
        block = ctx.enter_context(nc.Block())

        @block.scalar
        def _(act):
            def body(g):
                wait(act, s_put, g * (32 * TG))
                if not isinstance(g, int):
                    settle(act)
                for u in range(TG):
                    act.activation(stage[:, u, :], c["X"][:, g * TG + u, :], ACT.Copy).then_inc(s_stage, 1)
            body(0)
            with act.Fori(1, NG) as g:
                body(g)

        @block.gpsimd
        def _(q):
            def body(g):
                wait(q, s_put, g * (32 * TG))
                if not isinstance(g, int):
                    settle(q)
                for k in range(2):
                    nc.gpsimd.tensor_copy(now[:, k, :], moe["pos"][:, k, bass.ds(g * TG, TG)]).then_inc(s_now, 1)
                q.wait_ge(s_now, g * 2 + 2)
                for u in range(TG):
                    q.wait_ge(s_stage, g * TG + u + 1)
                    settle(q)
                    for k in range(2):
                        nc.gpsimd.indirect_dma_start(
                            out=dram["disp"][:, :], out_offset=bass.IndirectOffsetOnAxis(ap=now[:, k, u:u + 1], axis=0),
                            in_=stage[:, u, :], in_offset=None).then_inc(s_put, 16)
            body(0)
            with q.Fori(1, NG) as g:
                body(g)
            q.wait_ge(s_put, NG * 32 * TG)


def experts(nc, ins, dram, c, moe, sb, pb, sem):
    with ExitStack() as ctx:
        w1 = sb("w1_e", [P, 2, KD, HID], F32, ctx)
        w2 = sb("w2_e", [P, 2, HJ, D], F32, ctx)
        b2 = sb("b2_e", [P, 2, D], F32, ctx)
        tok = sb("tok_e", [P, 2, 2, D], F32, ctx)
        prm = sb("prm_e", [P, 2, PRM], F32, ctx)
        xe = sb("xe_e", [P, 2, KD, BR], F32, ctx)
        h = sb("h_e", [P, HJ, BR], F32, ctx)
        y = sb("y_e", [P, 2, 2, D], F32, ctx)
        pT = pb("pT_e", ctx)
        pH = [pb(f"pH_e{k}", ctx) for k in range(HJ // 2)]
        pY = [pb(f"pY_e{k}", ctx) for k in range(2)]
        s_w = [sem(f"e_w{q}") for q in range(2)]
        s_tok = [sem(f"e_tok{q}") for q in range(2)]
        s_st = [sem(f"e_store{q}") for q in range(2)]
        s_prm, s_T, s_xe, s_mm1, s_h, s_mm2, s_y = (sem("e_prm"), sem("e_T"), sem("e_xe"), sem("e_mm1"), sem("e_h"),
                                                    sem("e_mm2"), sem("e_y"))
        rows = dram["disp"].rearrange("(b m p) d -> p b m d", m=2, p=P)
        yrows = dram["y"].rearrange("(b m p) d -> p b m d", m=2, p=P)
        w1_d = ins["L0_ffn_W1"].rearrange("e (k p) h -> p e k h", p=P)
        w2_d = ins["L0_ffn_W2"].rearrange("e (j p) d -> p e j d", p=P)
        b2_d = ins["L0_ffn_b2"]
        block = ctx.enter_context(nc.Block())

        def pairs(eng, body):
            body(0)
            with eng.Fori(1, NBLK // 2) as i:
                body(i)

        @block.sync
        def _(sp):
            def tokens(b, q, use):
                wait(sp, s_T, b - 1)
                sp.dma_start(tok[:, q, :, :], rows[:, b, :, :]).then_inc(s_tok[q], 16)

            tokens(0, 0, 0)

            def body(i):
                for q in range(2):
                    b = i * 2 + q
                    e = sp.value_load(moe["expert"][0:1, bass.ds(b, 1)], min_val=0, max_val=NE - 1)
                    wait(sp, s_mm2, b - 1)
                    sp.dma_start(w1[:, q, :, :], w1_d[:, bass.ds(e, 1), :, :].rearrange("p o k h -> p (o k) h")).then_inc(s_w[q], 16)
                    sp.dma_start(w2[:, q, :, :], w2_d[:, bass.ds(e, 1), :, :].rearrange("p o j d -> p (o j) d")).then_inc(s_w[q], 16)
                    wait(sp, s_y, b * 2 - 2)
                    sp.dma_start(b2[:, q, :], b2_d[bass.ds(e, 1), :].to_broadcast([P, D])).then_inc(s_w[q], 16)
                    tokens(b + 1, 1 - q, None)
            pairs(sp, body)

        @block.vector
        def _(v):
            def inputs(b, q):
                e = v.value_load(moe["expert"][0:1, bass.ds(b, 1)], min_val=0, max_val=NE - 1)
                wait(v, s_h, b * 4 - 4)
                v.tensor_copy(prm[:, q, :], moe["prm"][:, bass.ds(e, 1), :].rearrange("p o n -> p (o n)")).then_inc(s_prm, 1)
                v.wait_ge(s_prm, b + 1)
                v.wait_ge(s_T, b + 1)
                for k in range(KD):
                    ins_ = v.tensor_scalar(xe[:, q, k, :], pT[:, k * BR:(k + 1) * BR], prm[:, q, k:k + 1],
                                           prm[:, q, KD + k:KD + k + 1], ALU.mult, ALU.add)
                ins_.then_inc(s_xe, 1)

            inputs(0, 0)

            def body(i):
                for q in range(2):
                    b = i * 2 + q
                    inputs(b + 1, 1 - q)
                    wait(v, s_st[q], i * 16)
                    if not isinstance(i, int):
                        settle(v)
                    v.wait_ge(s_mm2, b + 1)
                    for m in range(2):
                        v.tensor_tensor(y[:, q, m, :], pY[m][:, 0:D], b2[:, q, :], ALU.add).then_inc(s_y, 1)
            pairs(v, body)

        @block.scalar
        def _(act):
            def body(i):
                for q in range(2):
                    b = i * 2 + q
                    for j in range(HJ // 2):
                        act.wait_ge(s_mm1, b * (HJ // 2) + j + 1)
                        for n in range(2):
                            k = 2 * j + n
                            a = act.activation(h[:, k, :], pH[j][:, n * BR:(n + 1) * BR], ACT.Gelu,
                                               bias=prm[:, q, 2 * KD + k:2 * KD + k + 1])
                        a.then_inc(s_h, 1)
            pairs(act, body)

        @block.tensor
        def _(pe):
            def turn(b, q):
                pe.wait_ge(s_tok[q], 16)
                for m in range(2):
                    for k in range(KD):
                        mm = pe.transpose(pT[:, k * BR + m * P:k * BR + (m + 1) * P], tok[:, q, m, k * P:(k + 1) * P], c["ident"][:, :])
                mm.then_inc(s_T, 1)

            turn(0, 0)

            def body(i):
                for q in range(2):
                    b = i * 2 + q
                    pe.wait_ge(s_xe, b + 1)
                    pe.wait_ge(s_w[q], i * 48 + 48)
                    for j in range(HJ // 2):
                        for n in range(2):
                            o = (2 * j + n) * P
                            for k in range(KD):
                                mm = pe.matmul(pH[j][:, n * BR:(n + 1) * BR], w1[:, q, k, o:o + P], xe[:, q, k, :],
                                               start=(k == 0), stop=(k == KD - 1))
                        mm.then_inc(s_mm1, 1)
                    pe.wait_ge(s_tok[1 - q], i * 16 + 16 * (1 + q))
                    for m in range(2):
                        for k in range(KD):
                            mm = pe.transpose(pT[:, k * BR + m * P:k * BR + (m + 1) * P], tok[:, 1 - q, m, k * P:(k + 1) * P],
                                              c["ident"][:, :])
                    mm.then_inc(s_T, 1)
                    wait(pe, s_y, b * 2)
                    for j in range(HJ):
                        if j % 2 == 0:
                            pe.wait_ge(s_h, b * (HJ // 2) + j // 2 + 1)
                        for m in range(2):
                            mm = pe.matmul(pY[m][:, 0:D], h[:, j, m * P:(m + 1) * P], w2[:, q, j, :],
                                           start=(j == 0), stop=(j == HJ - 1))
                    mm.then_inc(s_mm2, 1)
            pairs(pe, body)

        @block.gpsimd
        def _(g):
            def body(i):
                for q in range(2):
                    b = i * 2 + q
                    g.wait_ge(s_y, b * 2 + 2)
                    settle(g)
                    g.dma_start(yrows[:, b, :, :], y[:, q, :, :]).then_inc(s_st[q], 16)
            pairs(g, body)
            for q in range(2):
                g.wait_ge(s_st[q], 16 * (NBLK // 2))


def mixture(nc, ins, dram, c, moe, sb, pb, sem):
    route(nc, ins, dram, c, moe, sb, pb, sem)
    place(nc, c, moe, sb, pb, sem)
    dispatch(nc, dram, c, moe, sb, sem)
    experts(nc, ins, dram, c, moe, sb, pb, sem)


def convolutions(nc, ins, dram, c, moe, sb, pb, sem):
    with ExitStack() as ctx:
        w = sb("w_g", [P, LAYERS, KD, D], F32, ctx)
        vec = sb("vec_g", [P, 3, LAYERS, D], F32, ctx)
        b = dict(
            w=w, vec=vec, z=sb("z_g", [P, TG, D], F32, ctx), xin=sb("xin_g", [P, TG, D], F32, ctx),
            xt=sb("xt_g", [P, TG, D], F32, ctx), stat=sb("stat_g", [P, TG, 6], F32, ctx),
            mv=sb("mv_g", [P, TG, 2], F32, ctx), sd=sb("sd_g", [P, TG], F32, ctx), rs=sb("rs_g", [P, TG], F32, ctx),
        )
        q = {name: sem(f"g_{name}") for name in (
            "w", "z", "stat", "mv", "sd", "rs", "zz", "z2", "z3", "xin", "T", "xt", "M", "h", "tab")}
        bank = [pb(f"bank_g{k}", ctx) for k in range(8)]
        b.update(pS=bank[0:OH], pT=bank[4:6], pM=bank[6:8])
        combine(nc, ins, dram, c, moe, b, q, sb, sem)
        late = nc.values_load(c["late"][0:1, 0:1], min_val=0, max_val=1,
                              skip_runtime_bounds_check_because="it is the minimum of 1 and a count")
        with nc.If(late > 0):
            layers_apart(nc, dram, c, b, q)
        with nc.Else():
            layers_overlapped(nc, dram, c, b, q)


def moments(v, b, q, n, src):
    for u in range(TG):
        v.bn_stats(b["stat"][:, u, :], src(u)).then_inc(q["stat"], 1)
    v.wait_ge(q["stat"], n * TG + TG)
    settle(v)
    for u in range(TG):
        v.bn_aggr(b["mv"][:, u, :], b["stat"][:, u, :]).then_inc(q["mv"], 1)
    v.wait_ge(q["sd"], n + 1)
    v.reciprocal(b["rs"][:, :], b["sd"][:, :]).then_inc(q["rs"], 1)
    v.wait_ge(q["rs"], n + 1)


def nodes_tensor(pe, c, b, q, l):
    w = b["w"]

    def turn(g, u):
        t = g * TG + u
        pe.wait_ge(q["xin"], l * NT + t + 1)
        if u >= 1:
            pe.wait_ge(q["xt"], l * NT + t)
        for k in range(KD):
            mm = pe.transpose(b["pT"][0][:, k * P:(k + 1) * P], b["xin"][:, u, k * P:(k + 1) * P], c["ident"][:, :])
        mm.then_inc(q["T"], 1)

    with pe.Fori(0, NG) as g:
        turn(g, 0)
        for u in range(TG):
            if u + 1 < TG:
                turn(g, u + 1)
            t = g * TG + u
            pe.wait_ge(q["xt"], l * NT + t + 1)
            if u >= 2:
                pe.wait_ge(q["h"], l * NT + t - 1)
            for k in range(KD):
                mm = pe.matmul(b["pM"][u % 2][:, 0:D], b["xt"][:, u, k * P:(k + 1) * P],
                               w[:, l, k, :] if isinstance(l, int) else w[:, bass.ds(l, 1), k, :].rearrange("p o d -> p (o d)"),
                               start=(k == 0), stop=(k == KD - 1))
            mm.then_inc(q["M"], 1)


def nodes_scalar(act, c, b, q, l):
    with act.Fori(0, NG) as g:
        act.wait_ge(q["mv"], l * NT + g * TG + TG)
        act.activation(b["sd"][:, :], b["mv"][:, :, 1], ACT.Sqrt, bias=c["eps"][:, 0:1]).then_inc(q["sd"], 1)
        if not isinstance(l, int):
            for u in range(TG):
                act.wait_ge(q["z3"], (l - 1) * NT + g * TG + u + 1)
                act.activation(b["xin"][:, u, :], b["z"][:, u, :], ACT.Relu).then_inc(q["xin"], 1)
        for u in range(TG + 1):
            if u < TG:
                act.wait_ge(q["T"], l * NT + g * TG + u + 1)
                act.activation(b["xt"][:, u, :], b["pT"][0][:, 0:D], ACT.Copy).then_inc(q["xt"], 1)
            if u > 0:
                t = g * TG + u - 1
                act.wait_ge(q["M"], l * NT + t + 2)
                settle(act)
                act.activation(c["ACC"][:, t, 0:D], b["pM"][(u - 1) % 2][:, 0:D], ACT.Copy,
                               scale=c["dinv"][:, bass.ds(t, 1)]).then_inc(q["h"], 1)


def nodes_sync(sp, dram, c, q, l):
    table = dram["table"].rearrange("(t p) d -> p t d", p=P)
    with sp.Fori(0, NG) as g:
        sp.wait_ge(q["h"], l * NT + g * TG + TG)
        sp.dma_start(table[:, bass.ds(g * TG, TG), :], c["ACC"][:, bass.ds(g * TG, TG), 0:D]).then_inc(q["tab"], 16)


def combine(nc, ins, dram, c, moe, b, q, sb, sem):
    w, vec, xin, mv, rs = b["w"], b["vec"], b["xin"], b["mv"], b["rs"]
    with ExitStack() as ctx:
        got = sb("got_c", [P, 2, TG, D], F32, ctx)
        now = sb("now_c", [P, 2, TG], I32, ctx)
        s_now, s_sum = sem("c_now"), sem("c_sum")
        s_got = [sem(f"c_got{u}") for u in range(TG)]
        block = ctx.enter_context(nc.Block())

        @block.sync
        def _(sp):
            sp.dma_start(w[:, :, :, :], ins["L1_gnn_W"].rearrange("l (k p) d -> p l k d", p=P)).then_inc(q["w"], 16)
            for k, name in enumerate(("L1_gnn_b", "L1_gnn_gamma", "L1_gnn_beta")):
                sp.dma_start(vec[:, k, :, :], ins[name].rearrange("(o l) d -> o l d", o=1).to_broadcast([P, LAYERS, D])).then_inc(q["w"], 16)
            nodes_sync(sp, dram, c, q, 0)
            sp.wait_ge(q["tab"], 16 * NG)
            sp.wait_ge(q["w"], 64)

        @block.gpsimd
        def _(g_):
            def body(g):
                wait(g_, s_sum, g * (2 * TG))
                if not isinstance(g, int):
                    settle(g_)
                for k in range(2):
                    nc.gpsimd.tensor_copy(now[:, k, :], moe["pos"][:, k, bass.ds(g * TG, TG)]).then_inc(s_now, 1)
                g_.wait_ge(s_now, g * 2 + 2)
                settle(g_)
                for u in range(TG):
                    for k in range(2):
                        nc.gpsimd.indirect_dma_start(
                            out=got[:, k, u, :], out_offset=None, in_=dram["y"][:, :],
                            in_offset=bass.IndirectOffsetOnAxis(ap=now[:, k, u:u + 1], axis=0)).then_inc(s_got[u], 16)
            body(0)
            with g_.Fori(1, NG) as g:
                body(g)

        @block.tensor
        def _(pe):
            pe.wait_ge(q["w"], 64)
            pe.matmul(b["pM"][0][:, 0:P], c["ident"][:, :], c["ident"][:, :], start=True, stop=True).then_inc(q["M"], 1)
            nodes_tensor(pe, c, b, q, 0)

        @block.scalar
        def _(act):
            nodes_scalar(act, c, b, q, 0)

        @block.vector
        def _(v):
            with v.Fori(0, NG) as g:
                for u in range(TG):
                    t = g * TG + u
                    v.wait_ge(s_got[u], g * 32 + 32)
                    v.scalar_tensor_tensor(out=c["X"][:, t, :], in0=got[:, 0, u, :], scalar=moe["wt"][:, 0, bass.ds(t, 1)],
                                           in1=c["ACC"][:, t, 0:D], op0=ALU.mult, op1=ALU.add).then_inc(s_sum, 1)
                    v.wait_ge(s_sum, t * 2 + 1)
                    v.scalar_tensor_tensor(out=c["X"][:, t, :], in0=got[:, 1, u, :], scalar=moe["wt"][:, 1, bass.ds(t, 1)],
                                           in1=c["X"][:, t, :], op0=ALU.mult, op1=ALU.add).then_inc(s_sum, 1)
                v.wait_ge(s_sum, g * (2 * TG) + 2 * TG)
                settle(v)
                moments(v, b, q, g, lambda u: c["X"][:, g * TG + u, :])
                for u in range(TG):
                    v.wait_ge(q["M"], g * TG + 1)
                    v.tensor_scalar(xin[:, u, :], c["X"][:, g * TG + u, :], mv[:, u, 0:1], rs[:, u:u + 1],
                                    ALU.subtract, ALU.mult).then_inc(q["xin"], 1)


def layers_apart(nc, dram, c, b, q):
    z, vec, mv, rs = b["z"], b["vec"], b["mv"], b["rs"]
    r = c["ring"]
    with nc.Block() as block:
        @block.sync
        def _(sp):
            with sp.Fori(1, LAYERS) as l:
                nodes_sync(sp, dram, c, q, l)
            sp.wait_ge(q["tab"], 16 * NG * LAYERS)

        @block.gpsimd
        def _(g):
            with g.Fori(0, LAYERS) as l:
                g.wait_ge(q["tab"], l * (16 * NG) + 16 * NG)
                settle(g)
                steps_pool(nc, c, r, g, l + 1, dram["table"])

        @block.tensor
        def _(pe):
            with pe.Fori(1, LAYERS) as l:
                steps_tensor(nc, c, r, pe, b["pS"], D, l)
                nodes_tensor(pe, c, b, q, l)
            steps_tensor(nc, c, r, pe, b["pS"], D, LAYERS)

        @block.scalar
        def _(act):
            with act.Fori(1, LAYERS) as l:
                nodes_scalar(act, c, b, q, l)
            with act.Fori(0, NG) as g:
                act.wait_ge(q["mv"], LAYERS * NT + g * TG + TG)
                act.activation(b["sd"][:, :], mv[:, :, 1], ACT.Sqrt, bias=c["eps"][:, 0:1]).then_inc(q["sd"], 1)

        @block.vector
        def _(v):
            def row(k, l):
                return vec[:, k, bass.ds(l, 1), :].rearrange("p o d -> p (o d)")

            def epilogue(l, g):
                n = l * NG + g
                for u in range(TG):
                    t = g * TG + u
                    v.scalar_tensor_tensor(out=z[:, u, :], in0=c["ACC"][:, t, 0:D], scalar=c["dinv"][:, bass.ds(t, 1)],
                                           in1=row(0, l), op0=ALU.mult, op1=ALU.add).then_inc(q["z"], 1)
                v.wait_ge(q["z"], n * TG + TG)
                moments(v, b, q, n + NG, lambda u: z[:, u, :])
                for u in range(TG):
                    v.scalar_tensor_tensor(out=z[:, u, :], in0=z[:, u, :], scalar=mv[:, u, 0:1], in1=row(1, l),
                                           op0=ALU.subtract, op1=ALU.mult).then_inc(q["z2"], 1)
                for u in range(TG):
                    v.wait_ge(q["z2"], n * TG + u + 1)
                    v.scalar_tensor_tensor(out=z[:, u, :], in0=z[:, u, :], scalar=rs[:, u:u + 1], in1=row(2, l),
                                           op0=ALU.mult, op1=ALU.add).then_inc(q["z3"], 1)

            with v.Fori(1, LAYERS) as l:
                steps_vector(nc, c, r, v, b["pS"], D, l)
                v.wait_ge(r["s_add"], (l + 1) * STEPS + OH)
                settle(v)
                with v.Fori(0, NG) as g:
                    v.wait_ge(q["xin"], l * NT + g * TG)
                    epilogue(l - 1, g)
            steps_vector(nc, c, r, v, b["pS"], D, LAYERS)
            v.wait_ge(r["s_add"], (LAYERS + 1) * STEPS + OH)
            with v.Fori(0, NG) as g:
                epilogue(LAYERS - 1, g)
                v.wait_ge(q["z3"], (LAYERS - 1) * NT + g * TG + TG)
                for u in range(TG):
                    t = g * TG + u
                    v.scalar_tensor_tensor(out=c["X"][:, t, :], in0=z[:, u, :], scalar=0.0, in1=c["X"][:, t, :],
                                           op0=ALU.max, op1=ALU.add).then_inc(q["zz"], 1)
                v.wait_ge(q["zz"], g * TG + TG)


def layers_overlapped(nc, dram, c, b, q):
    z, vec, xin, xt, stat, mv, sd, rs = (b[k] for k in ("z", "vec", "xin", "xt", "stat", "mv", "sd", "rs"))
    pT, pM = b["pT"], b["pM"]
    r = c["ring"]
    tables = [dram["table"], dram["table1"], dram["table2"]]

    def batch(i):
        if i is None:
            return NT - TAIL, TAIL, BATCHES - 1
        return i * TPB - LAG * TPB, TPB, i - LAG

    def dinv(t):
        return c["dinv"][:, t:t + 1] if isinstance(t, int) else c["dinv"][:, bass.ds(t, 1)]

    with nc.Block() as block:
        @block.sync
        def _(sp):
            for l in range(1, LAYERS):
                table = tables[l].rearrange("(t p) d -> p t d", p=P)

                def store(i):
                    t, n, _ = batch(i)
                    sp.wait_ge(q["h"], t + (l * NT + n))
                    sp.dma_start(table[:, bass.ds(t, n), :], c["ACC"][:, bass.ds(t, n), 0:D]).then_inc(q["tab"], 16)

                with sp.Fori(LAG, NB) as i:
                    store(i)
                store(None)
            sp.wait_ge(q["tab"], 16 * NG + 16 * BATCHES * (LAYERS - 1))

        @block.gpsimd
        def _(g):
            for l in range(1, LAYERS + 1):
                g.wait_ge(q["tab"], 16 * NG + 16 * BATCHES * (l - 1))
                steps_pool(nc, c, r, g, l, tables[l - 1])

        @block.tensor
        def _(pe):
            def turns(l, i):
                t, n, _ = batch(i)
                for k in range(n):
                    pe.wait_ge(q["xin"], t + (l * NT + k + 1))
                    pe.wait_ge(q["xt"], t + (l * NT if k < 2 else l * NT + k - 1))
                    for a in range(KD):
                        mm = pe.transpose(pT[k % 2][:, a * P:(a + 1) * P], xin[:, k, a * P:(a + 1) * P], c["ident"][:, :])
                    mm.then_inc(q["T"], 1)

            def products(l, i):
                t, n, _ = batch(i)
                for k in range(n):
                    pe.wait_ge(q["xt"], t + (l * NT + k + 1))
                    pe.wait_ge(q["h"], t + (l * NT if k < 2 else l * NT + k - 1))
                    for a in range(KD):
                        mm = pe.matmul(pM[k % 2][:, 0:D], xt[:, k, a * P:(a + 1) * P], b["w"][:, l, a, :],
                                       start=(a == 0), stop=(a == KD - 1))
                    mm.then_inc(q["M"], 1)

            for l in range(1, LAYERS + 1):
                def between(i, u):
                    if u == 14:
                        turns(l, i)
                    if u == 18:
                        products(l, i)

                steps_tensor(nc, c, r, pe, b["pS"], D, l, (0, LAG))
                steps_tensor(nc, c, r, pe, b["pS"], D, l, (LAG, NB), between if l < LAYERS else None)
                if l < LAYERS:
                    turns(l, None)
                    products(l, None)

        @block.scalar
        def _(act):
            def batch_scalar(l, i):
                t, n, j = batch(i)
                act.wait_ge(q["mv"], t + (l * NT + n))
                act.activation(sd[:, 0:n], mv[:, 0:n, 1], ACT.Sqrt, bias=c["eps"][:, 0:1]).then_inc(q["sd"], 1)
                if l == LAYERS:
                    return
                for k in range(n):
                    act.wait_ge(q["z3"], t + ((l - 1) * NT + k + 1))
                    act.activation(xin[:, k, :], z[:, k, :], ACT.Relu).then_inc(q["xin"], 1)
                for k in range(n):
                    act.wait_ge(q["T"], t + (l * NT + k + 1))
                    act.activation(xt[:, k, :], pT[k % 2][:, 0:D], ACT.Copy).then_inc(q["xt"], 1)
                for k in range(n):
                    act.wait_ge(q["M"], t + (l * NT + k + 2))
                    settle(act)
                    act.activation(c["ACC"][:, t + k, 0:D], pM[k % 2][:, 0:D], ACT.Copy,
                                   scale=dinv(t + k)).then_inc(q["h"], 1)

            for l in range(1, LAYERS + 1):
                with act.Fori(LAG, NB) as i:
                    batch_scalar(l, i)
                batch_scalar(l, None)

        @block.vector
        def _(v):
            def row(k, l):
                return vec[:, k, l - 1, :]

            def sums(l, i):
                t, n, _ = batch(i)
                if l < LAYERS:
                    v.wait_ge(q["xin"], t + l * NT)
                for k in range(n):
                    v.scalar_tensor_tensor(out=z[:, k, :], in0=c["ACC"][:, t + k, 0:D], scalar=dinv(t + k),
                                           in1=row(0, l), op0=ALU.mult, op1=ALU.add).then_inc(q["z"], 1)

            def stats(l, i):
                t, n, _ = batch(i)
                v.wait_ge(q["z"], t + ((l - 1) * NT + n))
                for k in range(n):
                    v.bn_stats(stat[:, k, :], z[:, k, :]).then_inc(q["stat"], 1)

            def aggregates(l, i):
                t, n, _ = batch(i)
                v.wait_ge(q["stat"], t + (l * NT + n))
                settle(v)
                for k in range(n):
                    v.bn_aggr(mv[:, k, :], stat[:, k, :]).then_inc(q["mv"], 1)

            def deviations(l, i):
                _, n, j = batch(i)
                v.wait_ge(q["sd"], j + (NG + (l - 1) * BATCHES + 1))
                v.reciprocal(rs[:, 0:n], sd[:, 0:n]).then_inc(q["rs"], 1)

            def gains(l, i):
                _, n, j = batch(i)
                for k in range(n):
                    v.scalar_tensor_tensor(out=z[:, k, :], in0=z[:, k, :], scalar=mv[:, k, 0:1], in1=row(1, l),
                                           op0=ALU.subtract, op1=ALU.mult).then_inc(q["z2"], 1)

            def shifts(l, i):
                t, n, j = batch(i)
                v.wait_ge(q["rs"], j + (NG + (l - 1) * BATCHES + 1))
                v.wait_ge(q["z2"], t + ((l - 1) * NT + n))
                for k in range(n):
                    v.scalar_tensor_tensor(out=z[:, k, :], in0=z[:, k, :], scalar=rs[:, k:k + 1], in1=row(2, l),
                                           op0=ALU.mult, op1=ALU.add).then_inc(q["z3"], 1)

            def results(l, i):
                t, n, _ = batch(i)
                if l < LAYERS:
                    return
                v.wait_ge(q["z3"], t + ((l - 1) * NT + n))
                for k in range(n):
                    v.scalar_tensor_tensor(out=c["X"][:, t + k, :], in0=z[:, k, :], scalar=0.0, in1=c["X"][:, t + k, :],
                                           op0=ALU.max, op1=ALU.add).then_inc(q["zz"], 1)

            for l in range(1, LAYERS + 1):
                def between(i, u):
                    if u == 0:
                        sums(l, i)
                    elif u == 1:
                        stats(l, i)
                    elif u == 2:
                        aggregates(l, i)
                    elif u == 5:
                        deviations(l, i)
                    elif u == 6:
                        gains(l, i)
                    elif u == 7:
                        shifts(l, i)
                    elif u == 9:
                        results(l, i)

                steps_vector(nc, c, r, v, b["pS"], D, l, (0, LAG))
                steps_vector(nc, c, r, v, b["pS"], D, l, (LAG, NB), between)
                v.wait_ge(r["s_add"], (l + 1) * STEPS + OH)
                if l == LAYERS:
                    v.wait_ge(q["zz"], NT - TAIL)
                for stage in (sums, stats, aggregates, deviations, gains, shifts, results):
                    stage(l, None)


def slices(nc, ins, out, c, sb, pb, sem):
    with ExitStack() as ctx:
        wc = sb("wc", [P, KD, HEADS * GS], F32, ctx)
        bc = sb("bc", [P, HEADS * GS], F32, ctx)
        SWT = sb("SWT", [P, NT, HEADS * GS], F32, ctx)
        mo = sb("mo", [P, PAIRS, D], F32, ctx)
        diag = sb("diag", [P, 4, P], F32, ctx)
        sums = sb("sums", [P, PAIRS, AW], F32, ctx)
        fold_weights(nc, ins, c, wc, bc, diag, sb, pb, sem)
        slice_nodes(nc, c, wc, bc, SWT, sums, sb, pb, sem)
        attend(nc, ins, c, diag, sums, mo, sb, pb, sem)
        project(nc, ins, out, c, SWT, mo, sb, pb, sem)


def fold_weights(nc, ins, c, wc, bc, diag, sb, pb, sem):
    with ExitStack() as ctx:
        wx = sb("wx_f", [P, KD, HEADS * DH], F32, ctx)
        wxt = sb("wxt_f", [P, KD, PAIRS, P], F32, ctx)
        bx = sb("bx_f", [P, PAIRS], F32, ctx)
        bxb = sb("bxb_f", [P, PAIRS, P], F32, ctx)
        bs = sb("bs_f", [P, GS], F32, ctx)
        tp = sb("tp_f", [P, HEADS], F32, ctx)
        rt = sb("rt_f", [P, HEADS], F32, ctx)
        pT = [pb(f"pT_f{k}", ctx) for k in range(KD)]
        pW = [pb(f"pW_f{k}", ctx) for k in range(KD)]
        pB = pb("pB_f", ctx)
        s_zero, s_in, s_xt, s_T, s_mm, s_v = (sem("f_zero"), sem("f_in"), sem("f_xt"), sem("f_T"), sem("f_mm"), sem("f_v"))
        s_mask = sem("f_mask")
        NIN = 2 * 4 + 4
        block = ctx.enter_context(nc.Block())

        @block.sync
        def _(sp):
            sp.wait_ge(s_zero, 1)
            for n, name in enumerate(("L1_ffn_W_slice", "L1_ffn_W_q", "L1_ffn_W_k", "L1_ffn_W_v")):
                for a in range(2):
                    sp.dma_start(diag[a * DH:(a + 1) * DH, n, a * DH:(a + 1) * DH], ins[name]).then_inc(s_in, 16)
            sp.dma_start(wx[:, :, :], ins["L1_ffn_W_x"].rearrange("(k p) n -> p k n", p=P)).then_inc(s_in, 16)
            sp.dma_start(bx[:, :], ins["L1_ffn_b_x"].rearrange("(a p) -> p a", p=P), allow_slow_non_contiguous=True).then_inc(s_in, 16)
            sp.dma_start(bs[:, :], ins["L1_ffn_b_slice"].rearrange("(o g) -> o g", o=1).to_broadcast([P, GS])).then_inc(s_in, 16)
            sp.dma_start(tp[:, :], ins["L1_ffn_temperature"].rearrange("o h a b -> o (h a b)").to_broadcast([P, HEADS])).then_inc(s_in, 16)

        @block.gpsimd
        def _(g):
            nc.gpsimd.affine_select(out=c["X"][:, NT - 1, :], in_=c["X"][:, NT - 1, :], compare_op=ALU.is_ge,
                                    fill=0.0, base=LAST - 1, pattern=[[0, D]], channel_multiplier=-1).then_inc(s_mask, 1)

        @block.vector
        def _(v):
            v.memset(diag[:, :, :], 0.0).then_inc(s_zero, 1)
            v.wait_ge(s_in, 16 * NIN)
            for a in range(PAIRS):
                ins_ = v.tensor_copy(bxb[:, a, :], bx[:, a:a + 1].to_broadcast([P, P]))
            ins_.then_inc(s_v, 1)
            v.tensor_scalar(tp[:, :], tp[:, :], 0.1, 5.0, ALU.max, ALU.min).then_inc(s_v, 1)
            v.wait_ge(s_v, 2)
            v.reciprocal(rt[:, :], tp[:, :]).then_inc(s_v, 1)
            for k in range(KD):
                v.wait_ge(s_T, k + 1)
                v.tensor_copy(wxt[:, k, :, :].rearrange("p a n -> p (a n)"), pT[k][:, :]).then_inc(s_xt, 1)
            v.wait_ge(s_v, 3)
            v.wait_ge(s_mm, KD + 1)
            for h in range(HEADS):
                cols = slice(h * GS, (h + 1) * GS)
                for k in range(KD):
                    v.tensor_scalar(wc[:, k, cols], pW[k][:, cols], rt[:, h:h + 1], None, ALU.mult)
                ins_ = v.tensor_tensor(bc[:, cols], pB[:, cols], bs[:, :], ALU.add)
            ins_.then_inc(s_v, 1)
            v.wait_ge(s_v, 4)
            for h in range(HEADS):
                cols = slice(h * GS, (h + 1) * GS)
                v.tensor_scalar(bc[:, cols], bc[:, cols], rt[:, h:h + 1], None, ALU.mult)

        @block.tensor
        def _(pe):
            pe.wait_ge(s_in, 16 * NIN)
            for k in range(KD):
                for a in range(PAIRS):
                    mm = pe.transpose(pT[k][:, a * P:(a + 1) * P], wx[:, k, a * P:(a + 1) * P], c["ident"][:, :])
                mm.then_inc(s_T, 1)
            for k in range(KD):
                pe.wait_ge(s_xt, k + 1)
                for a in range(PAIRS):
                    mm = pe.matmul(pW[k][:, a * P:(a + 1) * P], wxt[:, k, a, :], diag[:, 0, :], start=True, stop=True)
                mm.then_inc(s_mm, 1)
            pe.wait_ge(s_v, 1)
            for a in range(PAIRS):
                mm = pe.matmul(pB[:, a * P:(a + 1) * P], bxb[:, a, :], diag[:, 0, :], start=True, stop=True)
            mm.then_inc(s_mm, 1)


def slice_nodes(nc, c, wc, bc, SWT, sums, sb, pb, sem):
    SW = HEADS * GS
    RS = 3
    with ExitStack() as ctx:
        un = sb("un_s", [P, TG, AW], F32, ctx)
        ut = sb("ut_s", [P, 2, D], F32, ctx)
        z = sb("z_s", [P, RS, SW], F32, ctx)
        sw = sb("sw_s", [P, RS, SW], F32, ctx)
        red = sb("red_s", [P, RS, 3, HEADS], F32, ctx)
        zero = sb("zero_s", [P, AW], F32, ctx)
        stat = sb("stat_s", [P, TG, 6], F32, ctx)
        mv = sb("mv_s", [P, TG, 2], F32, ctx)
        sd = sb("sd_s", [P, TG], F32, ctx)
        rs = sb("rs_s", [P, TG], F32, ctx)
        s_stat, s_mv, s_sd, s_rs, s_un = sem("s_stat"), sem("s_mv"), sem("s_sd"), sem("s_rs"), sem("s_un")
        s_T, s_ut, s_L, s_z, s_max, s_sub, s_exp = (sem("s_T"), sem("s_ut"), sem("s_L"), sem("s_z"), sem("s_max"),
                                                    sem("s_sub"), sem("s_exp"))
        s_sum, s_inv, s_sw, s_W, s_swt, s_S, s_zero, s_end = (sem("s_sum"), sem("s_inv"), sem("s_sw"), sem("s_W"),
                                                              sem("s_swt"), sem("s_S"), sem("s_zero"), sem("s_end"))
        pT = pb("pT_s", ctx)
        pL = [pb(f"pL_s{k}", ctx) for k in range(2)]
        pW = pb("pW_s", ctx)
        pS = [pb(f"pS_s{k}", ctx) for k in range(PAIRS)]
        block = ctx.enter_context(nc.Block())

        def heads(ap):
            return ap.rearrange("p (h g) -> p h g", h=HEADS)

        @block.vector
        def _(v):
            v.memset(zero[:, :], 0.0).then_inc(s_zero, 1)
            v.memset(z[:, :, :], 0.0).then_inc(s_z, 1)

            def logits(g, u):
                t = g * TG + u
                x = u % RS
                v.wait_ge(s_L, t + 1)
                v.tensor_tensor(z[:, x, :], pL[u % 2][:, :], bc[:, :], ALU.add).then_inc(s_z, 1)
                v.wait_ge(s_z, t + 2)
                v.tensor_reduce(red[:, x, 0, :], heads(z[:, x, :]), AX.X, ALU.max).then_inc(s_max, 1)
                v.wait_ge(s_max, t + 1)
                v.tensor_tensor(heads(z[:, x, :]), heads(z[:, x, :]),
                                red[:, x, 0, :].rearrange("p (h o) -> p h o", o=1).to_broadcast([P, HEADS, GS]),
                                ALU.subtract).then_inc(s_sub, 1)

            def weights(g, u):
                t = g * TG + u
                x = u % RS
                v.wait_ge(s_exp, t + 1)
                v.tensor_reduce(red[:, x, 1, :], heads(z[:, x, :]), AX.X, ALU.add).then_inc(s_sum, 1)
                v.wait_ge(s_sum, t + 1)
                v.reciprocal(red[:, x, 2, :], red[:, x, 1, :]).then_inc(s_inv, 1)
                if u == 0:
                    v.wait_ge(s_S, t + 1)
                if u >= RS:
                    v.wait_ge(s_S, t - RS + 2)
                v.wait_ge(s_inv, t + 1)
                v.tensor_tensor(heads(sw[:, x, :]), heads(z[:, x, :]),
                                red[:, x, 2, :].rearrange("p (h o) -> p h o", o=1).to_broadcast([P, HEADS, GS]),
                                ALU.mult).then_inc(s_sw, 1)

            with v.Fori(0, NG) as g:
                for u in range(TG):
                    v.bn_stats(stat[:, u, :], c["X"][:, g * TG + u, :]).then_inc(s_stat, 1)
                v.wait_ge(s_stat, g * TG + TG)
                settle(v)
                for u in range(TG):
                    v.bn_aggr(mv[:, u, :], stat[:, u, :]).then_inc(s_mv, 1)
                v.wait_ge(s_sd, g + 1)
                v.reciprocal(rs[:, :], sd[:, :]).then_inc(s_rs, 1)
                v.wait_ge(s_rs, g + 1)
                v.wait_ge(s_S, g * TG + 1)
                v.tensor_copy(un[:, :, D:AW].rearrange("p u o -> p (u o)"), c["valid"][:, bass.ds(g * TG, TG)])
                for u in range(TG):
                    v.tensor_scalar(un[:, u, 0:D], c["X"][:, g * TG + u, :], mv[:, u, 0:1], rs[:, u:u + 1],
                                    ALU.subtract, ALU.mult).then_inc(s_un, 1)
                logits(g, 0)
                for u in range(TG):
                    if u + 1 < TG:
                        logits(g, u + 1)
                    weights(g, u)
            v.wait_ge(s_end, 1)
            for a in range(PAIRS):
                v.tensor_copy(sums[:, a, :], pS[a][:, 0:AW])

        @block.scalar
        def _(act):
            with act.Fori(0, NG) as g:
                act.wait_ge(s_mv, g * TG + TG)
                act.activation(sd[:, :], mv[:, :, 1], ACT.Sqrt, bias=c["eps"][:, 0:1]).then_inc(s_sd, 1)
                for k in range(TG + 4):
                    if k < TG:
                        act.wait_ge(s_T, g * TG + k + 1)
                        act.activation(ut[:, k % 2, :], pT[:, 0:D], ACT.Copy).then_inc(s_ut, 1)
                    if 0 <= k - 2 < TG:
                        act.wait_ge(s_sub, g * TG + k - 2 + 1)
                        act.activation(z[:, (k - 2) % RS, :], z[:, (k - 2) % RS, :], ACT.Exp).then_inc(s_exp, 1)
                    if 0 <= k - 4 < TG:
                        t = g * TG + k - 4
                        act.wait_ge(s_W, t + 1)
                        settle(act)
                        act.activation(SWT[:, t, :], pW[:, :], ACT.Copy).then_inc(s_swt, 1)

        @block.tensor
        def _(pe):
            pe.wait_ge(s_zero, 1)
            for a in range(PAIRS):
                mm = pe.matmul(pS[a][:, 0:AW], zero[:, 0:P], zero[:, :], start=True, stop=False, skip_group_check=True)
            mm.then_inc(s_S, 1)
            with pe.Fori(0, NG) as g:
                for k in range(TG + 3):
                    if k < TG:
                        t = g * TG + k
                        pe.wait_ge(s_un, t + 1)
                        if k >= 1:
                            pe.wait_ge(s_ut, t)
                        for n in range(KD):
                            mm = pe.transpose(pT[:, n * P:(n + 1) * P], un[:, k, n * P:(n + 1) * P], c["ident"][:, :])
                        mm.then_inc(s_T, 1)
                    if 0 <= k - 1 < TG:
                        u = k - 1
                        t = g * TG + u
                        pe.wait_ge(s_ut, t + 1)
                        if u == 0:
                            pe.wait_ge(s_z, t + 1)
                        if u >= 2:
                            pe.wait_ge(s_z, t)
                        for n in range(KD):
                            mm = pe.matmul(pL[u % 2][:, :], ut[:, u % 2, n * P:(n + 1) * P], wc[:, n, :],
                                           start=(n == 0), stop=(n == KD - 1))
                        mm.then_inc(s_L, 1)
                    if 0 <= k - 3 < TG:
                        u = k - 3
                        t = g * TG + u
                        pe.wait_ge(s_sw, t + 1)
                        if u >= 1:
                            pe.wait_ge(s_swt, t)
                        for a in range(PAIRS):
                            mm = pe.transpose(pW[:, a * P:(a + 1) * P], sw[:, u % RS, a * P:(a + 1) * P], c["ident"][:, :])
                        mm.then_inc(s_W, 1)
                        for a in range(PAIRS):
                            mm = pe.matmul(pS[a][:, 0:AW], sw[:, u % RS, a * P:(a + 1) * P], un[:, u, :],
                                           start=False, stop=False, skip_group_check=True)
                        mm.then_inc(s_S, 1)
            for a in range(PAIRS):
                mm = pe.matmul(pS[a][:, 0:AW], zero[:, 0:P], zero[:, :], start=False, stop=True, skip_group_check=True)
            mm.then_inc(s_end, 1)


def attend(nc, ins, c, diag, sums, mo, sb, pb, sem):
    with ExitStack() as ctx:
        wfx = sb("wfx_t", [P, KD, HEADS * DH], F32, ctx)
        bfx = sb("bfx_t", [P, HEADS * DH], F32, ctx)
        wo = sb("wo_t", [P, PAIRS, D], F32, ctx)
        st = sb("st_t", [P, KD, PAIRS, P], F32, ctx)
        inv = sb("inv_t", [P, 2, PAIRS], F32, ctx)
        tok = sb("tok_t", [P, PAIRS, P], F32, ctx)
        tokT = sb("tokT_t", [P, PAIRS, P], F32, ctx)
        qT = sb("qT_t", [P, PAIRS, P], F32, ctx)
        kT = sb("kT_t", [P, PAIRS, P], F32, ctx)
        vv = sb("vv_t", [P, PAIRS, P], F32, ctx)
        sc = sb("sc_t", [P, PAIRS, DH], F32, ctx)
        red = sb("red_t", [P, 3, PAIRS], F32, ctx)
        at = sb("at_t", [P, PAIRS, P], F32, ctx)
        atT = sb("atT_t", [P, PAIRS, P], F32, ctx)
        oT = sb("oT_t", [P, PAIRS, P], F32, ctx)
        bank = [pb(f"bank_t{k}", ctx) for k in range(8)]
        s_in, s_pe, s_v, s_exp = sem("t_in"), sem("t_pe"), sem("t_v"), sem("t_exp")
        block = ctx.enter_context(nc.Block())
        HALVES = [slice(0, DH), slice(DH, 2 * DH)]

        def flat(x):
            return x[:, :, :].rearrange("p a n -> p (a n)")

        @block.sync
        def _(sp):
            sp.dma_start(wfx[:, :, :], ins["L1_ffn_W_fx"].rearrange("(k p) n -> p k n", p=P)).then_inc(s_in, 16)
            sp.dma_start(bfx[:, :], ins["L1_ffn_b_fx"].rearrange("(o n) -> o n", o=1).to_broadcast([P, HEADS * DH])).then_inc(s_in, 16)
            sp.dma_start(wo[:, :, :], ins["L1_ffn_W_out"].rearrange("(a p) d -> p a d", p=P)).then_inc(s_in, 16)

        @block.tensor
        def _(pe):
            def done(n, fn):
                pe.wait_ge(s_v, n)
                for a in range(PAIRS):
                    mm = fn(a)
                mm.then_inc(s_pe, 1)

            pe.wait_ge(s_in, 48)
            cols = [slice(a * P, (a + 1) * P) for a in range(PAIRS)]
            for k in range(KD):
                for a in range(PAIRS):
                    mm = pe.transpose(bank[k][:, cols[a]], sums[:, a, k * P:(k + 1) * P], c["ident"][:, :])
            mm.then_inc(s_pe, 1)

            def tokens(a):
                for k in range(KD):
                    mm = pe.matmul(bank[2][:, cols[a]], st[:, k, a, :], wfx[:, k, cols[a]], start=(k == 0), stop=(k == KD - 1))
                return mm
            done(1, tokens)
            done(2, lambda a: pe.transpose(bank[3][:, cols[a]], tok[:, a, :], c["ident"][:, :]))

            def qkv(a):
                pe.matmul(bank[4][:, cols[a]], diag[:, 1, :], tokT[:, a, :], start=True, stop=True)
                pe.matmul(bank[5][:, cols[a]], diag[:, 2, :], tokT[:, a, :], start=True, stop=True)
                return pe.matmul(bank[6][:, cols[a]], tokT[:, a, :], diag[:, 3, :], start=True, stop=True)
            done(3, qkv)
            done(4, lambda a: pe.matmul(bank[7][:, cols[a]], qT[:, a, :], kT[:, a, :], start=True, stop=True))
            done(5, lambda a: pe.transpose(bank[0][:, cols[a]], at[:, a, :], c["ident"][:, :]))
            done(6, lambda a: pe.matmul(bank[1][:, cols[a]], vv[:, a, :], atT[:, a, :], start=True, stop=True))
            done(7, lambda a: pe.matmul(bank[2 + a // 2][:, (a % 2) * D:(a % 2 + 1) * D], oT[:, a, :], wo[:, a, :], start=True, stop=True))

        @block.scalar
        def _(act):
            act.wait_ge(s_exp, 1)
            act.activation(sc[:, :, :], sc[:, :, :], ACT.Exp).then_inc(s_exp, 1)

        @block.vector
        def _(v):
            s_c = sem("t_chain")
            n = [0]

            def then(i):
                i.then_inc(s_c, 1)
                n[0] += 1
                v.wait_ge(s_c, n[0])

            v.memset(tok[:, :, :], 0.0)
            v.memset(at[:, :, :], 0.0)
            v.tensor_scalar(inv[:, 0, :], sums[:, :, D], 1e-5, None, ALU.add)
            v.wait_ge(s_in, 48)
            v.wait_ge(s_pe, 1)
            v.tensor_copy(st[:, 0, :, :].rearrange("p a n -> p (a n)"), bank[0][:, :])
            then(v.tensor_copy(st[:, 1, :, :].rearrange("p a n -> p (a n)"), bank[1][:, :]))
            then(v.reciprocal(inv[:, 1, :], inv[:, 0, :]))
            v.memset(red[:, :, :], 0.0).then_inc(s_v, 1)
            v.wait_ge(s_pe, 2)
            for a in range(PAIRS):
                for x in range(2):
                    hs = slice(a * P + x * DH, a * P + (x + 1) * DH)
                    i = v.scalar_tensor_tensor(out=tok[HALVES[x], a, HALVES[x]], in0=bfx[HALVES[x], hs], scalar=sums[HALVES[x], a, D:AW],
                                               in1=bank[2][HALVES[x], hs], op0=ALU.mult, op1=ALU.add)
            then(i)
            for a in range(PAIRS):
                i = v.tensor_scalar(tok[:, a, :], tok[:, a, :], inv[:, 1, a:a + 1], None, ALU.mult)
            i.then_inc(s_v, 1)
            v.wait_ge(s_pe, 3)
            v.tensor_copy(flat(tokT), bank[3][:, :]).then_inc(s_v, 1)
            v.wait_ge(s_pe, 4)
            v.tensor_copy(flat(qT), bank[4][:, :])
            v.tensor_copy(flat(kT), bank[5][:, :])
            v.tensor_copy(flat(vv), bank[6][:, :]).then_inc(s_v, 1)
            v.wait_ge(s_pe, 5)
            for a in range(PAIRS):
                for x in range(2):
                    i = v.tensor_scalar(sc[HALVES[x], a, :], bank[7][HALVES[x], a * P + x * DH:a * P + (x + 1) * DH],
                                        float(DH) ** -0.5, None, ALU.mult)
            then(i)
            then(v.tensor_reduce(red[:, 0, :], sc[:, :, :], AX.X, ALU.max))

            def wide(k):
                return red[:, k, :].rearrange("p (a o) -> p a o", o=1).to_broadcast([P, PAIRS, DH])
            v.tensor_tensor(sc[:, :, :], sc[:, :, :], wide(0), ALU.subtract).then_inc(s_exp, 1)
            v.wait_ge(s_exp, 2)
            then(v.tensor_reduce(red[:, 1, :], sc[:, :, :], AX.X, ALU.add))
            then(v.reciprocal(red[:, 2, :], red[:, 1, :]))
            for x in range(2):
                i = v.tensor_tensor(at[HALVES[x], :, HALVES[x]], sc[HALVES[x], :, :],
                                    red[HALVES[x], 2, :].rearrange("p (a o) -> p a o", o=1).to_broadcast([DH, PAIRS, DH]), ALU.mult)
            i.then_inc(s_v, 1)
            v.wait_ge(s_pe, 6)
            v.tensor_copy(flat(atT), bank[0][:, :]).then_inc(s_v, 1)
            v.wait_ge(s_pe, 7)
            v.tensor_copy(flat(oT), bank[1][:, :]).then_inc(s_v, 1)
            v.wait_ge(s_pe, 8)
            for a in range(PAIRS):
                v.tensor_copy(mo[:, a, :], bank[2 + a // 2][:, (a % 2) * D:(a % 2 + 1) * D])


def project(nc, ins, out, c, SWT, mo, sb, pb, sem):
    with ExitStack() as ctx:
        bo = sb("bo_o", [P, D], F32, ctx)
        wt = sb("wt_o", [P, TG, HEADS * GS], F32, ctx)
        pO = [pb(f"pO_o{k}", ctx) for k in range(TG)]
        s_in, s_wt, s_b, s_mm, s_x, s_out = sem("o_in"), sem("o_wt"), sem("o_b"), sem("o_mm"), sem("o_x"), sem("o_out")
        block = ctx.enter_context(nc.Block())

        @block.sync
        def _(sp):
            sp.dma_start(bo[:, :], ins["L1_ffn_b_out"].rearrange("(o d) -> o d", o=1).to_broadcast([P, D])).then_inc(s_in, 16)
            rows = out[0:(NT - 1) * P, :].rearrange("(t p) d -> p t d", p=P)
            with sp.Fori(0, NG - 1) as g:
                sp.wait_ge(s_x, g * TG + TG)
                sp.dma_start(rows[:, bass.ds(g * TG, TG), :], c["X"][:, bass.ds(g * TG, TG), :]).then_inc(s_out, 16)
            sp.wait_ge(s_x, NT)
            sp.dma_start(rows[:, (NG - 1) * TG:NT - 1, :], c["X"][:, (NG - 1) * TG:NT - 1, :]).then_inc(s_out, 16)
            sp.dma_start(out[(NT - 1) * P:N, :], c["X"][0:LAST, NT - 1, :]).then_inc(s_out, 16)
            sp.wait_ge(s_out, 16 * (NG + 1))

        @block.scalar
        def _(act):
            def body(g):
                for u in range(TG):
                    wait(act, s_mm, (g - 1) * TG + u + 1)
                    if not isinstance(g, int):
                        settle(act)
                    act.activation(wt[:, u, :], SWT[:, g * TG + u, :], ACT.Copy).then_inc(s_wt, 1)
            body(0)
            with act.Fori(1, NG) as g:
                body(g)

        @block.tensor
        def _(pe):
            def body(g):
                for u in range(TG):
                    t = g * TG + u
                    pe.wait_ge(s_wt, t + 1)
                    wait(pe, s_x, t - TG + 1)
                    for a in range(PAIRS):
                        mm = pe.matmul(pO[u][:, 0:D], wt[:, u, a * P:(a + 1) * P], mo[:, a, :], start=(a == 0), stop=(a == PAIRS - 1))
                    mm.then_inc(s_mm, 1)
            body(0)
            with pe.Fori(1, NG) as g:
                body(g)

        @block.vector
        def _(v):
            v.wait_ge(s_in, 16)
            with v.Fori(0, NG) as g:
                for u in range(TG):
                    t = g * TG + u
                    v.tensor_tensor(c["X"][:, t, :], c["X"][:, t, :], bo[:, :], ALU.add).then_inc(s_b, 1)
                for u in range(TG):
                    t = g * TG + u
                    v.wait_ge(s_b, t + 1)
                    v.wait_ge(s_mm, t + 1)
                    v.tensor_tensor(c["X"][:, t, :], pO[u][:, 0:D], c["X"][:, t, :], ALU.add).then_inc(s_x, 1)


_INS = ['x', 'src', 'dst', 'edge_weight', 'L0_gnn_w_nbr', 'L0_gnn_w_own', 'L0_gnn_bias',
        'L0_ffn_Wr', 'L0_ffn_br', 'L0_ffn_ln_g', 'L0_ffn_ln_b', 'L0_ffn_W1', 'L0_ffn_b1', 'L0_ffn_W2', 'L0_ffn_b2',
        'L1_gnn_W', 'L1_gnn_b', 'L1_gnn_gamma', 'L1_gnn_beta', 'L1_ffn_W_fx', 'L1_ffn_b_fx', 'L1_ffn_W_x',
        'L1_ffn_b_x', 'L1_ffn_W_slice', 'L1_ffn_b_slice', 'L1_ffn_W_q', 'L1_ffn_W_k', 'L1_ffn_W_v', 'L1_ffn_W_out',
        'L1_ffn_b_out', 'L1_ffn_temperature']


def kernel(**inputs):
    import numpy as _np
    import concourse.bacc as _bacc
    from concourse import mybir as _mybir
    from concourse.bass_utils import run_bass_kernel_spmd as _run

    nc = _bacc.Bacc("TRN2", target_bir_lowering=False, num_devices=1)
    arrays, ins = {}, {}
    for name in _INS:
        a = _np.ascontiguousarray(inputs[name])
        arrays[f"in_{name}"] = a
        ins[name] = nc.dram_tensor(f"in_{name}", a.shape, _mybir.dt.from_np(a.dtype), kind="ExternalInput").ap()
    out = nc.dram_tensor("out_0", (N, D), _mybir.dt.float32, kind="ExternalOutput").ap()
    dram = {name: nc.dram_tensor(name, (rows, D), _mybir.dt.float32, kind="Internal").ap()
            for name, rows in (("table", NT * P), ("table1", NT * P), ("table2", NT * P), ("disp", SLOTS + BR), ("y", SLOTS + BR))}
    for name, shape, dt in (("src", (E,), I32), ("dst", (E,), I32), ("weight", (E,), F32), ("rec", (P * EF, 4), F32)):
        dram[name] = nc.dram_tensor(f"edges_{name}", shape, dt, kind="Internal").ap()
    build(nc, ins, out, dram)
    r = _run(nc, [arrays], core_ids=[0])
    return r.results[0]["out_0"]
```

```python
from contextlib import ExitStack

import concourse.bass as bass
from concourse import mybir

P = 128
F32 = mybir.dt.float32
I32 = mybir.dt.int32
U32 = mybir.dt.uint32
ALU = mybir.AluOpType
ACT = mybir.ActivationFunctionType
AX = mybir.AxisListType
EPS = 1e-5

N = 6250
D = 256
KD = D // P
NT = -(-N // P)
LAST = N - (NT - 1) * P
TG = 7
NG = NT // TG
E = 100000
ET = -(-E // P)
EC = -(-ET // P)
EF = -(-E // P)
EB = 17
U = 32
NB = -(-(ET + NT - 1) // U)
STEPS = NB * U
HALF = STEPS // 2
R = 16
OH = 4
AHEAD = OH - 1
Q = 4
LOADS = 8
AW = D + 1
FAR = 1 << 27
NE = 8
HID = 1024
HJ = HID // P
BR = 2 * P
NBLK = (2 * N + NE * (BR - 1)) // BR
NBLK += NBLK % 2
SLOTS = NBLK * BR
LAYERS = 3
TPB = 2
LAG = 3
BATCHES = NB - LAG + 1
TAIL = NT - (NB - LAG) * TPB
HEADS = 8
DH = 64
GS = 64
PAIRS = HEADS // 2
PRM = KD + KD + HJ


def build(nc, ins, out, dram):
    with ExitStack() as top:
        def sb(name, shape, dt=F32, ctx=top):
            return ctx.enter_context(nc.sbuf_tensor(name, shape, dt))

        def pb(name, ctx, shape=(P, 512), dt=F32):
            return ctx.enter_context(nc.psum_tensor(name, list(shape), dt))

        def sem(name):
            return top.enter_context(nc.semaphore(name))

        c = dict(ident=sb("ident", [P, P]), eps=sb("eps", [P, 1]), valid=sb("valid", [P, NT]), X=sb("X", [P, NT, D]),
                 mvx=sb("mvx", [P, NT, 2]), rsx=sb("rsx", [P, NT]))
        with ExitStack() as g:
            c.update(
                lane=sb("lane", [P, P], F32, g), ACC=sb("ACC", [P, NT, AW], F32, g),
                ones_row=sb("ones_row", [P, NT], F32, g),
                step_src=sb("step_src", [P, STEPS + R], I32, g), step_dst=sb("step_dst", [P, STEPS + AHEAD], F32, g),
                step_w=sb("step_w", [P, STEPS], F32, g), step_off=sb("step_off", [P, STEPS], I32, g),
                dinv=sb("dinv", [P, NT], F32, g), late=sb("late", [P, 1], I32, g),
                mv=sb("mv", [P, NT, 2], F32, g), rs=sb("rs", [P, NT], F32, g),
            )
            c["ring"] = gather_ring(nc, dram["table"], sb, sem, g)
            moe = dict(
                wt=sb("moe_w", [P, 2, NT], F32, g),
                pos=sb("moe_pos", [P, 2, NT + 1], I32, g),
                inv=sb("moe_inv", [P, 2 * (NBLK + 1)], I32, g),
                now=sem("m_now"),
                expert=sb("moe_expert", [P, NBLK + 1], I32, g), top=sb("moe_top", [P, NT, 2], F32, g),
                idx=sb("moe_idx", [P, NT, 2], U32, g), prm=sb("moe_prm", [P, NE, PRM], F32, g),
            )
            order_edges(nc, ins, dram, sb, pb, sem)
            prepare(nc, ins, dram, c, sb, pb, sem)
            first_layer(nc, ins, dram, c, sb, pb, sem)
            first_steps(nc, ins, dram, c, moe, sb, pb, sem)
            mixture(nc, ins, dram, c, moe, sb, pb, sem)
            convolutions(nc, ins, dram, c, moe, sb, pb, sem)
        slices(nc, ins, out, c, sb, pb, sem)


def order_edges(nc, ins, dram, sb, pb, sem):
    full = P - 1
    rest = E - full * EF
    with ExitStack() as ctx:
        dst_i = sb("dst_o", [P, EF + 1], I32, ctx)
        dst_f = sb("dstf_o", [P, EF + 1], F32, ctx)
        falls = sb("falls", [P, EF], F32, ctx)
        nfalls = sb("nfalls", [P, 1], F32, ctx)
        ones = sb("ones_o", [P, P], F32, ctx)
        flag_i = sb("flag_i", [P, 1], I32, ctx)
        BK = NT + 1
        t = dict(
            src_i=sb("src_o", [P, EF], I32, ctx),
            w_f=sb("w_o", [P, EF], F32, ctx),
            rec=sb("rec_o", [P, EF, 4], F32, ctx),
            bkt_i=sb("bkti_o", [P, EF], I32, ctx),
            bkt=sb("bkt_o", [P, EF], F32, ctx),
            mask=sb("mask_o", [P, EF], F32, ctx),
            run=sb("run_o", [P, EF], F32, ctx),
            one=sb("one_o", [P, EF], F32, ctx),
            pos_f=sb("posf_o", [P, EF], F32, ctx),
            pos_i=sb("posi_o", [P, EF], I32, ctx),
            number=sb("number_o", [P, BK], F32, ctx),
            cnt=sb("cnt_o", [P, BK], F32, ctx),
            tot=sb("tot_o", [P, BK], F32, ctx),
            off=sb("off_o", [P, BK], F32, ctx),
            before=sb("before_o", [P, P], F32, ctx),
            now=sb("now_o", [P, EB], I32, ctx),
            stage=sb("stage_o", [P, EB, 4], F32, ctx),
            pW=pb("pW_o", ctx), pC=pb("pC_o", ctx), dst_i=dst_i, ones=ones,
        )
        s_in, s_v, s_mm = sem("y_in"), sem("y_v"), sem("y_mm")

        def rows(a, t):
            return [(t[0:full, 0:EF], a[0:full * EF].rearrange("(p n) -> p n", p=full)),
                    (t[full:P, 0:rest], a[full * EF:E].rearrange("(p n) -> p n", p=1))]

        with ExitStack() as pc, nc.Block() as block:
            pN = pb("pN_o", pc)

            @block.sync
            def _(sp):
                sp.wait_ge(s_v, 1)
                for t, a in rows(ins["dst"], dst_i):
                    sp.dma_start(t, a).then_inc(s_in, 16)
                sp.dma_start(dst_i[0:full - 1, EF:EF + 1], ins["dst"][EF:full * EF].rearrange("(p n) -> p n", n=EF)[:, 0:1],
                             allow_slow_non_contiguous=True).then_inc(s_in, 16)
                sp.dma_start(dst_i[full - 1:full, EF:EF + 1], ins["dst"][full * EF:full * EF + 1].rearrange("(p n) -> p n", n=1)).then_inc(s_in, 16)

            @block.vector
            def _(v):
                v.memset(dst_i[:, :], NT * P).then_inc(s_v, 1)
                v.memset(ones[:, :], 1.0).then_inc(s_v, 1)
                v.wait_ge(s_in, 64)
                v.tensor_copy(dst_f[:, :], dst_i[:, :]).then_inc(s_v, 1)
                v.wait_ge(s_v, 3)
                v.tensor_tensor(falls[:, :], dst_f[:, 0:EF], dst_f[:, 1:EF + 1], ALU.is_gt).then_inc(s_v, 1)
                v.wait_ge(s_v, 4)
                v.tensor_reduce(nfalls[:, :], falls[:, :], AX.X, ALU.add).then_inc(s_v, 1)
                v.wait_ge(s_mm, 1)
                v.tensor_scalar(flag_i[:, :], pN[:, 0:1], 1.0, None, ALU.min)

            @block.tensor
            def _(pe):
                pe.wait_ge(s_v, 5)
                pe.matmul(pN[:, 0:1], ones[:, :], nfalls[:, :], start=True, stop=True).then_inc(s_mm, 1)

        unsorted = nc.values_load(flag_i[0:1, 0:1], min_val=0, max_val=1,
                                  skip_runtime_bounds_check_because="it is the minimum of 1 and a count")
        with nc.If(unsorted > 0):
            sort_edges(nc, ins, dram, t, rows, sem)
        with nc.Else():
            s_copy = sem("y_copy")
            with nc.Block() as block:
                def copy(eng, name, a):
                    eng.dma_start(dram[name].rearrange("(p n) -> p n", p=80), a.rearrange("(p n) -> p n", p=80)).then_inc(s_copy, 16)

                @block.sync
                def _(sp):
                    copy(sp, "dst", ins["dst"])
                    copy(sp, "src", ins["src"])
                    sp.wait_ge(s_copy, 48)

                @block.scalar
                def _(act):
                    copy(act, "weight", ins["edge_weight"])
                    act.wait_ge(s_copy, 48)


def sort_edges(nc, ins, dram, t, rows, sem):
    BK = NT + 1
    G = EF // EB
    src_i, w_f, rec, bkt_i, bkt, mask, run, one, pos_f = (t[k] for k in (
        "src_i", "w_f", "rec", "bkt_i", "bkt", "mask", "run", "one", "pos_f"))
    pos_i, number, cnt, tot, off, before, now, stage, pW, pC, dst_i, ones = (t[k] for k in (
        "pos_i", "number", "cnt", "tot", "off", "before", "now", "stage", "pW", "pC", "dst_i", "ones"))
    s_c, s_dma, s_v, s_b, s_d = sem("z_c"), sem("z_dma"), sem("z_v"), sem("z_b"), sem("z_d")
    s_cnt, s_mm, s_now, s_put = sem("z_cnt"), sem("z_mm"), sem("z_now"), sem("z_put")
    RECORDS = 9
    with nc.Block() as block:
        @block.sync
        def _(sp):
            sp.wait_ge(s_v, 2)
            for t, a in rows(ins["src"], src_i):
                sp.dma_start(t, a).then_inc(s_dma, 16)

        @block.scalar
        def _(act):
            act.wait_ge(s_v, 2)
            for t, a in rows(ins["edge_weight"], w_f):
                act.dma_start(t, a).then_inc(s_dma, 16)

        @block.gpsimd
        def _(g):
            nc.gpsimd.iota(number[:, :], [[1, BK]], base=0, channel_multiplier=0,
                           allow_small_or_imprecise_dtypes=True).then_inc(s_c, 1)
            nc.gpsimd.affine_select(out=before[:, :], in_=ones[:, :], compare_op=ALU.is_gt, fill=0.0,
                                    base=0, pattern=[[1, P]], channel_multiplier=-1).then_inc(s_c, 1)
            g.wait_ge(s_v, RECORDS)
            with g.Fori(0, G) as i:
                nc.gpsimd.tensor_copy(now[:, :], pos_i[:, bass.ds(i * EB, EB)]).then_inc(s_now, 1)
                nc.gpsimd.tensor_copy(stage[:, :, :], rec[:, bass.ds(i * EB, EB), :]).then_inc(s_now, 1)
                g.wait_ge(s_now, i * 2 + 2)
                settle(g)
                for u in range(EB):
                    nc.gpsimd.indirect_dma_start(
                        out=dram["rec"][:, :], out_offset=bass.IndirectOffsetOnAxis(ap=now[:, u:u + 1], axis=0),
                        in_=stage[:, u, :], in_offset=None).then_inc(s_put, 16)
                g.wait_ge(s_put, i * (16 * EB) + 16 * EB)
                settle(g)

        @block.tensor
        def _(pe):
            pe.wait_ge(s_c, 2)
            pe.wait_ge(s_cnt, 2 * BK)
            pe.matmul(pW[:, 0:BK], before[:, :], cnt[:, :], start=True, stop=True).then_inc(s_mm, 1)
            pe.matmul(pC[:, 0:BK], ones[:, :], cnt[:, :], start=True, stop=True).then_inc(s_mm, 1)

        @block.vector
        def _(v):
            n = [0]

            def then(i):
                i.then_inc(s_v, 1)
                n[0] += 1
                v.wait_ge(s_v, n[0])

            then(v.memset(src_i[:, :], 0))
            then(v.memset(w_f[:, :], 0.0))
            v.memset(one[:, :], 1.0)
            v.memset(pos_f[:, :], -1.0)
            v.memset(rec[:, :, 3], 0.0)
            then(v.tensor_scalar(bkt_i[:, :], dst_i[:, 0:EF], 7, None, ALU.arith_shift_right))
            then(v.tensor_copy(bkt[:, :], bkt_i[:, :]))
            v.wait_ge(s_c, 2)
            with v.Fori(0, BK) as b:
                v.tensor_scalar(mask[:, :], bkt[:, :], number[:, bass.ds(b, 1)], None, ALU.is_equal).then_inc(s_cnt, 1)
                v.wait_ge(s_cnt, b * 2 + 1)
                v.tensor_reduce(cnt[:, bass.ds(b, 1)], mask[:, :], AX.X, ALU.add).then_inc(s_cnt, 1)
                v.wait_ge(s_cnt, b * 2 + 2)
                settle(v)
            v.wait_ge(s_mm, 2)
            then(v.tensor_copy(tot[:, :], pC[:, 0:BK]))
            then(v.tensor_tensor_scan(out=off[:, :], data0=one[:, 0:BK], data1=tot[:, :], initial=0.0,
                                      op0=ALU.mult, op1=ALU.add))
            then(v.tensor_tensor(off[:, :], off[:, :], tot[:, :], ALU.subtract))
            then(v.tensor_tensor(off[:, :], off[:, :], pW[:, 0:BK], ALU.add))
            with v.Fori(0, BK) as b:
                v.tensor_scalar(mask[:, :], bkt[:, :], number[:, bass.ds(b, 1)], None, ALU.is_equal).then_inc(s_b, 1)
                v.wait_ge(s_b, b * 4 + 1)
                v.tensor_tensor_scan(out=run[:, :], data0=one[:, :], data1=mask[:, :], initial=off[:, bass.ds(b, 1)],
                                     op0=ALU.mult, op1=ALU.add).then_inc(s_b, 1)
                v.wait_ge(s_b, b * 4 + 2)
                v.tensor_tensor(run[:, :], run[:, :], mask[:, :], ALU.mult).then_inc(s_b, 1)
                v.wait_ge(s_b, b * 4 + 3)
                v.tensor_tensor(pos_f[:, :], pos_f[:, :], run[:, :], ALU.add).then_inc(s_b, 1)
                v.wait_ge(s_b, b * 4 + 4)
                settle(v)
            v.wait_ge(s_dma, 64)
            v.tensor_copy(pos_i[:, :], pos_f[:, :])
            v.tensor_copy(rec[:, :, 0], src_i[:, :])
            v.tensor_copy(rec[:, :, 1], dst_i[:, 0:EF])
            then(v.tensor_copy(rec[:, :, 2], w_f[:, :]))
            assert n[0] == RECORDS

    with nc.Block() as block:
        @block.sync
        def _(sp):
            got = dram["rec"].rearrange("n c -> (n c)")
            sp.dma_start(rec[0:P - 1, :, :].rearrange("p n c -> p (n c)"),
                         got[0:(P - 1) * EF * 4].rearrange("(p n) -> p n", p=P - 1)).then_inc(s_dma, 16)
            rest = E - (P - 1) * EF
            sp.dma_start(rec[P - 1:P, 0:rest, :].rearrange("p n c -> p (n c)"),
                         got[(P - 1) * EF * 4:E * 4].rearrange("(p n) -> p n", p=1)).then_inc(s_dma, 16)
            sp.wait_ge(s_d, 3)
            for name, t in (("src", src_i), ("dst", bkt_i), ("weight", w_f)):
                for on_chip, a in rows(dram[name], t):
                    sp.dma_start(a, on_chip).then_inc(s_dma, 16)
            sp.wait_ge(s_dma, 64 + 32 + 96)

        @block.vector
        def _(v):
            v.wait_ge(s_dma, 64 + 32)
            v.tensor_copy(src_i[:, :], rec[:, :, 0]).then_inc(s_d, 1)
            v.tensor_copy(bkt_i[:, :], rec[:, :, 1]).then_inc(s_d, 1)
            v.tensor_copy(w_f[:, :], rec[:, :, 2]).then_inc(s_d, 1)


def prepare(nc, ins, dram, c, sb, pb, sem):
    full = (EC - 1) * P * P
    rows = (E - full) // P
    rest = E - full - rows * P
    with ExitStack() as ctx:
        src_i = sb("src_i", [P, EC, P], I32, ctx)
        dst_i = sb("dst_i", [P, EC, P], I32, ctx)
        w_f = sb("w_f", [P, EC, P], F32, ctx)
        src_f = sb("src_f", [P, EC, P], F32, ctx)
        dst_f = sb("dst_f", [P, EC, P], F32, ctx)
        tile_f = sb("tile_f", [P, EC, P], F32, ctx)
        ends_i = sb("ends_i", [P, 2, EC], I32, ctx)
        ends_b = sb("ends_b", [P, 2, EC], I32, ctx)
        ends_f = sb("ends_f", [P, 2, EC], F32, ctx)
        start_f = sb("start_f", [P, 2, EC], F32, ctx)
        step_i = sb("step_i", [P, STEPS], F32, ctx)
        sel = sb("sel", [P, EC, STEPS], F32, ctx)
        ge = sb("ge", [P, 2, STEPS], F32, ctx)
        tmp = sb("tmp", [P, STEPS], F32, ctx)
        tmp2 = sb("tmp2", [P, STEPS], F32, ctx)
        need = sb("need", [P, NB - LAG], F32, ctx)
        seen = sb("seen", [P, NB - LAG], F32, ctx)
        nlate = sb("nlate", [P, 1], F32, ctx)
        ps = [pb(f"pp{k}", ctx) for k in range(8)]
        s_clear = sem("p_clear")
        s_const = sem("p_const")
        s_x = sem("p_x")
        s_sd = sem("p_sd")
        s_stat = sem("p_stat")
        s_mv = sem("p_mv")
        stat = sb("stat_p", [P, NT, 6], F32, ctx)
        sd = sb("sd_p", [P, NT], F32, ctx)
        s_edges = sem("p_edges")
        s_ends = sem("p_ends")
        s_cast = sem("p_cast")
        s_start = sem("p_start")
        s_ge = sem("p_ge")
        s_sel = sem("p_sel")
        s_mm = sem("p_mm")
        s_out = sem("p_out")

        def by_tile(a, t):
            return [(t[:, 0:EC - 1, :], a[0:full].rearrange("(c p e) -> p c e", p=P, e=P)),
                    (t[0:rows, EC - 1, :], a[full:full + rows * P].rearrange("(p e) -> p e", e=P)),
                    (t[rows:rows + 1, EC - 1, 0:rest], a[full + rows * P:E].rearrange("(p e) -> p e", p=1))]

        def heads(a, t, shift):
            o = shift * P
            r = rows - shift
            out = [(t[:, shift, 0:EC - 1], a[o:o + full].rearrange("(c p e) -> p c e", p=P, e=P)[:, :, 0]),
                   (t[0:r, shift, EC - 1:EC], a[o + full:o + full + r * P].rearrange("(p e) -> p e", e=P)[:, 0:1]),
                   (t[r:r + 1, shift, EC - 1:EC], a[full + rows * P:full + rows * P + 1].rearrange("(p e) -> p e", p=1))]
            return out

        block = ctx.enter_context(nc.Block())

        @block.sync
        def _(sp):
            sp.wait_ge(s_clear, 4)
            for t, a in (*heads(dram["dst"], ends_i, 0), *heads(dram["dst"], ends_i, 1)):
                sp.dma_start(t, a, allow_slow_non_contiguous=True).then_inc(s_ends, 16)
            for t, a in (*by_tile(dram["dst"], dst_i), *by_tile(dram["src"], src_i),
                         *by_tile(dram["weight"], w_f)):
                sp.dma_start(t, a).then_inc(s_edges, 16)

        @block.scalar
        def _(act):
            act.wait_ge(s_edges, 16 * 9)
            act.wait_ge(s_clear, 5)
            x = ins["x"]
            act.dma_start(c["X"][:, 0:NT - 1, :], x[0:(NT - 1) * P, :].rearrange("(t p) d -> p t d", p=P)).then_inc(s_x, 16)
            act.dma_start(c["X"][0:LAST, NT - 1, :], x[(NT - 1) * P:N, :]).then_inc(s_x, 16)
            act.wait_ge(s_mv, NT)
            act.activation(sd[:, :], c["mv"][:, :, 1], ACT.Sqrt, bias=c["eps"][:, 0:1]).then_inc(s_sd, 1)

        @block.gpsimd
        def _(g):
            nc.gpsimd.iota(step_i[:, :], [[1, STEPS]], base=0, channel_multiplier=0,
                           allow_small_or_imprecise_dtypes=True).then_inc(s_const, 1)
            nc.gpsimd.iota(tile_f[:, :, :], [[P, EC], [0, P]], base=0, channel_multiplier=1,
                           allow_small_or_imprecise_dtypes=True).then_inc(s_const, 1)
            nc.gpsimd.iota(c["lane"][:, :], [[1, P]], base=0, channel_multiplier=0,
                           allow_small_or_imprecise_dtypes=True).then_inc(s_const, 1)
            nc.gpsimd.memset(c["ident"][:, :], 0.0).then_inc(s_const, 1)
            nc.gpsimd.iota(need[:, :], [[AW * TPB, NB - LAG]], base=AW * TPB, channel_multiplier=0,
                           allow_small_or_imprecise_dtypes=True).then_inc(s_const, 1)
            g.wait_ge(s_const, 5)
            nc.gpsimd.affine_select(out=c["ident"][:, :], in_=c["ident"][:, :], compare_op=ALU.not_equal,
                                    fill=1.0, base=0, pattern=[[-1, P]], channel_multiplier=1).then_inc(s_const, 1)

        @block.vector
        def _(v):
            v.memset(dst_i[:, EC - 1, :], -1).then_inc(s_clear, 1)
            v.memset(src_i[:, EC - 1, :], 0).then_inc(s_clear, 1)
            v.memset(w_f[:, EC - 1, :], 0.0).then_inc(s_clear, 1)
            v.memset(ends_i[:, :, :], FAR).then_inc(s_clear, 1)
            v.memset(c["X"][:, NT - 1, :], 0.0).then_inc(s_clear, 1)
            v.memset(c["eps"][:, :], EPS)
            v.memset(c["ones_row"][:, :], 1.0)
            v.memset(c["step_dst"][:, STEPS:STEPS + AHEAD], -1.0)
            v.memset(c["step_src"][:, STEPS:STEPS + R], 0)
            v.wait_ge(s_ends, 16 * 6)
            v.tensor_scalar(ends_b[:, :, :], ends_i[:, :, :], 7, None, ALU.arith_shift_right).then_inc(s_start, 1)
            v.wait_ge(s_start, 1)
            v.tensor_copy(ends_f[:, :, :], ends_b[:, :, :]).then_inc(s_start, 1)
            v.wait_ge(s_start, 2)
            v.wait_ge(s_const, 6)
            for k in range(2):
                v.tensor_tensor(start_f[:, k, :], ends_f[:, k, :], tile_f[:, :, 0], ALU.add).then_inc(s_start, 1)
            v.wait_ge(s_start, 4)
            v.tensor_scalar(start_f[:, 1, :], start_f[:, 1, :], 1.0, None, ALU.add).then_inc(s_start, 1)
            v.wait_ge(s_start, 5)
            for k in range(EC):
                if k >= 2:
                    v.wait_ge(s_sel, k - 1)
                v.tensor_scalar(ge[:, k % 2, :], step_i[:, :], start_f[:, 0, k:k + 1], None, ALU.is_ge).then_inc(s_ge, 1)
                v.wait_ge(s_ge, k + 1)
                v.scalar_tensor_tensor(out=sel[:, k, :], in0=step_i[:, :], scalar=start_f[:, 1, k:k + 1],
                                       in1=ge[:, k % 2, :], op0=ALU.is_lt, op1=ALU.mult).then_inc(s_sel, 1)
                if k == 1:
                    v.wait_ge(s_edges, 16 * 9)
                    v.tensor_copy(src_f[:, :, :], src_i[:, :, :]).then_inc(s_cast, 1)
                    v.tensor_scalar(dst_f[:, :, :], dst_i[:, :, :], 1.0, None, ALU.add).then_inc(s_cast, 1)
            v.wait_ge(s_x, 32)
            for t in range(NT):
                v.bn_stats(stat[:, t, :], c["X"][:, t, :]).then_inc(s_stat, 1)
            v.wait_ge(s_stat, NT)
            for t in range(NT):
                v.bn_aggr(c["mv"][:, t, :], stat[:, t, :]).then_inc(s_mv, 1)
            v.wait_ge(s_sd, 1)
            v.reciprocal(c["rs"][:, :], sd[:, :])
            v.wait_ge(s_mm, 8)
            n = 0
            for h in range(2):
                r = slice(h * HALF, h * HALF + HALF)
                v.tensor_copy(c["step_src"][:, r], ps[0 + h][:, 0:HALF])
                v.tensor_copy(c["step_w"][:, r], ps[4 + h][:, 0:HALF])
                v.tensor_tensor(tmp[:, r], step_i[:, r], ps[6 + h][:, 0:HALF], ALU.subtract).then_inc(s_out, 1)
                n += 1
                v.wait_ge(s_out, n)
                v.tensor_scalar(c["step_off"][:, r], tmp[:, r], float(NT - 1), float(AW), ALU.min, ALU.mult).then_inc(s_out, 1)
                n += 1
                v.tensor_scalar(tmp2[:, r], tmp[:, r], float(-P), -1.0, ALU.mult, ALU.add).then_inc(s_out, 1)
                n += 1
                v.wait_ge(s_out, n)
                v.tensor_tensor(c["step_dst"][:, r], tmp2[:, r], ps[2 + h][:, 0:HALF], ALU.add)
            v.tensor_copy(seen[:, :], c["step_off"][:, U * LAG:STEPS:U]).then_inc(s_out, 1)
            v.wait_ge(s_out, n + 1)
            v.tensor_tensor(seen[:, :], seen[:, :], need[:, :], ALU.is_lt).then_inc(s_out, 1)
            v.wait_ge(s_out, n + 2)
            v.tensor_reduce(nlate[:, :], seen[:, :], AX.X, ALU.add).then_inc(s_out, 1)
            v.wait_ge(s_out, n + 3)
            v.tensor_scalar(c["late"][:, :], nlate[:, :], 1.0, None, ALU.min)

        @block.tensor
        def _(pe):
            pe.wait_ge(s_const, 6)
            pe.wait_ge(s_edges, 16 * 9)
            pe.wait_ge(s_cast, 2)
            for k in range(EC):
                pe.wait_ge(s_sel, k + 1)
                for q, lst in enumerate((src_f, dst_f, w_f, tile_f)):
                    for h in range(2):
                        mm = pe.matmul(ps[2 * q + h][:, 0:HALF], lst[:, k, :], sel[:, k, h * HALF:(h + 1) * HALF],
                                       start=(k == 0), stop=(k == EC - 1))
                        if k == EC - 1:
                            mm.then_inc(s_mm, 1)


def settle(eng):
    eng.nop(nofuse=True)


def gather_ring(nc, table, sb, sem, ctx):
    return dict(
        rows=sb("rows", [P, R, AW], F32, ctx), now=sb("now", [P, R], I32, ctx), hot=sb("hot", [P, OH, P], F32, ctx),
        table=table, s_now=sem("s_now"), s_row=[sem(f"s_row{u}") for u in range(R)],
        s_scaled=sem("s_scaled"), s_hot=sem("s_hot"), s_mm=sem("s_mm"), s_add=sem("s_add"),
    )


def steps_pool(nc, c, r, g, layer, table=None):
    table = r["table"] if table is None else table
    with g.Fori(0, NB) as i:
        now = g.snap((layer * NB + i) * (U // Q) + layer * (R // Q))
        for u in range(U):
            x = u % R
            if u % Q == 0:
                g.wait_ge(r["s_now"], now + (u // Q + 1))
                settle(g)
            nc.gpsimd.indirect_dma_start(
                out=r["rows"][:, x, 0:D], out_offset=None, in_=table[:, :],
                in_offset=bass.IndirectOffsetOnAxis(ap=r["now"][:, x:x + 1], axis=0)).then_inc(r["s_row"][x], 16)


def steps_tensor(nc, c, r, pe, psum, width, layer, bodies=(0, NB), between=None):
    scaled = isinstance(layer, int) and layer == 0
    with pe.Fori(*bodies) as i:
        landed = [pe.snap((layer * NB + i) * (16 * U // R) + 16 * (n + 1)) for n in range(U // R)]
        step = pe.snap((layer * NB + i) * U)
        hots = pe.snap(step + layer * AHEAD)
        for u in range(U):
            if scaled:
                if u % 2 == 0:
                    pe.wait_ge(r["s_scaled"], step + (u + 2))
            else:
                pe.wait_ge(r["s_row"][u % R], landed[u // R])
            if u % 2 == 0:
                pe.wait_ge(r["s_hot"], hots + (u + 2))
                pe.wait_ge(r["s_add"], step + (u + 2))
            pe.matmul(psum[u % OH][:, 0:width], r["hot"][:, u % OH, :], r["rows"][:, u % R, 0:width],
                      start=True, stop=True).then_inc(r["s_mm"], 1)
            if between is not None:
                between(i, u)


def steps_vector(nc, c, r, v, psum, width, layer, bodies=(0, NB), between=None):
    acc = c["ACC"][:, :, :].rearrange("p t d -> p (t d)")

    def hot(s, slot):
        v.tensor_scalar(r["hot"][:, slot, :], c["lane"][:, :], c["step_dst"][:, bass.ds(s, 1)], None,
                        ALU.is_equal).then_inc(r["s_hot"], 1)

    def indices(s, slot):
        v.tensor_copy(r["now"][:, slot:slot + Q], c["step_src"][:, bass.ds(s, Q)]).then_inc(r["s_now"], 1)

    if bodies[0] == 0:
        for u in range(0, R, Q):
            indices(u, u)
        for s in range(AHEAD):
            hot(s, s)
    with v.Fori(*bodies) as i:
        col = v.snap(i * U)
        step = v.snap((layer * NB + i) * U)
        for u in range(U):
            hot(col + (u + AHEAD), (u + AHEAD) % OH)
            if u % LOADS == 0:
                _, offs = nc.values_load_multi_w_load_instructions(
                    c["step_off"][0:1, bass.ds(col + u, LOADS)], engines=(mybir.EngineType.DVE,),
                    min_val=0, max_val=AW * (NT - 1),
                    skip_runtime_bounds_check_because="prepare() keeps every step's bucket within 0 and NT - 1")
            a = acc[:, bass.ds(offs[u % LOADS], width)]
            v.wait_ge(r["s_mm"], step + (u + 1))
            v.wait_ge(r["s_add"], step + (u + OH))
            v.tensor_tensor(a, psum[u % OH][:, 0:width], a, ALU.add).then_inc(r["s_add"], 1)
            if u % Q == Q - 1:
                indices(col + (u + 1 - Q + R), (u + 1 - Q) % R)
            if between is not None:
                between(i, u)


def steps_scale(nc, c, r, act, layer, bodies=(0, NB), between=None):
    with act.Fori(*bodies) as i:
        landed = [act.snap((layer * NB + i) * (16 * U // R) + 16 * (n + 1)) for n in range(U // R)]
        col = act.snap(i * U)
        for u in range(U):
            act.wait_ge(r["s_row"][u % R], landed[u // R])
            settle(act)
            act.activation(r["rows"][:, u % R, 0:D], r["rows"][:, u % R, 0:D], ACT.Copy,
                           scale=c["step_w"][:, bass.ds(col + u, 1)]).then_inc(r["s_scaled"], 1)
            if between is not None:
                between(i, u)


def credits(nc, r, v):
    v.memset(r["rows"][:, :, D:AW], 1.0)
    v.memset(r["hot"][:, :, :], 0.0).then_inc(r["s_add"], OH)


def first_layer(nc, ins, dram, c, sb, pb, sem):
    with ExitStack() as ctx:
        r = c["ring"]
        w = sb("w_both", [P, KD, 2 * D], F32, ctx)
        bias = sb("bias_a", [P, D], F32, ctx)
        xn = sb("xn_a", [P, TG, D], F32, ctx)
        xt = sb("xt_a", [P, TG, D], F32, ctx)
        h = sb("h_a", [P, NT, D], F32, ctx)
        zero = sb("zero_a", [P, 2 * D], F32, ctx)
        s_w = sem("n_w")
        s_zero = sem("n_zero")
        s_fill = sem("n_fill")
        s_xn = sem("n_xn")
        s_T = sem("n_T")
        s_xt = sem("n_xt")
        s_M = sem("n_M")
        s_h = sem("n_h")
        s_own = sem("n_own")
        s_tab = sem("n_tab")

        with ExitStack() as pc, nc.Block() as block:
            turn_of = [u % 3 if u < TG - 1 else 1 for u in range(TG)]
            pT = [pb(f"pT_a{k}", pc) for k in range(2)]
            pN = [pb(f"pN_a{k}", pc) for k in range(3)]
            pO = [pb(f"pO_a{k}", pc) for k in range(3)]

            @block.sync
            def _(sp):
                sp.dma_start(w[:, :, 0:D], ins["L0_gnn_w_nbr"].rearrange("(k p) d -> p k d", p=P)).then_inc(s_w, 16)
                sp.dma_start(w[:, :, D:2 * D], ins["L0_gnn_w_own"].rearrange("(k p) d -> p k d", p=P)).then_inc(s_w, 16)
                sp.dma_start(bias[:, :], ins["L0_gnn_bias"].rearrange("(o d) -> o d", o=1).to_broadcast([P, D])).then_inc(s_w, 16)
                sp.wait_ge(s_zero, 1)
                sp.dma_start(dram["y"][SLOTS:SLOTS + BR, :].rearrange("(p r) d -> p (r d)", r=2), zero[:, :]).then_inc(s_fill, 16)
                table = dram["table"].rearrange("(t p) d -> p t d", p=P)
                with sp.Fori(0, NG) as g:
                    sp.wait_ge(s_h, g * TG + TG)
                    sp.dma_start(table[:, bass.ds(g * TG, TG), :], h[:, bass.ds(g * TG, TG), :]).then_inc(s_tab, 16)
                sp.wait_ge(s_tab, 16 * NG)
                sp.wait_ge(s_fill, 16)

            @block.vector
            def _(v):
                credits(nc, r, v)
                v.memset(zero[:, :], 0.0).then_inc(s_zero, 1)

                def normalised(t, slot):
                    v.tensor_scalar(xn[:, slot, :], c["X"][:, t, :], c["mv"][:, t, 0:1] if isinstance(t, int) else c["mv"][:, bass.ds(t, 1), 0],
                                    c["rs"][:, t:t + 1] if isinstance(t, int) else c["rs"][:, bass.ds(t, 1)],
                                    ALU.subtract, ALU.mult).then_inc(s_xn, 1)

                for u in range(TG):
                    normalised(u, u)
                v.wait_ge(s_w, 48)

                def group(g, ahead):
                    for u in range(TG):
                        t = g * TG + u
                        v.wait_ge(s_M, t + 2)
                        v.tensor_tensor(c["ACC"][:, t, 0:D], pO[turn_of[u]][:, 0:D], c["X"][:, t, :], ALU.add).then_inc(s_own, 1)
                        if ahead:
                            normalised(t + TG, u)
                        v.wait_ge(s_own, t + 1)
                        v.tensor_tensor(c["ACC"][:, t, 0:D], c["ACC"][:, t, 0:D], bias[:, :], ALU.add)

                with v.Fori(0, NG - 1) as g:
                    group(g, True)
                group(NG - 1, False)
                v.memset(c["ACC"][:, :, D:AW], 1.0)

            @block.scalar
            def _(act):
                with act.Fori(0, NG) as g:
                    for u in range(TG + 1):
                        if u < TG:
                            t = g * TG + u
                            act.wait_ge(s_T, t + 1)
                            act.activation(xt[:, u, :], pT[u % 2][:, 0:D], ACT.Copy).then_inc(s_xt, 1)
                        if u > 0:
                            t = g * TG + u - 1
                            act.wait_ge(s_M, t + 2)
                            settle(act)
                            act.activation(h[:, t, :], pN[turn_of[u - 1]][:, 0:D], ACT.Copy).then_inc(s_h, 1)

            @block.tensor
            def _(pe):
                pe.wait_ge(s_w, 48)
                pe.matmul(pN[0][:, 0:P], c["ident"][:, :], c["ident"][:, :], start=True, stop=True).then_inc(s_M, 1)

                def turn(g, u):
                    pe.wait_ge(s_xn, g * TG + (u + 1))
                    wait(pe, s_xt, g * TG + (u - 1 if u else 0))
                    for k in range(KD):
                        mm = pe.transpose(pT[u % 2][:, k * P:(k + 1) * P], xn[:, u, k * P:(k + 1) * P], c["ident"][:, :])
                    mm.then_inc(s_T, 1)

                def group(g):
                    turn(g, 0)
                    for u in range(TG):
                        if u + 1 < TG:
                            turn(g, u + 1)
                        pe.wait_ge(s_xt, g * TG + (u + 1))
                        wait(pe, s_h, g * TG + (u - 1))
                        wait(pe, s_own, g * TG + (u - 1))
                        for n, bank in enumerate((pN[turn_of[u]], pO[turn_of[u]])):
                            for k in range(KD):
                                mm = pe.matmul(bank[:, 0:D], xt[:, u, k * P:(k + 1) * P], w[:, k, n * D:(n + 1) * D],
                                               start=(k == 0), stop=(k == KD - 1))
                        mm.then_inc(s_M, 1)

                group(0)
                with pe.Fori(1, NG) as g:
                    group(g)


def wait(eng, s, value):
    if not isinstance(value, int) or value > 0:
        eng.wait_ge(s, value)


def first_steps(nc, ins, dram, c, moe, sb, pb, sem):
    with ExitStack() as ctx:
        b = dict(
            u1=sb("u_r", [P, TG, D], F32, ctx), ut=sb("ut_r", [P, TG, D], F32, ctx),
            wr=sb("wr_r", [P, KD, NE], F32, ctx), br=sb("br_r", [P, NE], F32, ctx),
            lg=sb("lg_r", [P, TG, NE], F32, ctx),
            stat=sb("stat_r", [P, TG, 6], F32, ctx), mv=sb("mv_r", [P, TG, 2], F32, ctx),
            sd=sb("sd_r", [P, TG], F32, ctx), rs=sb("rs_r", [P, TG], F32, ctx),
            t8=sb("t8_r", [P, TG, 8], F32, ctx), i8=sb("i8_r", [P, TG, 8], U32, ctx),
            dsd=sb("dsd_r", [P, NT], F32, ctx), bank=[pb(f"bank_r{k}", ctx) for k in range(8)],
        )
        q = {name: sem(f"r_{name}") for name in (
            "w", "deg", "rows", "stat", "mv", "sd", "rs", "u", "x", "T", "ut", "L", "lg", "top")}
        late = nc.values_load(c["late"][0:1, 0:1], min_val=0, max_val=1,
                              skip_runtime_bounds_check_because="it is the minimum of 1 and a count")
        with nc.If(late > 0):
            steps_apart(nc, c, b["bank"])
            route_apart(nc, ins, dram, c, moe, b, q)
        with nc.Else():
            steps_and_route(nc, ins, dram, c, moe, b, q)


def token_rows(sp, dram, c, q, t, n):
    rows = dram["tokens"].rearrange("(t p) d -> p t d", p=P)
    sp.wait_ge(q["x"], t + n)
    sp.dma_start(rows[:, bass.ds(t, n), :], c["X"][:, bass.ds(t, n), :]).then_inc(q["rows"], 16)


def route_sync(sp, ins, moe, b, q):
    sp.dma_start(b["wr"][:, :, :], ins["L0_ffn_Wr"].rearrange("(k p) e -> p k e", p=P)).then_inc(q["w"], 16)
    sp.dma_start(b["br"][:, :], ins["L0_ffn_br"].rearrange("(o e) -> o e", o=1).to_broadcast([P, NE])).then_inc(q["w"], 16)
    for e in range(NE):
        at = 0
        for name, n in (("L0_ffn_ln_g", KD), ("L0_ffn_ln_b", KD), ("L0_ffn_b1", HJ)):
            sp.dma_start(moe["prm"][:, e, at:at + n], ins[name][e, :].rearrange("(k p) -> p k", p=P),
                         allow_slow_non_contiguous=True).then_inc(q["w"], 16)
            at += n
    sp.wait_ge(q["w"], 16 * (2 + 3 * NE))


def steps_apart(nc, c, bank):
    r = c["ring"]
    with nc.Block() as block:
        psum = bank[0:OH]

        @block.gpsimd
        def _(g):
            steps_pool(nc, c, r, g, 0)

        @block.scalar
        def _(act):
            steps_scale(nc, c, r, act, 0)

        @block.tensor
        def _(pe):
            steps_tensor(nc, c, r, pe, psum, AW, 0)

        @block.vector
        def _(v):
            steps_vector(nc, c, r, v, psum, AW, 0)


def steps_and_route(nc, ins, dram, c, moe, b, q):
    u1, ut, lg, stat, mv, sd, rs, t8, i8 = (b[k] for k in ("u1", "ut", "lg", "stat", "mv", "sd", "rs", "t8", "i8"))
    psum, pT, pL = b["bank"][0:OH], b["bank"][4:6], b["bank"][6:8]
    r = c["ring"]
    SUMS = STEPS + OH
    with nc.Block() as block:
        @block.sync
        def _(sp):
            route_sync(sp, ins, moe, b, q)
            with sp.Fori(LAG, NB) as i:
                token_rows(sp, dram, c, q, *batch(i)[0:2])
            token_rows(sp, dram, c, q, *batch(None)[0:2])
            sp.wait_ge(q["rows"], 16 * BATCHES)

        @block.gpsimd
        def _(g):
            steps_pool(nc, c, r, g, 0)

        @block.tensor
        def _(pe):
            def turns(i):
                t, n, _ = batch(i)
                for k in range(n):
                    pe.wait_ge(q["u"], t + (k + 1))
                    if k >= 2:
                        pe.wait_ge(q["ut"], t + (k - 1))
                    for a in range(KD):
                        mm = pe.transpose(pT[k % 2][:, a * P:(a + 1) * P], u1[:, k, a * P:(a + 1) * P], c["ident"][:, :])
                    mm.then_inc(q["T"], 1)

            def logits(i):
                t, n, _ = batch(i)
                pe.wait_ge(q["w"], 16 * (2 + 3 * NE))
                for k in range(n):
                    pe.wait_ge(q["ut"], t + (k + 1))
                    if k >= 2:
                        pe.wait_ge(q["lg"], t + (k - 1))
                    for a in range(KD):
                        mm = pe.matmul(pL[k % 2][:, 0:NE], ut[:, k, a * P:(a + 1) * P], b["wr"][:, a, :],
                                       start=(a == 0), stop=(a == KD - 1))
                    mm.then_inc(q["L"], 1)

            def between(i, u):
                if u == 13:
                    turns(i)
                elif u == 24:
                    logits(i)

            steps_tensor(nc, c, r, pe, psum, AW, 0, (0, LAG))
            steps_tensor(nc, c, r, pe, psum, AW, 0, (LAG, NB), between)
            turns(None)
            logits(None)

        @block.scalar
        def _(act):
            def root(i, k):
                t, n, _ = batch(i)
                act.wait_ge(q["mv"], t * 2 + (k * n + n))
                act.activation(sd[:, 0:n], mv[:, 0:n, 1], ACT.Sqrt, bias=c["eps"][:, 0:1]).then_inc(q["sd"], 1)

            def turned(i):
                t, n, _ = batch(i)
                for k in range(n):
                    act.wait_ge(q["T"], t + (k + 1))
                    act.activation(ut[:, k, :], pT[k % 2][:, 0:D], ACT.Copy).then_inc(q["ut"], 1)

            def between(i, u):
                if u == 4:
                    root(i, 0)
                elif u == 14:
                    root(i, 1)
                elif u == 20:
                    turned(i)

            steps_scale(nc, c, r, act, 0, (0, LAG))
            steps_scale(nc, c, r, act, 0, (LAG, NB), between)
            act.wait_ge(r["s_add"], SUMS)
            act.activation(b["dsd"][:, :], c["ACC"][:, :, D], ACT.Sqrt).then_inc(q["deg"], 1)
            root(None, 0)
            root(None, 1)
            turned(None)

        @block.vector
        def _(v):
            def source(t, k, half):
                return u1[:, k, :] if half else c["ACC"][:, t + k, 0:D]

            def stats(i, half):
                t, n, _ = batch(i)
                if half:
                    v.wait_ge(q["u"], t + n)
                    settle(v)
                for k in range(n):
                    v.bn_stats(stat[:, k, :], source(t, k, half)).then_inc(q["stat"], 1)

            def aggregates(i, half):
                t, n, _ = batch(i)
                v.wait_ge(q["stat"], t * 2 + (half * n + n))
                settle(v)
                for k in range(n):
                    v.bn_aggr(mv[:, k, :], stat[:, k, :]).then_inc(q["mv"], 1)

            def deviations(i, half):
                _, n, j = batch(i)
                v.wait_ge(q["sd"], j * 2 + (half + 1))
                v.reciprocal(rs[:, 0:n], sd[:, 0:n]).then_inc(q["rs"], 1)

            def normalised(i, half):
                t, n, j = batch(i)
                v.wait_ge(q["rs"], j * 2 + (half + 1))
                for k in range(n):
                    v.tensor_scalar(c["X"][:, t + k, :] if half else u1[:, k, :], source(t, k, half), mv[:, k, 0:1],
                                    rs[:, k:k + 1], ALU.subtract, ALU.mult).then_inc(q["x" if half else "u"], 1)

            def biased(i):
                t, n, _ = batch(i)
                v.wait_ge(q["w"], 16 * (2 + 3 * NE))
                for k in range(n):
                    v.wait_ge(q["L"], t + (k + 1))
                    v.tensor_tensor(lg[:, k, :], pL[k % 2][:, 0:NE], b["br"][:, :], ALU.add).then_inc(q["lg"], 1)

            def largest(i):
                t, n, _ = batch(i)
                v.wait_ge(q["lg"], t + n)
                settle(v)
                for k in range(n):
                    v.max(t8[:, k, :], lg[:, k, :]).then_inc(q["top"], 1)

            def where(i):
                t, n, _ = batch(i)
                v.wait_ge(q["top"], t * 2 + n)
                settle(v)
                for k in range(n):
                    v.max_index(i8[:, k, :], t8[:, k, :], lg[:, k, :]).then_inc(q["top"], 1)

            def kept(i):
                t, n, _ = batch(i)
                v.wait_ge(q["top"], t * 2 + 2 * n)
                settle(v)
                v.tensor_copy(moe["top"][:, bass.ds(t, n), :], t8[:, 0:n, 0:2])
                v.tensor_copy(moe["idx"][:, bass.ds(t, n), :], i8[:, 0:n, 0:2])

            def between(i, u):
                if u in (0, 9):
                    stats(i, u // 9)
                elif u in (1, 10):
                    aggregates(i, u // 9)
                elif u in (7, 17):
                    deviations(i, u // 17)
                elif u in (8, 18):
                    normalised(i, u // 18)
                elif u == 27:
                    biased(i)
                elif u == 28:
                    largest(i)
                elif u == 29:
                    where(i)
                elif u == 30:
                    kept(i)

            steps_vector(nc, c, r, v, psum, AW, 0, (0, LAG))
            steps_vector(nc, c, r, v, psum, AW, 0, (LAG, NB), between)
            v.wait_ge(r["s_add"], SUMS)
            for half in range(2):
                stats(None, half)
                aggregates(None, half)
                deviations(None, half)
                normalised(None, half)
            biased(None)
            largest(None)
            where(None)
            kept(None)
            v.wait_ge(q["deg"], 1)
            v.reciprocal(c["dinv"][:, :], b["dsd"][:, :])


def batch(i):
    if i is None:
        return NT - TAIL, TAIL, BATCHES - 1
    return i * TPB - LAG * TPB, TPB, i - LAG


def route_apart(nc, ins, dram, c, moe, b, q):
    u1, ut, wr, br, lg, stat, mv, sd, rs, t8, i8, dsd = (
        b[k] for k in ("u1", "ut", "wr", "br", "lg", "stat", "mv", "sd", "rs", "t8", "i8", "dsd"))
    pT, pL = b["bank"][0:3], b["bank"][3:6]
    with nc.Block() as block:
        @block.sync
        def _(sp):
            route_sync(sp, ins, moe, b, q)
            with sp.Fori(0, NG) as g:
                token_rows(sp, dram, c, q, g * TG, TG)
            sp.wait_ge(q["rows"], 16 * NG)

        @block.vector
        def _(v):
            v.wait_ge(q["deg"], 1)
            v.reciprocal(c["dinv"][:, :], dsd[:, :])
            v.wait_ge(q["w"], 16 * (2 + 3 * NE))

            def normalise(g, src, dst, r, done):
                for u in range(TG):
                    v.bn_stats(stat[:, u, :], src(u)).then_inc(q["stat"], 1)
                v.wait_ge(q["stat"], r * TG + TG)
                settle(v)
                for u in range(TG):
                    v.bn_aggr(mv[:, u, :], stat[:, u, :]).then_inc(q["mv"], 1)
                v.wait_ge(q["sd"], r + 1)
                v.reciprocal(rs[:, :], sd[:, :]).then_inc(q["rs"], 1)
                v.wait_ge(q["rs"], r + 1)
                for u in range(TG):
                    v.tensor_scalar(dst(u), src(u), mv[:, u, 0:1], rs[:, u:u + 1],
                                    ALU.subtract, ALU.mult).then_inc(done, 1)

            with v.Fori(0, NG) as g:
                normalise(g, lambda u: c["ACC"][:, g * TG + u, 0:D], lambda u: u1[:, u, :], g * 2, q["u"])
                v.wait_ge(q["u"], g * TG + TG)
                normalise(g, lambda u: u1[:, u, :], lambda u: c["X"][:, g * TG + u, :], g * 2 + 1, q["x"])
                for u in range(TG):
                    v.wait_ge(q["L"], g * TG + u + 1)
                    v.tensor_tensor(lg[:, u, :], pL[u % 3][:, 0:NE], br[:, :], ALU.add).then_inc(q["lg"], 1)
                v.wait_ge(q["lg"], g * TG + TG)
                settle(v)
                for u in range(TG):
                    v.max(t8[:, u, :], lg[:, u, :]).then_inc(q["top"], 1)
                v.wait_ge(q["top"], g * (3 * TG) + TG)
                settle(v)
                for u in range(TG):
                    v.max_index(i8[:, u, :], t8[:, u, :], lg[:, u, :]).then_inc(q["top"], 2)
                v.wait_ge(q["top"], g * (3 * TG) + 3 * TG)
                settle(v)
                v.tensor_copy(moe["top"][:, bass.ds(g * TG, TG), :], t8[:, :, 0:2])
                v.tensor_copy(moe["idx"][:, bass.ds(g * TG, TG), :], i8[:, :, 0:2])

        @block.scalar
        def _(act):
            act.activation(dsd[:, :], c["ACC"][:, :, D], ACT.Sqrt).then_inc(q["deg"], 1)
            with act.Fori(0, NG) as g:
                for k in range(2):
                    act.wait_ge(q["mv"], (g * 2 + k) * TG + TG)
                    act.activation(sd[:, :], mv[:, :, 1], ACT.Sqrt, bias=c["eps"][:, 0:1]).then_inc(q["sd"], 1)
                for u in range(TG):
                    act.wait_ge(q["T"], g * TG + u + 1)
                    act.activation(ut[:, u, :], pT[u % 3][:, 0:D], ACT.Copy).then_inc(q["ut"], 1)

        @block.tensor
        def _(pe):
            pe.wait_ge(q["w"], 16 * (2 + 3 * NE))

            def turn(g, u):
                pe.wait_ge(q["u"], g * TG + u + 1)
                if u >= 3:
                    pe.wait_ge(q["ut"], g * TG + u - 2)
                for k in range(KD):
                    mm = pe.transpose(pT[u % 3][:, k * P:(k + 1) * P], u1[:, u, k * P:(k + 1) * P], c["ident"][:, :])
                mm.then_inc(q["T"], 1)

            with pe.Fori(0, NG) as g:
                turn(g, 0)
                for u in range(TG):
                    if u + 1 < TG:
                        turn(g, u + 1)
                    pe.wait_ge(q["ut"], g * TG + u + 1)
                    if u >= 3:
                        pe.wait_ge(q["lg"], g * TG + u - 2)
                    for k in range(KD):
                        mm = pe.matmul(pL[u % 3][:, 0:NE], ut[:, u, k * P:(k + 1) * P], wr[:, k, :],
                                       start=(k == 0), stop=(k == KD - 1))
                    mm.then_inc(q["L"], 1)


def place(nc, c, moe, sb, pb, sem):
    with ExitStack() as ctx:
        EN = NE * NT
        node = sb("node", [P, NT], F32, ctx)
        blk = sb("blk", [P, NBLK + 1], F32, ctx)
        before = sb("before", [P, P], F32, ctx)
        ones = sb("ones", [P, P], F32, ctx)
        idxf = sb("idxf", [P, 2, NT], F32, ctx)
        gap = sb("gap", [P, NT], F32, ctx)
        ratio = sb("ratio", [P, NT], F32, ctx)
        den = sb("den", [P, NT], F32, ctx)
        spare = sb("spare", [P, 2, NT], F32, ctx)
        mk = sb("mk", [P, 2, NE, NT], F32, ctx)
        m = sb("m", [P, NE, NT], F32, ctx)
        cnt = sb("cnt", [P, NE, NT], F32, ctx)
        inc = sb("inc", [P, NE, NT], F32, ctx)
        row = sb("row", [P, NE, NT], F32, ctx)
        nbi = sb("nbi", [P, 2, NE], I32, ctx)
        nbf = sb("nbf", [P, NE], F32, ctx)
        cum = sb("cum", [P, NE], F32, ctx)
        base = sb("base", [P, NE], F32, ctx)
        posf = sb("posf", [P, 2, NT], F32, ctx)
        ebf = sb("ebf", [P, NBLK + 1], F32, ctx)
        pW, pC = pb("pW", ctx), pb("pC", ctx)
        s_c, s_v, s_e, s_r, s_mm = sem("l_const"), sem("l_step"), sem("l_exp"), sem("l_gap"), sem("l_mm")
        s_m = sem("l_m")
        block = ctx.enter_context(nc.Block())

        @block.gpsimd
        def _(g):
            nc.gpsimd.iota(node[:, :], [[P, NT]], base=0, channel_multiplier=1,
                           allow_small_or_imprecise_dtypes=True).then_inc(s_c, 1)
            nc.gpsimd.iota(blk[:, :], [[1, NBLK + 1]], base=0, channel_multiplier=0,
                           allow_small_or_imprecise_dtypes=True).then_inc(s_c, 1)
            nc.gpsimd.memset(ones[:, :], 1.0).then_inc(s_c, 1)
            g.wait_ge(s_c, 3)
            nc.gpsimd.affine_select(out=before[:, :], in_=ones[:, :], compare_op=ALU.is_gt, fill=0.0,
                                    base=0, pattern=[[1, P]], channel_multiplier=-1).then_inc(s_c, 1)

        @block.scalar
        def _(act):
            act.wait_ge(s_r, 1)
            act.activation(ratio[:, :], gap[:, :], ACT.Exp).then_inc(s_e, 1)

        @block.tensor
        def _(pe):
            pe.wait_ge(s_c, 4)
            pe.wait_ge(s_m, 1)
            mf = m[:, :, :].rearrange("p e t -> p (e t)")
            pe.matmul(pW[:, 0:EN], before[:, :], mf, start=True, stop=True).then_inc(s_mm, 1)
            pe.matmul(pC[:, 0:EN], ones[:, :], mf, start=True, stop=True).then_inc(s_mm, 1)

        @block.vector
        def _(v):
            n = [0]

            def then(ins):
                ins.then_inc(s_v, 1)
                n[0] += 1
                v.wait_ge(s_v, n[0])

            v.wait_ge(s_c, 4)
            v.tensor_tensor(gap[:, :], moe["top"][:, :, 1], moe["top"][:, :, 0], ALU.subtract).then_inc(s_r, 1)
            v.tensor_scalar(c["valid"][:, :], node[:, :], float(N), None, ALU.is_lt)
            for k in range(2):
                ins = v.tensor_copy(idxf[:, k, :], moe["idx"][:, :, k])
            then(ins)
            for k in range(2):
                for e in range(NE):
                    ins = v.scalar_tensor_tensor(out=mk[:, k, e, :], in0=idxf[:, k, :], scalar=float(e),
                                                 in1=c["valid"][:, :], op0=ALU.is_equal, op1=ALU.mult)
            then(ins)
            v.tensor_tensor(m[:, :, :], mk[:, 0, :, :], mk[:, 1, :, :], ALU.add).then_inc(s_m, 1)
            v.wait_ge(s_e, 1)
            then(v.tensor_scalar(den[:, :], ratio[:, :], 1.0, None, ALU.add))
            then(v.reciprocal(moe["wt"][:, 0, :], den[:, :]))
            v.tensor_tensor(moe["wt"][:, 1, :], moe["wt"][:, 0, :], ratio[:, :], ALU.mult)
            for k in range(2):
                v.tensor_scalar(spare[:, k, :], node[:, :], float(SLOTS - (NT - 1) * P + k * P), None, ALU.add)
            then(v.tensor_scalar(gap[:, :], c["valid"][:, :], -1.0, 1.0, ALU.mult, ALU.add))
            for k in range(2):
                ins = v.tensor_tensor(spare[:, k, :], spare[:, k, :], gap[:, :], ALU.mult)
            then(ins)
            v.wait_ge(s_mm, 2)
            then(v.tensor_copy(cnt[:, :, :], pC[:, 0:EN].rearrange("p (e t) -> p e t", e=NE)))
            for e in range(NE):
                ins = v.tensor_tensor_scan(out=inc[:, e, :], data0=c["ones_row"][:, :], data1=cnt[:, e, :],
                                           initial=0.0, op0=ALU.mult, op1=ALU.add)
            then(ins)
            then(v.tensor_scalar(nbi[:, 0, :], inc[:, :, NT - 1], float(BR - 1), None, ALU.add))
            then(v.tensor_scalar(nbi[:, 1, :], nbi[:, 0, :], 8, None, ALU.arith_shift_right))
            then(v.tensor_copy(nbf[:, :], nbi[:, 1, :]))
            then(v.tensor_tensor_scan(out=cum[:, :], data0=c["ones_row"][:, 0:NE], data1=nbf[:, :],
                                      initial=0.0, op0=ALU.mult, op1=ALU.add))
            then(v.tensor_tensor(base[:, :], cum[:, :], nbf[:, :], ALU.subtract))
            then(v.tensor_scalar(base[:, :], base[:, :], float(BR), None, ALU.mult))
            then(v.tensor_tensor(row[:, :, :], inc[:, :, :], cnt[:, :, :], ALU.subtract))
            then(v.tensor_tensor(row[:, :, :], row[:, :, :], pW[:, 0:EN].rearrange("p (e t) -> p e t", e=NE), ALU.add))
            for e in range(NE):
                ins = v.tensor_scalar(row[:, e, :], row[:, e, :], base[:, e:e + 1], None, ALU.add)
            then(ins)
            for k in range(2):
                ins = v.tensor_tensor(mk[:, k, :, :], mk[:, k, :, :], row[:, :, :], ALU.mult)
            then(ins)
            for k in range(2):
                ins = v.tensor_reduce(posf[:, k, :], mk[:, k, :, :].rearrange("p e t -> p t e"), AX.X, ALU.add)
            then(ins)
            v.tensor_tensor(moe["pos"][:, :, 0:NT], posf[:, :, :], spare[:, :, :], ALU.add)
            v.memset(moe["pos"][:, :, NT:NT + 1], 0)
            then(v.memset(ebf[:, :], 0.0))
            for e in range(NE):
                then(v.scalar_tensor_tensor(out=ebf[:, :], in0=blk[:, :], scalar=cum[:, e:e + 1], in1=ebf[:, :],
                                            op0=ALU.is_ge, op1=ALU.add))
            v.tensor_scalar(moe["expert"][:, :], ebf[:, :], float(NE - 1), None, ALU.min)


def invert(nc, c, moe, sb, pb, sem):
    COLS = SLOTS // P
    M = 2 * TG
    with ExitStack() as ctx:
        lane_i = sb("lane_i", [P, 2, NT], I32, ctx)
        col_i = sb("col_i", [P, 2, NT], I32, ctx)
        lane_f = sb("lane_f", [P, 2, NT], F32, ctx)
        col_f = sb("col_f", [P, 2, NT], F32, ctx)
        token = sb("token", [P, NT], F32, ctx)
        rows = sb("rows_i", [P, M, P], F32, ctx)
        cols = sb("cols_i", [P, M, COLS], F32, ctx)
        s_c, s_v, s_hot, s_mm = sem("i_const"), sem("i_v"), sem("i_hot"), sem("i_mm")
        pI = pb("pI", ctx)
        block = ctx.enter_context(nc.Block())

        @block.gpsimd
        def _(g):
            nc.gpsimd.iota(token[:, :], [[P, NT]], base=0, channel_multiplier=1,
                           allow_small_or_imprecise_dtypes=True).then_inc(s_c, 1)

        @block.vector
        def _(v):
            v.tensor_scalar(lane_i[:, :, :], moe["pos"][:, :, 0:NT], P - 1, None, ALU.bitwise_and).then_inc(s_v, 1)
            v.tensor_scalar(col_i[:, :, :], moe["pos"][:, :, 0:NT], 7, None, ALU.arith_shift_right).then_inc(s_v, 1)
            v.memset(moe["inv"][:, COLS:], 0)
            v.wait_ge(s_v, 2)
            v.tensor_copy(lane_f[:, :, :], lane_i[:, :, :]).then_inc(s_v, 1)
            v.tensor_copy(col_f[:, :, :], col_i[:, :, :]).then_inc(s_v, 1)
            v.wait_ge(s_v, 4)
            v.wait_ge(s_c, 1)

            def body(g):
                for n in range(M):
                    k, t = n % 2, g * TG + n // 2
                    wait(v, s_mm, g * M + (n + 1 - M))
                    v.tensor_scalar(rows[:, n, :], c["lane"][:, :], lane_f[:, k, bass.ds(t, 1)], None, ALU.is_equal)
                    v.tensor_scalar(cols[:, n, :], c["lane"][:, 0:COLS], col_f[:, k, bass.ds(t, 1)], token[:, bass.ds(t, 1)],
                                    ALU.is_equal, ALU.mult).then_inc(s_hot, 1)

            body(0)
            with v.Fori(1, NG) as g:
                body(g)
            v.wait_ge(s_mm, NG * M)
            v.tensor_copy(moe["inv"][:, 0:COLS], pI[:, 0:COLS])

        @block.tensor
        def _(pe):
            def body(g):
                for n in range(M):
                    pe.wait_ge(s_hot, g * M + (n + 1))
                    first = isinstance(g, int) and g == 0 and n == 0
                    last = isinstance(g, int) and g == NG - 1 and n == M - 1
                    pe.matmul(pI[:, 0:COLS], rows[:, n, :], cols[:, n, :], start=first, stop=last,
                              skip_group_check=True).then_inc(s_mm, 1)

            body(0)
            with pe.Fori(1, NG - 1) as g:
                body(g)
            body(NG - 1)


def experts(nc, ins, dram, c, moe, sb, pb, sem):
    with ExitStack() as ctx:
        w1 = sb("w1_e", [P, 2, KD, HID], F32, ctx)
        w2 = sb("w2_e", [P, 2, HJ, D], F32, ctx)
        b2 = sb("b2_e", [P, 2, D], F32, ctx)
        tok = sb("tok_e", [P, 2, 2, D], F32, ctx)
        now = sb("now_e", [P, 2, 2], I32, ctx)
        s_now = moe["now"]
        prm = sb("prm_e", [P, 2, PRM], F32, ctx)
        xe = sb("xe_e", [P, 2, KD, BR], F32, ctx)
        h = sb("h_e", [P, HJ, BR], F32, ctx)
        y = sb("y_e", [P, 2, 2, D], F32, ctx)
        pT = pb("pT_e", ctx)
        pH = [pb(f"pH_e{k}", ctx) for k in range(HJ // 2)]
        pY = [pb(f"pY_e{k}", ctx) for k in range(2)]
        s_w = [sem(f"e_w{q}") for q in range(2)]
        s_tok = [sem(f"e_tok{q}") for q in range(2)]
        s_st = [sem(f"e_store{q}") for q in range(2)]
        s_prm, s_T, s_xe, s_mm1, s_h, s_mm2, s_y = (sem("e_prm"), sem("e_T"), sem("e_xe"), sem("e_mm1"), sem("e_h"),
                                                    sem("e_mm2"), sem("e_y"))
        yrows = dram["y"].rearrange("(b m p) d -> p b m d", m=2, p=P)
        w1_d = ins["L0_ffn_W1"].rearrange("e (k p) h -> p e k h", p=P)
        w2_d = ins["L0_ffn_W2"].rearrange("e (j p) d -> p e j d", p=P)
        b2_d = ins["L0_ffn_b2"]
        block = ctx.enter_context(nc.Block())

        def pairs(eng, body):
            body(0)
            with eng.Fori(1, NBLK // 2) as i:
                body(i)

        @block.sync
        def _(sp):
            def store(b, q):
                sp.dma_start(yrows[:, b, :, :], y[:, q, :, :]).then_inc(s_st[q], 16)

            def body(i):
                for q in range(2):
                    b = i * 2 + q
                    e = sp.value_load(moe["expert"][0:1, bass.ds(b, 1)], min_val=0, max_val=NE - 1)
                    wait(sp, s_mm2, b - 1)
                    sp.dma_start(w1[:, q, :, :], w1_d[:, bass.ds(e, 1), :, :].rearrange("p o k h -> p (o k) h")).then_inc(s_w[q], 16)
                    sp.dma_start(w2[:, q, :, :], w2_d[:, bass.ds(e, 1), :, :].rearrange("p o j d -> p (o j) d")).then_inc(s_w[q], 16)
                    wait(sp, s_y, b * 2 - 2)
                    sp.dma_start(b2[:, q, :], b2_d[bass.ds(e, 1), :].to_broadcast([P, D])).then_inc(s_w[q], 16)
                    if not isinstance(i, int):
                        store(b - 2, q)
            pairs(sp, body)
            for q in range(2):
                sp.wait_ge(s_y, (NBLK - 2 + q) * 2 + 2)
                store(NBLK - 2 + q, q)
            for q in range(2):
                sp.wait_ge(s_st[q], 16 * (NBLK // 2))

        @block.vector
        def _(v):
            def inputs(b, q):
                e = v.value_load(moe["expert"][0:1, bass.ds(b, 1)], min_val=0, max_val=NE - 1)
                wait(v, s_h, b * 4 - 4)
                v.tensor_copy(prm[:, q, :], moe["prm"][:, bass.ds(e, 1), :].rearrange("p o n -> p (o n)")).then_inc(s_prm, 1)
                v.wait_ge(s_prm, b + 1)
                v.wait_ge(s_T, b + 1)
                for k in range(KD):
                    ins_ = v.tensor_scalar(xe[:, q, k, :], pT[:, k * BR:(k + 1) * BR], prm[:, q, k:k + 1],
                                           prm[:, q, KD + k:KD + k + 1], ALU.mult, ALU.add)
                ins_.then_inc(s_xe, 1)

            inputs(0, 0)

            def body(i):
                for q in range(2):
                    b = i * 2 + q
                    inputs(b + 1, 1 - q)
                    wait(v, s_st[q], i * 16)
                    if not isinstance(i, int):
                        settle(v)
                    v.wait_ge(s_mm2, b + 1)
                    for m in range(2):
                        v.tensor_tensor(y[:, q, m, :], pY[m][:, 0:D], b2[:, q, :], ALU.add).then_inc(s_y, 1)
            pairs(v, body)

        @block.scalar
        def _(act):
            def body(i):
                for q in range(2):
                    b = i * 2 + q
                    for j in range(HJ // 2):
                        act.wait_ge(s_mm1, b * (HJ // 2) + j + 1)
                        for n in range(2):
                            k = 2 * j + n
                            a = act.activation(h[:, k, :], pH[j][:, n * BR:(n + 1) * BR], ACT.Gelu,
                                               bias=prm[:, q, 2 * KD + k:2 * KD + k + 1])
                        a.then_inc(s_h, 1)
            pairs(act, body)

        @block.tensor
        def _(pe):
            def turn(b, q):
                pe.wait_ge(s_tok[q], 32)
                for m in range(2):
                    for k in range(KD):
                        mm = pe.transpose(pT[:, k * BR + m * P:k * BR + (m + 1) * P], tok[:, q, m, k * P:(k + 1) * P], c["ident"][:, :])
                mm.then_inc(s_T, 1)

            turn(0, 0)

            def body(i):
                for q in range(2):
                    b = i * 2 + q
                    pe.wait_ge(s_xe, b + 1)
                    pe.wait_ge(s_w[q], i * 48 + 48)
                    for j in range(HJ // 2):
                        for n in range(2):
                            o = (2 * j + n) * P
                            for k in range(KD):
                                mm = pe.matmul(pH[j][:, n * BR:(n + 1) * BR], w1[:, q, k, o:o + P], xe[:, q, k, :],
                                               start=(k == 0), stop=(k == KD - 1))
                        mm.then_inc(s_mm1, 1)
                    pe.wait_ge(s_tok[1 - q], i * 32 + 32 * (1 + q))
                    for m in range(2):
                        for k in range(KD):
                            mm = pe.transpose(pT[:, k * BR + m * P:k * BR + (m + 1) * P], tok[:, 1 - q, m, k * P:(k + 1) * P],
                                              c["ident"][:, :])
                    mm.then_inc(s_T, 1)
                    wait(pe, s_y, b * 2)
                    for j in range(HJ):
                        if j % 2 == 0:
                            pe.wait_ge(s_h, b * (HJ // 2) + j // 2 + 1)
                        for m in range(2):
                            mm = pe.matmul(pY[m][:, 0:D], h[:, j, m * P:(m + 1) * P], w2[:, q, j, :],
                                           start=(j == 0), stop=(j == HJ - 1))
                    mm.then_inc(s_mm2, 1)
            pairs(pe, body)

        @block.gpsimd
        def _(g):
            def tokens(b, q):
                wait(g, s_T, b - 1)
                if not isinstance(b, int):
                    settle(g)
                nc.gpsimd.tensor_copy(now[:, q, :], moe["inv"][:, bass.ds(b * 2, 2)]).then_inc(s_now, 1)
                g.wait_ge(s_now, b + 1)
                settle(g)
                for m in range(2):
                    nc.gpsimd.indirect_dma_start(
                        out=tok[:, q, m, :], out_offset=None, in_=dram["tokens"][:, :],
                        in_offset=bass.IndirectOffsetOnAxis(ap=now[:, q, m:m + 1], axis=0)).then_inc(s_tok[q], 16)

            tokens(0, 0)

            def body(i):
                for q in range(2):
                    b = i * 2 + q
                    tokens(b + 1, 1 - q)
            pairs(g, body)
            for q in range(2):
                g.wait_ge(s_tok[q], 32 * (NBLK // 2 + 1 - q))


def mixture(nc, ins, dram, c, moe, sb, pb, sem):
    place(nc, c, moe, sb, pb, sem)
    invert(nc, c, moe, sb, pb, sem)
    experts(nc, ins, dram, c, moe, sb, pb, sem)


def convolutions(nc, ins, dram, c, moe, sb, pb, sem):
    with ExitStack() as ctx:
        w = sb("w_g", [P, LAYERS, KD, D], F32, ctx)
        vec = sb("vec_g", [P, 3, LAYERS, D], F32, ctx)
        b = dict(
            w=w, vec=vec, z=sb("z_g", [P, TG, D], F32, ctx), xin=sb("xin_g", [P, TG, D], F32, ctx),
            xt=sb("xt_g", [P, TG, D], F32, ctx), stat=sb("stat_g", [P, TG, 6], F32, ctx),
            mv=sb("mv_g", [P, TG, 2], F32, ctx), sd=sb("sd_g", [P, TG], F32, ctx), rs=sb("rs_g", [P, TG], F32, ctx),
        )
        q = {name: sem(f"g_{name}") for name in (
            "w", "z", "stat", "mv", "sd", "rs", "zz", "z2", "z3", "xin", "T", "xt", "M", "h", "tab")}
        bank = [pb(f"bank_g{k}", ctx) for k in range(8)]
        b.update(pS=bank[0:OH], pT=bank[4:6], pM=bank[6:8])
        combine(nc, ins, dram, c, moe, b, q, sb, sem)
        late = nc.values_load(c["late"][0:1, 0:1], min_val=0, max_val=1,
                              skip_runtime_bounds_check_because="it is the minimum of 1 and a count")
        with nc.If(late > 0):
            layers_apart(nc, dram, c, b, q)
        with nc.Else():
            layers_overlapped(nc, dram, c, b, q)


def moments(v, b, q, n, src):
    for u in range(TG):
        v.bn_stats(b["stat"][:, u, :], src(u)).then_inc(q["stat"], 1)
    v.wait_ge(q["stat"], n * TG + TG)
    settle(v)
    for u in range(TG):
        v.bn_aggr(b["mv"][:, u, :], b["stat"][:, u, :]).then_inc(q["mv"], 1)
    v.wait_ge(q["sd"], n + 1)
    v.reciprocal(b["rs"][:, :], b["sd"][:, :]).then_inc(q["rs"], 1)
    v.wait_ge(q["rs"], n + 1)


def nodes_tensor(pe, c, b, q, l):
    w = b["w"]

    def turn(g, u):
        t = g * TG + u
        pe.wait_ge(q["xin"], l * NT + t + 1)
        if u >= 1:
            pe.wait_ge(q["xt"], l * NT + t)
        for k in range(KD):
            mm = pe.transpose(b["pT"][0][:, k * P:(k + 1) * P], b["xin"][:, u, k * P:(k + 1) * P], c["ident"][:, :])
        mm.then_inc(q["T"], 1)

    with pe.Fori(0, NG) as g:
        turn(g, 0)
        for u in range(TG):
            if u + 1 < TG:
                turn(g, u + 1)
            t = g * TG + u
            pe.wait_ge(q["xt"], l * NT + t + 1)
            if u >= 2:
                pe.wait_ge(q["h"], l * NT + t - 1)
            for k in range(KD):
                mm = pe.matmul(b["pM"][u % 2][:, 0:D], b["xt"][:, u, k * P:(k + 1) * P],
                               w[:, l, k, :] if isinstance(l, int) else w[:, bass.ds(l, 1), k, :].rearrange("p o d -> p (o d)"),
                               start=(k == 0), stop=(k == KD - 1))
            mm.then_inc(q["M"], 1)


def nodes_scalar(act, c, b, q, l):
    with act.Fori(0, NG) as g:
        act.wait_ge(q["mv"], l * NT + g * TG + TG)
        act.activation(b["sd"][:, :], b["mv"][:, :, 1], ACT.Sqrt, bias=c["eps"][:, 0:1]).then_inc(q["sd"], 1)
        if not isinstance(l, int):
            for u in range(TG):
                act.wait_ge(q["z3"], (l - 1) * NT + g * TG + u + 1)
                act.activation(b["xin"][:, u, :], b["z"][:, u, :], ACT.Relu).then_inc(q["xin"], 1)
        for u in range(TG + 1):
            if u < TG:
                act.wait_ge(q["T"], l * NT + g * TG + u + 1)
                act.activation(b["xt"][:, u, :], b["pT"][0][:, 0:D], ACT.Copy).then_inc(q["xt"], 1)
            if u > 0:
                t = g * TG + u - 1
                act.wait_ge(q["M"], l * NT + t + 2)
                settle(act)
                act.activation(c["ACC"][:, t, 0:D], b["pM"][(u - 1) % 2][:, 0:D], ACT.Copy,
                               scale=c["dinv"][:, bass.ds(t, 1)]).then_inc(q["h"], 1)


def nodes_sync(sp, dram, c, q, l):
    table = dram["table"].rearrange("(t p) d -> p t d", p=P)
    with sp.Fori(0, NG) as g:
        sp.wait_ge(q["h"], l * NT + g * TG + TG)
        sp.dma_start(table[:, bass.ds(g * TG, TG), :], c["ACC"][:, bass.ds(g * TG, TG), 0:D]).then_inc(q["tab"], 16)


def combine(nc, ins, dram, c, moe, b, q, sb, sem):
    w, vec, xin, mv, rs = b["w"], b["vec"], b["xin"], b["mv"], b["rs"]
    with ExitStack() as ctx:
        got = sb("got_c", [P, 2, TG, D], F32, ctx)
        now = sb("now_c", [P, 2, TG], I32, ctx)
        s_now, s_sum = moe["now"], sem("c_sum")
        s_got = [sem(f"c_got{u}") for u in range(TG)]
        block = ctx.enter_context(nc.Block())

        @block.sync
        def _(sp):
            sp.dma_start(w[:, :, :, :], ins["L1_gnn_W"].rearrange("l (k p) d -> p l k d", p=P)).then_inc(q["w"], 16)
            for k, name in enumerate(("L1_gnn_b", "L1_gnn_gamma", "L1_gnn_beta")):
                sp.dma_start(vec[:, k, :, :], ins[name].rearrange("(o l) d -> o l d", o=1).to_broadcast([P, LAYERS, D])).then_inc(q["w"], 16)
            nodes_sync(sp, dram, c, q, 0)
            sp.wait_ge(q["tab"], 16 * NG)
            sp.wait_ge(q["w"], 64)

        @block.gpsimd
        def _(g_):
            def places(g, u):
                wait(g_, s_sum, g * (2 * TG) + (2 * u + 2 - 2 * TG))
                if not isinstance(g, int):
                    settle(g_)
                nc.gpsimd.tensor_copy(now[:, :, u], moe["pos"][:, :, bass.ds(g * TG + u, 1)].rearrange("p k o -> p (k o)")).then_inc(s_now, 1)

            def body(g):
                for u in range(TG):
                    places(g + (u + 1) // TG, (u + 1) % TG)
                    g_.wait_ge(s_now, g * TG + (NBLK + 1 + u + 1))
                    settle(g_)
                    for k in range(2):
                        nc.gpsimd.indirect_dma_start(
                            out=got[:, k, u, :], out_offset=None, in_=dram["y"][:, :],
                            in_offset=bass.IndirectOffsetOnAxis(ap=now[:, k, u:u + 1], axis=0)).then_inc(s_got[u], 16)
            places(0, 0)
            body(0)
            with g_.Fori(1, NG) as g:
                body(g)

        @block.tensor
        def _(pe):
            pe.wait_ge(q["w"], 64)
            pe.matmul(b["pM"][0][:, 0:P], c["ident"][:, :], c["ident"][:, :], start=True, stop=True).then_inc(q["M"], 1)
            nodes_tensor(pe, c, b, q, 0)

        @block.scalar
        def _(act):
            nodes_scalar(act, c, b, q, 0)

        @block.vector
        def _(v):
            with v.Fori(0, NG) as g:
                for u in range(TG):
                    t = g * TG + u
                    v.wait_ge(s_got[u], g * 32 + 32)
                    v.scalar_tensor_tensor(out=c["X"][:, t, :], in0=got[:, 0, u, :], scalar=moe["wt"][:, 0, bass.ds(t, 1)],
                                           in1=c["ACC"][:, t, 0:D], op0=ALU.mult, op1=ALU.add).then_inc(s_sum, 1)
                    v.wait_ge(s_sum, t * 2 + 1)
                    v.scalar_tensor_tensor(out=c["X"][:, t, :], in0=got[:, 1, u, :], scalar=moe["wt"][:, 1, bass.ds(t, 1)],
                                           in1=c["X"][:, t, :], op0=ALU.mult, op1=ALU.add).then_inc(s_sum, 1)
                v.wait_ge(s_sum, g * (2 * TG) + 2 * TG)
                settle(v)
                moments(v, b, q, g, lambda u: c["X"][:, g * TG + u, :])
                for u in range(TG):
                    v.wait_ge(q["M"], g * TG + 1)
                    v.tensor_scalar(xin[:, u, :], c["X"][:, g * TG + u, :], mv[:, u, 0:1], rs[:, u:u + 1],
                                    ALU.subtract, ALU.mult).then_inc(q["xin"], 1)


def result_moments(v, c, b, q, t, n):
    result_stats(v, c, b, q, t, n)
    result_aggregates(v, b, q, t, n)
    result_kept(v, c, b, q, t, n)


def result_stats(v, c, b, q, t, n):
    v.wait_ge(q["zz"], t * 3 + n)
    settle(v)
    for k in range(n):
        v.bn_stats(b["stat"][:, k, :], c["X"][:, t + k, :]).then_inc(q["zz"], 1)


def result_aggregates(v, b, q, t, n):
    v.wait_ge(q["zz"], t * 3 + 2 * n)
    settle(v)
    for k in range(n):
        v.bn_aggr(b["mv"][:, k, :], b["stat"][:, k, :]).then_inc(q["zz"], 1)


def result_kept(v, c, b, q, t, n):
    v.wait_ge(q["zz"], t * 3 + 3 * n)
    settle(v)
    v.tensor_copy(c["mvx"][:, bass.ds(t, n), :], b["mv"][:, 0:n, :])


def layers_apart(nc, dram, c, b, q):
    z, vec, mv, rs = b["z"], b["vec"], b["mv"], b["rs"]
    r = c["ring"]
    with nc.Block() as block:
        @block.sync
        def _(sp):
            with sp.Fori(1, LAYERS) as l:
                nodes_sync(sp, dram, c, q, l)
            sp.wait_ge(q["tab"], 16 * NG * LAYERS)

        @block.gpsimd
        def _(g):
            with g.Fori(0, LAYERS) as l:
                g.wait_ge(q["tab"], l * (16 * NG) + 16 * NG)
                settle(g)
                steps_pool(nc, c, r, g, l + 1, dram["table"])

        @block.tensor
        def _(pe):
            with pe.Fori(1, LAYERS) as l:
                steps_tensor(nc, c, r, pe, b["pS"], D, l)
                nodes_tensor(pe, c, b, q, l)
            steps_tensor(nc, c, r, pe, b["pS"], D, LAYERS)

        @block.scalar
        def _(act):
            with act.Fori(1, LAYERS) as l:
                nodes_scalar(act, c, b, q, l)
            with act.Fori(0, NG) as g:
                act.wait_ge(q["mv"], LAYERS * NT + g * TG + TG)
                act.activation(b["sd"][:, :], mv[:, :, 1], ACT.Sqrt, bias=c["eps"][:, 0:1]).then_inc(q["sd"], 1)

        @block.vector
        def _(v):
            def row(k, l):
                return vec[:, k, bass.ds(l, 1), :].rearrange("p o d -> p (o d)")

            def epilogue(l, g):
                n = l * NG + g
                for u in range(TG):
                    t = g * TG + u
                    v.scalar_tensor_tensor(out=z[:, u, :], in0=c["ACC"][:, t, 0:D], scalar=c["dinv"][:, bass.ds(t, 1)],
                                           in1=row(0, l), op0=ALU.mult, op1=ALU.add).then_inc(q["z"], 1)
                v.wait_ge(q["z"], n * TG + TG)
                moments(v, b, q, n + NG, lambda u: z[:, u, :])
                for u in range(TG):
                    v.scalar_tensor_tensor(out=z[:, u, :], in0=z[:, u, :], scalar=mv[:, u, 0:1], in1=row(1, l),
                                           op0=ALU.subtract, op1=ALU.mult).then_inc(q["z2"], 1)
                for u in range(TG):
                    v.wait_ge(q["z2"], n * TG + u + 1)
                    v.scalar_tensor_tensor(out=z[:, u, :], in0=z[:, u, :], scalar=rs[:, u:u + 1], in1=row(2, l),
                                           op0=ALU.mult, op1=ALU.add).then_inc(q["z3"], 1)

            with v.Fori(1, LAYERS) as l:
                steps_vector(nc, c, r, v, b["pS"], D, l)
                v.wait_ge(r["s_add"], (l + 1) * STEPS + OH)
                settle(v)
                with v.Fori(0, NG) as g:
                    v.wait_ge(q["xin"], l * NT + g * TG)
                    epilogue(l - 1, g)
            steps_vector(nc, c, r, v, b["pS"], D, LAYERS)
            v.wait_ge(r["s_add"], (LAYERS + 1) * STEPS + OH)
            with v.Fori(0, NG) as g:
                epilogue(LAYERS - 1, g)
                v.wait_ge(q["z3"], (LAYERS - 1) * NT + g * TG + TG)
                for u in range(TG):
                    t = g * TG + u
                    v.scalar_tensor_tensor(out=c["X"][:, t, :], in0=z[:, u, :], scalar=0.0, in1=c["X"][:, t, :],
                                           op0=ALU.max, op1=ALU.add).then_inc(q["zz"], 1)
                result_moments(v, c, b, q, g * TG, TG)


def layers_overlapped(nc, dram, c, b, q):
    z, vec, xin, xt, stat, mv, sd, rs = (b[k] for k in ("z", "vec", "xin", "xt", "stat", "mv", "sd", "rs"))
    pT, pM = b["pT"], b["pM"]
    r = c["ring"]
    tables = [dram["table"], dram["table1"], dram["table2"]]

    def dinv(t):
        return c["dinv"][:, t:t + 1] if isinstance(t, int) else c["dinv"][:, bass.ds(t, 1)]

    with nc.Block() as block:
        @block.sync
        def _(sp):
            for l in range(1, LAYERS):
                table = tables[l].rearrange("(t p) d -> p t d", p=P)

                def store(i):
                    t, n, _ = batch(i)
                    sp.wait_ge(q["h"], t + (l * NT + n))
                    sp.dma_start(table[:, bass.ds(t, n), :], c["ACC"][:, bass.ds(t, n), 0:D]).then_inc(q["tab"], 16)

                with sp.Fori(LAG, NB) as i:
                    store(i)
                store(None)
            sp.wait_ge(q["tab"], 16 * NG + 16 * BATCHES * (LAYERS - 1))

        @block.gpsimd
        def _(g):
            for l in range(1, LAYERS + 1):
                g.wait_ge(q["tab"], 16 * NG + 16 * BATCHES * (l - 1))
                steps_pool(nc, c, r, g, l, tables[l - 1])

        @block.tensor
        def _(pe):
            def turns(l, i):
                t, n, _ = batch(i)
                for k in range(n):
                    pe.wait_ge(q["xin"], t + (l * NT + k + 1))
                    pe.wait_ge(q["xt"], t + (l * NT if k < 2 else l * NT + k - 1))
                    for a in range(KD):
                        mm = pe.transpose(pT[k % 2][:, a * P:(a + 1) * P], xin[:, k, a * P:(a + 1) * P], c["ident"][:, :])
                    mm.then_inc(q["T"], 1)

            def products(l, i):
                t, n, _ = batch(i)
                for k in range(n):
                    pe.wait_ge(q["xt"], t + (l * NT + k + 1))
                    pe.wait_ge(q["h"], t + (l * NT if k < 2 else l * NT + k - 1))
                    for a in range(KD):
                        mm = pe.matmul(pM[k % 2][:, 0:D], xt[:, k, a * P:(a + 1) * P], b["w"][:, l, a, :],
                                       start=(a == 0), stop=(a == KD - 1))
                    mm.then_inc(q["M"], 1)

            for l in range(1, LAYERS + 1):
                def between(i, u):
                    if u == 14:
                        turns(l, i)
                    if u == 18:
                        products(l, i)

                steps_tensor(nc, c, r, pe, b["pS"], D, l, (0, LAG))
                steps_tensor(nc, c, r, pe, b["pS"], D, l, (LAG, NB), between if l < LAYERS else None)
                if l < LAYERS:
                    turns(l, None)
                    products(l, None)

        @block.scalar
        def _(act):
            def batch_scalar(l, i):
                t, n, j = batch(i)
                act.wait_ge(q["mv"], t + (l * NT + n))
                act.activation(sd[:, 0:n], mv[:, 0:n, 1], ACT.Sqrt, bias=c["eps"][:, 0:1]).then_inc(q["sd"], 1)
                if l == LAYERS:
                    return
                for k in range(n):
                    act.wait_ge(q["z3"], t + ((l - 1) * NT + k + 1))
                    act.activation(xin[:, k, :], z[:, k, :], ACT.Relu).then_inc(q["xin"], 1)
                for k in range(n):
                    act.wait_ge(q["T"], t + (l * NT + k + 1))
                    act.activation(xt[:, k, :], pT[k % 2][:, 0:D], ACT.Copy).then_inc(q["xt"], 1)
                for k in range(n):
                    act.wait_ge(q["M"], t + (l * NT + k + 2))
                    settle(act)
                    act.activation(c["ACC"][:, t + k, 0:D], pM[k % 2][:, 0:D], ACT.Copy,
                                   scale=dinv(t + k)).then_inc(q["h"], 1)

            for l in range(1, LAYERS + 1):
                with act.Fori(LAG, NB) as i:
                    batch_scalar(l, i)
                batch_scalar(l, None)

        @block.vector
        def _(v):
            def row(k, l):
                return vec[:, k, l - 1, :]

            def sums(l, i):
                t, n, _ = batch(i)
                if l < LAYERS:
                    v.wait_ge(q["xin"], t + l * NT)
                for k in range(n):
                    v.scalar_tensor_tensor(out=z[:, k, :], in0=c["ACC"][:, t + k, 0:D], scalar=dinv(t + k),
                                           in1=row(0, l), op0=ALU.mult, op1=ALU.add).then_inc(q["z"], 1)

            def stats(l, i):
                t, n, _ = batch(i)
                v.wait_ge(q["z"], t + ((l - 1) * NT + n))
                for k in range(n):
                    v.bn_stats(stat[:, k, :], z[:, k, :]).then_inc(q["stat"], 1)

            def aggregates(l, i):
                t, n, _ = batch(i)
                v.wait_ge(q["stat"], t + (l * NT + n))
                settle(v)
                for k in range(n):
                    v.bn_aggr(mv[:, k, :], stat[:, k, :]).then_inc(q["mv"], 1)

            def deviations(l, i):
                _, n, j = batch(i)
                v.wait_ge(q["sd"], j + (NG + (l - 1) * BATCHES + 1))
                v.reciprocal(rs[:, 0:n], sd[:, 0:n]).then_inc(q["rs"], 1)

            def gains(l, i):
                _, n, j = batch(i)
                for k in range(n):
                    v.scalar_tensor_tensor(out=z[:, k, :], in0=z[:, k, :], scalar=mv[:, k, 0:1], in1=row(1, l),
                                           op0=ALU.subtract, op1=ALU.mult).then_inc(q["z2"], 1)

            def shifts(l, i):
                t, n, j = batch(i)
                v.wait_ge(q["rs"], j + (NG + (l - 1) * BATCHES + 1))
                v.wait_ge(q["z2"], t + ((l - 1) * NT + n))
                for k in range(n):
                    v.scalar_tensor_tensor(out=z[:, k, :], in0=z[:, k, :], scalar=rs[:, k:k + 1], in1=row(2, l),
                                           op0=ALU.mult, op1=ALU.add).then_inc(q["z3"], 1)

            def results(l, i):
                t, n, _ = batch(i)
                if l < LAYERS:
                    return
                v.wait_ge(q["z3"], t + ((l - 1) * NT + n))
                for k in range(n):
                    v.scalar_tensor_tensor(out=c["X"][:, t + k, :], in0=z[:, k, :], scalar=0.0, in1=c["X"][:, t + k, :],
                                           op0=ALU.max, op1=ALU.add).then_inc(q["zz"], 1)

            for l in range(1, LAYERS + 1):
                def between(i, u):
                    if u == 0:
                        sums(l, i)
                    elif u == 1:
                        stats(l, i)
                    elif u == 2:
                        aggregates(l, i)
                    elif u == 5:
                        deviations(l, i)
                    elif u == 6:
                        gains(l, i)
                    elif u == 7:
                        shifts(l, i)
                    elif u == 9:
                        results(l, i)
                    elif u == 11 and l == LAYERS:
                        result_stats(v, c, b, q, *batch(i)[0:2])
                    elif u == 12 and l == LAYERS:
                        result_aggregates(v, b, q, *batch(i)[0:2])
                    elif u == 13 and l == LAYERS:
                        result_kept(v, c, b, q, *batch(i)[0:2])

                steps_vector(nc, c, r, v, b["pS"], D, l, (0, LAG))
                steps_vector(nc, c, r, v, b["pS"], D, l, (LAG, NB), between)
                v.wait_ge(r["s_add"], (l + 1) * STEPS + OH)
                for stage in (sums, stats, aggregates, deviations, gains, shifts, results):
                    stage(l, None)
            result_moments(v, c, b, q, *batch(None)[0:2])


def slices(nc, ins, out, c, sb, pb, sem):
    with ExitStack() as ctx:
        wc = sb("wc", [P, KD, HEADS * GS], F32, ctx)
        bc = sb("bc", [P, HEADS * GS], F32, ctx)
        SWT = sb("SWT", [P, NT, HEADS * GS], F32, ctx)
        mo = sb("mo", [P, PAIRS, D], F32, ctx)
        diag = sb("diag", [P, 4, P], F32, ctx)
        sums = sb("sums", [P, PAIRS, AW], F32, ctx)
        fold_weights(nc, ins, c, wc, bc, diag, sb, pb, sem)
        slice_nodes(nc, c, wc, bc, SWT, sums, sb, pb, sem)
        attend(nc, ins, c, diag, sums, mo, sb, pb, sem)
        project(nc, ins, out, c, SWT, mo, sb, pb, sem)


def fold_weights(nc, ins, c, wc, bc, diag, sb, pb, sem):
    with ExitStack() as ctx:
        wx = sb("wx_f", [P, KD, HEADS * DH], F32, ctx)
        wxt = sb("wxt_f", [P, KD, PAIRS, P], F32, ctx)
        bx = sb("bx_f", [P, PAIRS], F32, ctx)
        bxb = sb("bxb_f", [P, PAIRS, P], F32, ctx)
        bs = sb("bs_f", [P, GS], F32, ctx)
        tp = sb("tp_f", [P, HEADS], F32, ctx)
        rt = sb("rt_f", [P, HEADS], F32, ctx)
        sdx = sb("sdx_f", [P, NT], F32, ctx)
        pT = [pb(f"pT_f{k}", ctx) for k in range(KD)]
        pW = [pb(f"pW_f{k}", ctx) for k in range(KD)]
        pB = pb("pB_f", ctx)
        s_zero, s_in, s_xt, s_T, s_mm, s_v = (sem("f_zero"), sem("f_in"), sem("f_xt"), sem("f_T"), sem("f_mm"), sem("f_v"))
        s_mask = sem("f_mask")
        NIN = 2 * 4 + 4
        block = ctx.enter_context(nc.Block())

        @block.sync
        def _(sp):
            sp.wait_ge(s_zero, 1)
            for n, name in enumerate(("L1_ffn_W_slice", "L1_ffn_W_q", "L1_ffn_W_k", "L1_ffn_W_v")):
                for a in range(2):
                    sp.dma_start(diag[a * DH:(a + 1) * DH, n, a * DH:(a + 1) * DH], ins[name]).then_inc(s_in, 16)
            sp.dma_start(wx[:, :, :], ins["L1_ffn_W_x"].rearrange("(k p) n -> p k n", p=P)).then_inc(s_in, 16)
            sp.dma_start(bx[:, :], ins["L1_ffn_b_x"].rearrange("(a p) -> p a", p=P), allow_slow_non_contiguous=True).then_inc(s_in, 16)
            sp.dma_start(bs[:, :], ins["L1_ffn_b_slice"].rearrange("(o g) -> o g", o=1).to_broadcast([P, GS])).then_inc(s_in, 16)
            sp.dma_start(tp[:, :], ins["L1_ffn_temperature"].rearrange("o h a b -> o (h a b)").to_broadcast([P, HEADS])).then_inc(s_in, 16)

        @block.gpsimd
        def _(g):
            nc.gpsimd.affine_select(out=c["X"][:, NT - 1, :], in_=c["X"][:, NT - 1, :], compare_op=ALU.is_ge,
                                    fill=0.0, base=LAST - 1, pattern=[[0, D]], channel_multiplier=-1)
            nc.gpsimd.affine_select(out=c["mvx"][:, NT - 1, :], in_=c["mvx"][:, NT - 1, :], compare_op=ALU.is_ge,
                                    fill=0.0, base=LAST - 1, pattern=[[0, 2]], channel_multiplier=-1).then_inc(s_mask, 1)

        @block.vector
        def _(v):
            v.memset(diag[:, :, :], 0.0).then_inc(s_zero, 1)
            v.wait_ge(s_mask, 2)
            v.reciprocal(c["rsx"][:, :], sdx[:, :])
            v.wait_ge(s_in, 16 * NIN)
            for a in range(PAIRS):
                ins_ = v.tensor_copy(bxb[:, a, :], bx[:, a:a + 1].to_broadcast([P, P]))
            ins_.then_inc(s_v, 1)
            v.tensor_scalar(tp[:, :], tp[:, :], 0.1, 5.0, ALU.max, ALU.min).then_inc(s_v, 1)
            v.wait_ge(s_v, 2)
            v.reciprocal(rt[:, :], tp[:, :]).then_inc(s_v, 1)
            for k in range(KD):
                v.wait_ge(s_T, k + 1)
                v.tensor_copy(wxt[:, k, :, :].rearrange("p a n -> p (a n)"), pT[k][:, :]).then_inc(s_xt, 1)
            v.wait_ge(s_v, 3)
            v.wait_ge(s_mm, KD + 1)
            for h in range(HEADS):
                cols = slice(h * GS, (h + 1) * GS)
                for k in range(KD):
                    v.tensor_scalar(wc[:, k, cols], pW[k][:, cols], rt[:, h:h + 1], None, ALU.mult)
                ins_ = v.tensor_tensor(bc[:, cols], pB[:, cols], bs[:, :], ALU.add)
            ins_.then_inc(s_v, 1)
            v.wait_ge(s_v, 4)
            for h in range(HEADS):
                cols = slice(h * GS, (h + 1) * GS)
                v.tensor_scalar(bc[:, cols], bc[:, cols], rt[:, h:h + 1], None, ALU.mult)

        @block.scalar
        def _(act):
            act.wait_ge(s_mask, 1)
            act.activation(sdx[:, :], c["mvx"][:, :, 1], ACT.Sqrt, bias=c["eps"][:, 0:1]).then_inc(s_mask, 1)

        @block.tensor
        def _(pe):
            pe.wait_ge(s_in, 16 * NIN)
            for k in range(KD):
                for a in range(PAIRS):
                    mm = pe.transpose(pT[k][:, a * P:(a + 1) * P], wx[:, k, a * P:(a + 1) * P], c["ident"][:, :])
                mm.then_inc(s_T, 1)
            for k in range(KD):
                pe.wait_ge(s_xt, k + 1)
                for a in range(PAIRS):
                    mm = pe.matmul(pW[k][:, a * P:(a + 1) * P], wxt[:, k, a, :], diag[:, 0, :], start=True, stop=True)
                mm.then_inc(s_mm, 1)
            pe.wait_ge(s_v, 1)
            for a in range(PAIRS):
                mm = pe.matmul(pB[:, a * P:(a + 1) * P], bxb[:, a, :], diag[:, 0, :], start=True, stop=True)
            mm.then_inc(s_mm, 1)


def slice_nodes(nc, c, wc, bc, SWT, sums, sb, pb, sem):
    SW = HEADS * GS
    UN, RS = 8, 4
    LEAD = 5
    BODY = 8
    with ExitStack() as ctx:
        un = sb("un_s", [P, UN, AW], F32, ctx)
        ut = sb("ut_s", [P, 2, D], F32, ctx)
        z = sb("z_s", [P, RS, SW], F32, ctx)
        sw = sb("sw_s", [P, RS, SW], F32, ctx)
        red = sb("red_s", [P, RS, 3, HEADS], F32, ctx)
        zero = sb("zero_s", [P, AW], F32, ctx)
        s_un = sem("s_un")
        s_T, s_ut, s_L, s_z, s_max, s_sub, s_exp = (sem("s_T"), sem("s_ut"), sem("s_L"), sem("s_z"), sem("s_max"),
                                                    sem("s_sub"), sem("s_exp"))
        s_sum, s_inv, s_sw, s_W, s_swt, s_S, s_zero, s_end = (sem("s_sum"), sem("s_inv"), sem("s_sw"), sem("s_W"),
                                                              sem("s_swt"), sem("s_S"), sem("s_zero"), sem("s_end"))
        pT = pb("pT_s", ctx)
        pL = [pb(f"pL_s{k}", ctx) for k in range(2)]
        pW = pb("pW_s", ctx)
        pS = [pb(f"pS_s{k}", ctx) for k in range(PAIRS)]
        block = ctx.enter_context(nc.Block())

        def heads(ap):
            return ap.rearrange("p (h g) -> p h g", h=HEADS)

        def run(eng, step, lag):
            def straight(a, b):
                for s in range(a, b):
                    step(s, s % BODY, lambda d, s=s: 0 <= s + d < NT)

            straight(0, BODY)
            with eng.Fori(1, NT // BODY - 1) as i:
                for x in range(BODY):
                    step(i * BODY + x, x, lambda d: True)
            straight((NT // BODY - 1) * BODY, NT + lag)

        @block.vector
        def _(v):
            v.memset(zero[:, :], 0.0).then_inc(s_zero, 1)
            v.memset(z[:, :, :], 0.0).then_inc(s_z, 1)

            def normalised(t, x):
                wait(v, s_S, t + (2 - UN) if not isinstance(t, int) or t >= UN else 0)
                v.tensor_copy(un[:, x, D:AW], c["valid"][:, bass.ds(t, 1)])
                v.tensor_scalar(un[:, x, 0:D], c["X"][:, t, :], c["mvx"][:, bass.ds(t, 1), 0], c["rsx"][:, bass.ds(t, 1)],
                                ALU.subtract, ALU.mult).then_inc(s_un, 1)

            def logits(t, x):
                v.wait_ge(s_L, t + 1)
                v.tensor_tensor(z[:, x, :], pL[x % 2][:, :], bc[:, :], ALU.add).then_inc(s_z, 1)
                v.wait_ge(s_z, t + 2)
                v.tensor_reduce(red[:, x, 0, :], heads(z[:, x, :]), AX.X, ALU.max).then_inc(s_max, 1)
                v.wait_ge(s_max, t + 1)
                v.tensor_tensor(heads(z[:, x, :]), heads(z[:, x, :]),
                                red[:, x, 0, :].rearrange("p (h o) -> p h o", o=1).to_broadcast([P, HEADS, GS]),
                                ALU.subtract).then_inc(s_sub, 1)

            def weights(t, x):
                v.wait_ge(s_exp, t + 1)
                v.tensor_reduce(red[:, x, 1, :], heads(z[:, x, :]), AX.X, ALU.add).then_inc(s_sum, 1)
                v.wait_ge(s_sum, t + 1)
                v.reciprocal(red[:, x, 2, :], red[:, x, 1, :]).then_inc(s_inv, 1)
                wait(v, s_S, t + (2 - RS) if not isinstance(t, int) or t >= RS else 0)
                v.wait_ge(s_inv, t + 1)
                v.tensor_tensor(heads(sw[:, x, :]), heads(z[:, x, :]),
                                red[:, x, 2, :].rearrange("p (h o) -> p h o", o=1).to_broadcast([P, HEADS, GS]),
                                ALU.mult).then_inc(s_sw, 1)

            for t in range(LEAD):
                normalised(t, t)
            logits(0, 0)

            def step(s, x, live):
                if live(1):
                    logits(s + 1, (x + 1) % RS)
                if live(LEAD):
                    normalised(s + LEAD, (x + LEAD) % UN)
                weights(s, x % RS)

            run(v, step, 0)
            v.wait_ge(s_end, 1)
            for a in range(PAIRS):
                v.tensor_copy(sums[:, a, :], pS[a][:, 0:AW])

        @block.scalar
        def _(act):
            def step(s, x, live):
                if live(0):
                    act.wait_ge(s_T, s + 1)
                    act.activation(ut[:, x % 2, :], pT[:, 0:D], ACT.Copy).then_inc(s_ut, 1)
                if live(-2):
                    act.wait_ge(s_sub, s - 1)
                    act.activation(z[:, (x - 2) % RS, :], z[:, (x - 2) % RS, :], ACT.Exp).then_inc(s_exp, 1)
                if live(-4):
                    act.wait_ge(s_W, s - 3)
                    settle(act)
                    act.activation(SWT[:, s - 4, :], pW[:, :], ACT.Copy).then_inc(s_swt, 1)

            run(act, step, 4)

        @block.tensor
        def _(pe):
            pe.wait_ge(s_zero, 1)
            for a in range(PAIRS):
                mm = pe.matmul(pS[a][:, 0:AW], zero[:, 0:P], zero[:, :], start=True, stop=False, skip_group_check=True)
            mm.then_inc(s_S, 1)

            def step(s, x, live):
                if live(0):
                    pe.wait_ge(s_un, s + 1)
                    wait(pe, s_ut, s)
                    for n in range(KD):
                        mm = pe.transpose(pT[:, n * P:(n + 1) * P], un[:, x, n * P:(n + 1) * P], c["ident"][:, :])
                    mm.then_inc(s_T, 1)
                if live(-1):
                    pe.wait_ge(s_ut, s)
                    wait(pe, s_z, s - 1)
                    for n in range(KD):
                        mm = pe.matmul(pL[(x - 1) % 2][:, :], ut[:, (x - 1) % 2, n * P:(n + 1) * P], wc[:, n, :],
                                       start=(n == 0), stop=(n == KD - 1))
                    mm.then_inc(s_L, 1)
                if live(-3):
                    pe.wait_ge(s_sw, s - 2)
                    wait(pe, s_swt, s - 3)
                    slot = (x - 3) % RS
                    for a in range(PAIRS):
                        mm = pe.transpose(pW[:, a * P:(a + 1) * P], sw[:, slot, a * P:(a + 1) * P], c["ident"][:, :])
                    mm.then_inc(s_W, 1)
                    for a in range(PAIRS):
                        mm = pe.matmul(pS[a][:, 0:AW], sw[:, slot, a * P:(a + 1) * P], un[:, (x - 3) % UN, :],
                                       start=False, stop=False, skip_group_check=True)
                    mm.then_inc(s_S, 1)

            run(pe, step, 3)
            for a in range(PAIRS):
                mm = pe.matmul(pS[a][:, 0:AW], zero[:, 0:P], zero[:, :], start=False, stop=True, skip_group_check=True)
            mm.then_inc(s_end, 1)


def attend(nc, ins, c, diag, sums, mo, sb, pb, sem):
    with ExitStack() as ctx:
        wfx = sb("wfx_t", [P, KD, HEADS * DH], F32, ctx)
        bfx = sb("bfx_t", [P, HEADS * DH], F32, ctx)
        wo = sb("wo_t", [P, PAIRS, D], F32, ctx)
        st = sb("st_t", [P, KD, PAIRS, P], F32, ctx)
        inv = sb("inv_t", [P, 2, PAIRS], F32, ctx)
        tok = sb("tok_t", [P, PAIRS, P], F32, ctx)
        tokT = sb("tokT_t", [P, PAIRS, P], F32, ctx)
        qT = sb("qT_t", [P, PAIRS, P], F32, ctx)
        kT = sb("kT_t", [P, PAIRS, P], F32, ctx)
        vv = sb("vv_t", [P, PAIRS, P], F32, ctx)
        sc = sb("sc_t", [P, PAIRS, DH], F32, ctx)
        red = sb("red_t", [P, 3, PAIRS], F32, ctx)
        at = sb("at_t", [P, PAIRS, P], F32, ctx)
        atT = sb("atT_t", [P, PAIRS, P], F32, ctx)
        oT = sb("oT_t", [P, PAIRS, P], F32, ctx)
        bank = [pb(f"bank_t{k}", ctx) for k in range(8)]
        s_in, s_pe, s_v, s_exp = sem("t_in"), sem("t_pe"), sem("t_v"), sem("t_exp")
        block = ctx.enter_context(nc.Block())
        HALVES = [slice(0, DH), slice(DH, 2 * DH)]

        def flat(x):
            return x[:, :, :].rearrange("p a n -> p (a n)")

        @block.sync
        def _(sp):
            sp.dma_start(wfx[:, :, :], ins["L1_ffn_W_fx"].rearrange("(k p) n -> p k n", p=P)).then_inc(s_in, 16)
            sp.dma_start(bfx[:, :], ins["L1_ffn_b_fx"].rearrange("(o n) -> o n", o=1).to_broadcast([P, HEADS * DH])).then_inc(s_in, 16)
            sp.dma_start(wo[:, :, :], ins["L1_ffn_W_out"].rearrange("(a p) d -> p a d", p=P)).then_inc(s_in, 16)

        @block.tensor
        def _(pe):
            def done(n, fn):
                pe.wait_ge(s_v, n)
                for a in range(PAIRS):
                    mm = fn(a)
                mm.then_inc(s_pe, 1)

            pe.wait_ge(s_in, 48)
            cols = [slice(a * P, (a + 1) * P) for a in range(PAIRS)]
            for k in range(KD):
                for a in range(PAIRS):
                    mm = pe.transpose(bank[k][:, cols[a]], sums[:, a, k * P:(k + 1) * P], c["ident"][:, :])
            mm.then_inc(s_pe, 1)

            def tokens(a):
                for k in range(KD):
                    mm = pe.matmul(bank[2][:, cols[a]], st[:, k, a, :], wfx[:, k, cols[a]], start=(k == 0), stop=(k == KD - 1))
                return mm
            done(1, tokens)
            done(2, lambda a: pe.transpose(bank[3][:, cols[a]], tok[:, a, :], c["ident"][:, :]))

            def qkv(a):
                pe.matmul(bank[4][:, cols[a]], diag[:, 1, :], tokT[:, a, :], start=True, stop=True)
                pe.matmul(bank[5][:, cols[a]], diag[:, 2, :], tokT[:, a, :], start=True, stop=True)
                return pe.matmul(bank[6][:, cols[a]], tokT[:, a, :], diag[:, 3, :], start=True, stop=True)
            done(3, qkv)
            done(4, lambda a: pe.matmul(bank[7][:, cols[a]], qT[:, a, :], kT[:, a, :], start=True, stop=True))
            done(5, lambda a: pe.transpose(bank[0][:, cols[a]], at[:, a, :], c["ident"][:, :]))
            done(6, lambda a: pe.matmul(bank[1][:, cols[a]], vv[:, a, :], atT[:, a, :], start=True, stop=True))
            done(7, lambda a: pe.matmul(bank[2 + a // 2][:, (a % 2) * D:(a % 2 + 1) * D], oT[:, a, :], wo[:, a, :], start=True, stop=True))

        @block.scalar
        def _(act):
            act.wait_ge(s_exp, 1)
            act.activation(sc[:, :, :], sc[:, :, :], ACT.Exp).then_inc(s_exp, 1)

        @block.vector
        def _(v):
            s_c = sem("t_chain")
            n = [0]

            def then(i):
                i.then_inc(s_c, 1)
                n[0] += 1
                v.wait_ge(s_c, n[0])

            v.memset(tok[:, :, :], 0.0)
            v.memset(at[:, :, :], 0.0)
            v.tensor_scalar(inv[:, 0, :], sums[:, :, D], 1e-5, None, ALU.add)
            v.wait_ge(s_in, 48)
            v.wait_ge(s_pe, 1)
            v.tensor_copy(st[:, 0, :, :].rearrange("p a n -> p (a n)"), bank[0][:, :])
            then(v.tensor_copy(st[:, 1, :, :].rearrange("p a n -> p (a n)"), bank[1][:, :]))
            then(v.reciprocal(inv[:, 1, :], inv[:, 0, :]))
            v.memset(red[:, :, :], 0.0).then_inc(s_v, 1)
            v.wait_ge(s_pe, 2)
            for a in range(PAIRS):
                for x in range(2):
                    hs = slice(a * P + x * DH, a * P + (x + 1) * DH)
                    i = v.scalar_tensor_tensor(out=tok[HALVES[x], a, HALVES[x]], in0=bfx[HALVES[x], hs], scalar=sums[HALVES[x], a, D:AW],
                                               in1=bank[2][HALVES[x], hs], op0=ALU.mult, op1=ALU.add)
            then(i)
            for a in range(PAIRS):
                i = v.tensor_scalar(tok[:, a, :], tok[:, a, :], inv[:, 1, a:a + 1], None, ALU.mult)
            i.then_inc(s_v, 1)
            v.wait_ge(s_pe, 3)
            v.tensor_copy(flat(tokT), bank[3][:, :]).then_inc(s_v, 1)
            v.wait_ge(s_pe, 4)
            v.tensor_copy(flat(qT), bank[4][:, :])
            v.tensor_copy(flat(kT), bank[5][:, :])
            v.tensor_copy(flat(vv), bank[6][:, :]).then_inc(s_v, 1)
            v.wait_ge(s_pe, 5)
            for a in range(PAIRS):
                for x in range(2):
                    i = v.tensor_scalar(sc[HALVES[x], a, :], bank[7][HALVES[x], a * P + x * DH:a * P + (x + 1) * DH],
                                        float(DH) ** -0.5, None, ALU.mult)
            then(i)
            then(v.tensor_reduce(red[:, 0, :], sc[:, :, :], AX.X, ALU.max))

            def wide(k):
                return red[:, k, :].rearrange("p (a o) -> p a o", o=1).to_broadcast([P, PAIRS, DH])
            v.tensor_tensor(sc[:, :, :], sc[:, :, :], wide(0), ALU.subtract).then_inc(s_exp, 1)
            v.wait_ge(s_exp, 2)
            then(v.tensor_reduce(red[:, 1, :], sc[:, :, :], AX.X, ALU.add))
            then(v.reciprocal(red[:, 2, :], red[:, 1, :]))
            for x in range(2):
                i = v.tensor_tensor(at[HALVES[x], :, HALVES[x]], sc[HALVES[x], :, :],
                                    red[HALVES[x], 2, :].rearrange("p (a o) -> p a o", o=1).to_broadcast([DH, PAIRS, DH]), ALU.mult)
            i.then_inc(s_v, 1)
            v.wait_ge(s_pe, 6)
            v.tensor_copy(flat(atT), bank[0][:, :]).then_inc(s_v, 1)
            v.wait_ge(s_pe, 7)
            v.tensor_copy(flat(oT), bank[1][:, :]).then_inc(s_v, 1)
            v.wait_ge(s_pe, 8)
            for a in range(PAIRS):
                v.tensor_copy(mo[:, a, :], bank[2 + a // 2][:, (a % 2) * D:(a % 2 + 1) * D])


def project(nc, ins, out, c, SWT, mo, sb, pb, sem):
    with ExitStack() as ctx:
        bo = sb("bo_o", [P, D], F32, ctx)
        wt = sb("wt_o", [P, TG, HEADS * GS], F32, ctx)
        pO = [pb(f"pO_o{k}", ctx) for k in range(TG)]
        s_in, s_wt, s_b, s_mm, s_x, s_out = sem("o_in"), sem("o_wt"), sem("o_b"), sem("o_mm"), sem("o_x"), sem("o_out")
        block = ctx.enter_context(nc.Block())

        @block.sync
        def _(sp):
            sp.dma_start(bo[:, :], ins["L1_ffn_b_out"].rearrange("(o d) -> o d", o=1).to_broadcast([P, D])).then_inc(s_in, 16)
            rows = out[0:(NT - 1) * P, :].rearrange("(t p) d -> p t d", p=P)
            with sp.Fori(0, NG - 1) as g:
                sp.wait_ge(s_x, g * TG + TG)
                sp.dma_start(rows[:, bass.ds(g * TG, TG), :], c["X"][:, bass.ds(g * TG, TG), :]).then_inc(s_out, 16)
            sp.wait_ge(s_x, NT)
            sp.dma_start(rows[:, (NG - 1) * TG:NT - 1, :], c["X"][:, (NG - 1) * TG:NT - 1, :]).then_inc(s_out, 16)
            sp.dma_start(out[(NT - 1) * P:N, :], c["X"][0:LAST, NT - 1, :]).then_inc(s_out, 16)
            sp.wait_ge(s_out, 16 * (NG + 1))

        @block.scalar
        def _(act):
            def body(g):
                for u in range(TG):
                    wait(act, s_mm, (g - 1) * TG + u + 1)
                    if not isinstance(g, int):
                        settle(act)
                    act.activation(wt[:, u, :], SWT[:, g * TG + u, :], ACT.Copy).then_inc(s_wt, 1)
            body(0)
            with act.Fori(1, NG) as g:
                body(g)

        @block.tensor
        def _(pe):
            def body(g):
                for u in range(TG):
                    t = g * TG + u
                    pe.wait_ge(s_wt, t + 1)
                    wait(pe, s_x, t - TG + 1)
                    for a in range(PAIRS):
                        mm = pe.matmul(pO[u][:, 0:D], wt[:, u, a * P:(a + 1) * P], mo[:, a, :], start=(a == 0), stop=(a == PAIRS - 1))
                    mm.then_inc(s_mm, 1)
            body(0)
            with pe.Fori(1, NG) as g:
                body(g)

        @block.vector
        def _(v):
            v.wait_ge(s_in, 16)
            with v.Fori(0, NG) as g:
                for u in range(TG):
                    t = g * TG + u
                    v.tensor_tensor(c["X"][:, t, :], c["X"][:, t, :], bo[:, :], ALU.add).then_inc(s_b, 1)
                for u in range(TG):
                    t = g * TG + u
                    v.wait_ge(s_b, t + 1)
                    v.wait_ge(s_mm, t + 1)
                    v.tensor_tensor(c["X"][:, t, :], pO[u][:, 0:D], c["X"][:, t, :], ALU.add).then_inc(s_x, 1)


_INS = ['x', 'src', 'dst', 'edge_weight', 'L0_gnn_w_nbr', 'L0_gnn_w_own', 'L0_gnn_bias',
        'L0_ffn_Wr', 'L0_ffn_br', 'L0_ffn_ln_g', 'L0_ffn_ln_b', 'L0_ffn_W1', 'L0_ffn_b1', 'L0_ffn_W2', 'L0_ffn_b2',
        'L1_gnn_W', 'L1_gnn_b', 'L1_gnn_gamma', 'L1_gnn_beta', 'L1_ffn_W_fx', 'L1_ffn_b_fx', 'L1_ffn_W_x',
        'L1_ffn_b_x', 'L1_ffn_W_slice', 'L1_ffn_b_slice', 'L1_ffn_W_q', 'L1_ffn_W_k', 'L1_ffn_W_v', 'L1_ffn_W_out',
        'L1_ffn_b_out', 'L1_ffn_temperature']


def kernel(**inputs):
    import numpy as _np
    import concourse.bacc as _bacc
    from concourse import mybir as _mybir
    from concourse.bass_utils import run_bass_kernel_spmd as _run

    nc = _bacc.Bacc("TRN2", target_bir_lowering=False, num_devices=1)
    arrays, ins = {}, {}
    for name in _INS:
        a = _np.ascontiguousarray(inputs[name])
        arrays[f"in_{name}"] = a
        ins[name] = nc.dram_tensor(f"in_{name}", a.shape, _mybir.dt.from_np(a.dtype), kind="ExternalInput").ap()
    out = nc.dram_tensor("out_0", (N, D), _mybir.dt.float32, kind="ExternalOutput").ap()
    dram = {name: nc.dram_tensor(name, (rows, D), _mybir.dt.float32, kind="Internal").ap()
            for name, rows in (("table", NT * P), ("table1", NT * P), ("table2", NT * P), ("tokens", NT * P), ("y", SLOTS + BR))}
    for name, shape, dt in (("src", (E,), I32), ("dst", (E,), I32), ("weight", (E,), F32), ("rec", (P * EF, 4), F32)):
        dram[name] = nc.dram_tensor(f"edges_{name}", shape, dt, kind="Internal").ap()
    build(nc, ins, out, dram)
    r = _run(nc, [arrays], core_ids=[0])
    return r.results[0]["out_0"]
```
